# Optimizing a Trainium2 kernel written in Bass

```python
import numpy as np
import jax
import jax.numpy as jnp

def _softmax(x, axis=-1):
    return jax.nn.softmax(x, axis=axis)

def _gelu(x):
    return jax.nn.gelu(x, approximate=True)

def _silu(x):
    return jax.nn.silu(x)

def _sigmoid(x):
    return jax.nn.sigmoid(x)

def _layernorm(x, axis=-1, eps=1e-05):
    m = jnp.mean(x, axis=axis, keepdims=True)
    v = jnp.var(x, axis=axis, keepdims=True)
    return (x - m) / jnp.sqrt(v + eps)

def _scatter_add(tgt, idx, src, axis=0):
    return tgt.at[idx].add(src)

def _segment_sum(src, seg, n):
    return jax.ops.segment_sum(src, seg, n)
kernel_name = 'mk_decoder_postln_d1_seqx_r8_bb1ab0'

def setup_inputs(seed: int=0):
    np.random.seed(seed)
    _w = jnp.asarray

    def _rec_inputs():
        import jax
        import jax.numpy as jnp
        _rk = jax.random.key(seed)
        x = 7.22e-05 + 1 * jax.random.normal(jax.random.fold_in(_rk, 1), (128, 64, 128), jnp.float32)
        _lenS = 64 - jax.random.randint(jax.random.fold_in(_rk, 7), (128,), 0, max(1, 64 // 4) + 1, jnp.int32)
        _lenS2 = 64 - jax.random.randint(jax.random.fold_in(_rk, 8), (128,), 0, max(1, 64 // 4) + 1, jnp.int32)
        _ctx_1024P = jax.random.normal(jax.random.fold_in(_rk, 11), (128, 16, 128), jnp.float32)
        _ctx_1024c = jax.random.dirichlet(jax.random.fold_in(_rk, 511), 0.3 * jnp.ones((16,), jnp.float32), (128, 64))
        _ctx_1024t = jnp.einsum('bsk,bkd->bsd', _ctx_1024c, _ctx_1024P)
        _ctx_1024t = _ctx_1024t * jax.lax.rsqrt(jnp.mean(jnp.square(_ctx_1024t)) + 1e-12) * 0.953939
        ctx_1024 = 4.13588e-05 + 0.999923 * (_ctx_1024t + 0.3 * jax.random.normal(jax.random.fold_in(_rk, 611), (128, 64, 128), jnp.float32))
        return (x, ctx_1024)
    x, ctx_1024 = _rec_inputs()

    def _L0_attn_setup():
        import jax, jax.numpy as jnp
        import numpy as np
        B, T, H = (2, 256, 128)
        I, N, R, K = (256, 16, 64, 4)
        EPS = 1e-06
        key = jax.random.key(seed)
        ks = jax.random.split(key, 8)
        s = lambda k, shape, sc=0.02: jax.random.normal(k, shape, dtype=jnp.float32) * sc
        return dict(x=jax.random.normal(ks[0], (B, T, H), dtype=jnp.float32), norm_scale=jnp.ones((H,), jnp.float32), in_w=s(ks[1], (H, 2 * I)), in_b=jnp.zeros((2 * I,), jnp.float32), conv_w=jax.random.normal(ks[2], (K, I), dtype=jnp.float32) / np.float32(np.sqrt(K * I)), conv_b=jnp.zeros((I,), jnp.float32), xproj_w=s(ks[3], (I, R + 2 * N)), dt_w=s(ks[4], (R, I)), dt_b=s(ks[5], (I,), 0.1), A_log=jnp.tile(jnp.log(jnp.arange(1, N + 1, dtype=jnp.float32))[None, :], (I, 1)), D=jnp.ones((I,), jnp.float32), out_w=s(ks[6], (I, H)), out_b=jnp.zeros((H,), jnp.float32))
    _L0_attn_all = _L0_attn_setup()
    _L0_attn_in = {k: v for k, v in _L0_attn_all.items() if k in ('norm_scale', 'in_w', 'in_b', 'conv_w', 'conv_b', 'xproj_w', 'dt_w', 'dt_b', 'A_log', 'D', 'out_w', 'out_b')}
    del _L0_attn_all

    def _L0_xattn_setup():
        import jax, jax.numpy as jnp
        import numpy as np
        D_MODEL = 128
        NHEAD = 16
        HEAD_DIM = D_MODEL // NHEAD
        key = jax.random.key(seed)
        ks = jax.random.split(key, 11)
        B, S, D = (4, 256, D_MODEL)
        scale = 1.0 / np.sqrt(D)
        inp = {'q': jax.random.normal(ks[0], (B, S, D), jnp.float32), 'k': jax.random.normal(ks[1], (B, S, D), jnp.float32), 'v': jax.random.normal(ks[2], (B, S, D), jnp.float32), 'Wq': jax.random.normal(ks[3], (D, D), jnp.float32) * scale, 'bq': jnp.zeros((D,), jnp.float32), 'Wk': jax.random.normal(ks[4], (D, D), jnp.float32) * scale, 'bk': jnp.zeros((D,), jnp.float32), 'Wv': jax.random.normal(ks[5], (D, D), jnp.float32) * scale, 'bv': jnp.zeros((D,), jnp.float32), 'Wo': jax.random.normal(ks[6], (D, D), jnp.float32) * scale, 'bo': jnp.zeros((D,), jnp.float32)}
        return inp
    _L0_xattn_all = _L0_xattn_setup()
    _L0_xattn_in = {k: v for k, v in _L0_xattn_all.items() if k in ('Wq', 'bq', 'Wk', 'bk', 'Wv', 'bv', 'Wo', 'bo')}
    del _L0_xattn_all

    def _L0_ffn_setup():
        import jax, jax.numpy as jnp
        import numpy as np
        H = 128
        E = 8
        K = 2
        I = 176
        B, S = (2, 128)

        def _moe_forward(x, w_router, wg, wu, wd, wg_s, wu_s, wd_s):
            b, s, h = x.shape
            xf = x.reshape(-1, h)
            scores = jax.nn.softmax(xf @ w_router.T, axis=-1)
            topk_w, topk_idx = jax.lax.top_k(scores, K)
            topk_w = topk_w / (topk_w.sum(axis=-1, keepdims=True) + 1e-20)
            cw = (jax.nn.one_hot(topk_idx, E, dtype=xf.dtype) * topk_w[..., None]).sum(axis=1)
            g = jnp.einsum('th,ehi->tei', xf, wg)
            u = jnp.einsum('th,ehi->tei', xf, wu)
            eo = jnp.einsum('tei,eih->teh', jax.nn.silu(g) * u, wd)
            y = jnp.einsum('te,teh->th', cw, eo)
            y = y + jax.nn.silu(xf @ wg_s) * (xf @ wu_s) @ wd_s
            return y.reshape(b, s, h)
        key = jax.random.key(seed)
        ks = jax.random.split(key, 8)
        sc = 0.02
        return {'x': jax.random.normal(ks[0], (B, S, H), dtype=jnp.float32), 'w_router': jax.random.normal(ks[1], (E, H), dtype=jnp.float32) * sc, 'wg': jax.random.normal(ks[2], (E, H, I), dtype=jnp.float32) * sc, 'wu': jax.random.normal(ks[3], (E, H, I), dtype=jnp.float32) * sc, 'wd': jax.random.normal(ks[4], (E, I, H), dtype=jnp.float32) * sc, 'wg_s': jax.random.normal(ks[5], (H, I), dtype=jnp.float32) * sc, 'wu_s': jax.random.normal(ks[6], (H, I), dtype=jnp.float32) * sc, 'wd_s': jax.random.normal(ks[7], (I, H), dtype=jnp.float32) * sc}
    _L0_ffn_all = _L0_ffn_setup()
    _L0_ffn_in = {k: v for k, v in _L0_ffn_all.items() if k in ('w_router', 'wg', 'wu', 'wd', 'wg_s', 'wu_s', 'wd_s')}
    del _L0_ffn_all
    return {'x': x, 'ctx_1024': ctx_1024, 'L0_attn_norm_scale': _L0_attn_in['norm_scale'], 'L0_attn_in_w': _L0_attn_in['in_w'], 'L0_attn_in_b': _L0_attn_in['in_b'], 'L0_attn_conv_w': _L0_attn_in['conv_w'], 'L0_attn_conv_b': _L0_attn_in['conv_b'], 'L0_attn_xproj_w': _L0_attn_in['xproj_w'], 'L0_attn_dt_w': _L0_attn_in['dt_w'], 'L0_attn_dt_b': _L0_attn_in['dt_b'], 'L0_attn_A_log': _L0_attn_in['A_log'], 'L0_attn_D': _L0_attn_in['D'], 'L0_attn_out_w': _L0_attn_in['out_w'], 'L0_attn_out_b': _L0_attn_in['out_b'], 'L0_xattn_Wq': _L0_xattn_in['Wq'], 'L0_xattn_bq': _L0_xattn_in['bq'], 'L0_xattn_Wk': _L0_xattn_in['Wk'], 'L0_xattn_bk': _L0_xattn_in['bk'], 'L0_xattn_Wv': _L0_xattn_in['Wv'], 'L0_xattn_bv': _L0_xattn_in['bv'], 'L0_xattn_Wo': _L0_xattn_in['Wo'], 'L0_xattn_bo': _L0_xattn_in['bo'], 'L0_ffn_w_router': _L0_ffn_in['w_router'], 'L0_ffn_wg': _L0_ffn_in['wg'], 'L0_ffn_wu': _L0_ffn_in['wu'], 'L0_ffn_wd': _L0_ffn_in['wd'], 'L0_ffn_wg_s': _L0_ffn_in['wg_s'], 'L0_ffn_wu_s': _L0_ffn_in['wu_s'], 'L0_ffn_wd_s': _L0_ffn_in['wd_s']}

def reference(x, ctx_1024, L0_attn_norm_scale, L0_attn_in_w, L0_attn_in_b, L0_attn_conv_w, L0_attn_conv_b, L0_attn_xproj_w, L0_attn_dt_w, L0_attn_dt_b, L0_attn_A_log, L0_attn_D, L0_attn_out_w, L0_attn_out_b, L0_xattn_Wq, L0_xattn_bq, L0_xattn_Wk, L0_xattn_bk, L0_xattn_Wv, L0_xattn_bv, L0_xattn_Wo, L0_xattn_bo, L0_ffn_w_router, L0_ffn_wg, L0_ffn_wu, L0_ffn_wd, L0_ffn_wg_s, L0_ffn_wu_s, L0_ffn_wd_s):
    import jax
    import jax.numpy as jnp

    def _L0_attn_ref(x, norm_scale, in_w, in_b, conv_w, conv_b, xproj_w, dt_w, dt_b, A_log, D, out_w, out_b):
        import jax, jax.numpy as jnp
        import numpy as np
        B, T, H = (2, 256, 128)
        I, N, R, K = (256, 16, 64, 4)
        EPS = 1e-06
        Bsz, Tlen, Hd = x.shape
        Kk, Ii = conv_w.shape
        Nn = A_log.shape[1]
        Rr = dt_w.shape[0]
        xn = x * jax.lax.rsqrt(jnp.mean(x * x, axis=-1, keepdims=True) + EPS) * norm_scale
        proj = xn @ in_w + in_b
        hidden, gate = jnp.split(proj, 2, axis=-1)
        xp = jnp.pad(hidden, ((0, 0), (Kk - 1, 0), (0, 0)))
        conv = sum((conv_w[k] * xp[:, k:k + Tlen, :] for k in range(Kk))) + conv_b
        conv = jax.nn.silu(conv)
        xpj = conv @ xproj_w
        ts = xpj[..., :Rr]
        Bm = xpj[..., Rr:Rr + Nn]
        Cm = xpj[..., Rr + Nn:]
        delta = jax.nn.softplus(ts @ dt_w + dt_b)
        A = -jnp.exp(A_log)
        gate_a = jax.nn.silu(gate)

        def step(state, inp):
            h_t, d_t, g_t, B_t, C_t = inp
            dA = jnp.exp(A[None, :, :] * d_t[:, :, None])
            new = dA * state + d_t[:, :, None] * B_t[:, None, :] * h_t[:, :, None]
            y = jnp.einsum('bin,bn->bi', new, C_t) + D * h_t
            return (new, y * g_t)
        tm = lambda a: jnp.swapaxes(a, 0, 1)
        init = jnp.zeros((Bsz, Ii, Nn), x.dtype)
        _, ys = jax.lax.scan(step, init, (tm(conv), tm(delta), tm(gate_a), tm(Bm), tm(Cm)))
        ssm = jnp.swapaxes(ys, 0, 1)
        return ssm @ out_w + out_b

    def _L0_xattn_ref(q, k, v, Wq, bq, Wk, bk, Wv, bv, Wo, bo):
        import jax, jax.numpy as jnp
        import numpy as np
        D_MODEL = 128
        NHEAD = 16
        HEAD_DIM = D_MODEL // NHEAD
        B, S, D = q.shape
        H, Hd = (NHEAD, HEAD_DIM)
        qh = (q @ Wq.T + bq).reshape(B, S, H, Hd).transpose(0, 2, 1, 3)
        kh = (k @ Wk.T + bk).reshape(B, S, H, Hd).transpose(0, 2, 1, 3)
        vh = (v @ Wv.T + bv).reshape(B, S, H, Hd).transpose(0, 2, 1, 3)
        scores = jnp.einsum('bhqd,bhkd->bhqk', qh, kh) / jnp.sqrt(jnp.float32(Hd))
        attn = jax.nn.softmax(scores, axis=-1)
        out = jnp.einsum('bhqk,bhkd->bhqd', attn, vh)
        out = out.transpose(0, 2, 1, 3).reshape(B, S, D)
        return out @ Wo.T + bo

    def _L0_ffn_ref(x, w_router, wg, wu, wd, wg_s, wu_s, wd_s):
        import jax, jax.numpy as jnp
        import numpy as np
        H = 128
        E = 8
        K = 2
        I = 176
        B, S = (2, 128)

        def _moe_forward(x, w_router, wg, wu, wd, wg_s, wu_s, wd_s):
            b, s, h = x.shape
            xf = x.reshape(-1, h)
            scores = jax.nn.softmax(xf @ w_router.T, axis=-1)
            topk_w, topk_idx = jax.lax.top_k(scores, K)
            topk_w = topk_w / (topk_w.sum(axis=-1, keepdims=True) + 1e-20)
            cw = (jax.nn.one_hot(topk_idx, E, dtype=xf.dtype) * topk_w[..., None]).sum(axis=1)
            g = jnp.einsum('th,ehi->tei', xf, wg)
            u = jnp.einsum('th,ehi->tei', xf, wu)
            eo = jnp.einsum('tei,eih->teh', jax.nn.silu(g) * u, wd)
            y = jnp.einsum('te,teh->th', cw, eo)
            y = y + jax.nn.silu(xf @ wg_s) * (xf @ wu_s) @ wd_s
            return y.reshape(b, s, h)
        return _moe_forward(x, w_router, wg, wu, wd, wg_s, wu_s, wd_s)
    x = _layernorm(x + _L0_attn_ref(x, L0_attn_norm_scale, L0_attn_in_w, L0_attn_in_b, L0_attn_conv_w, L0_attn_conv_b, L0_attn_xproj_w, L0_attn_dt_w, L0_attn_dt_b, L0_attn_A_log, L0_attn_D, L0_attn_out_w, L0_attn_out_b), axis=-1)
    x = _layernorm(x + _L0_xattn_ref(x, ctx_1024, ctx_1024, L0_xattn_Wq, L0_xattn_bq, L0_xattn_Wk, L0_xattn_bk, L0_xattn_Wv, L0_xattn_bv, L0_xattn_Wo, L0_xattn_bo), axis=-1)
    x = _layernorm(x + _L0_ffn_ref(x, L0_ffn_w_router, L0_ffn_wg, L0_ffn_wu, L0_ffn_wd, L0_ffn_wg_s, L0_ffn_wu_s, L0_ffn_wd_s), axis=-1)
    return x

_drawn_inputs = setup_inputs


def setup_inputs(seed=0):
    import zlib

    import numpy as np

    out = dict(_drawn_inputs(seed))
    spreads = {'L0_attn_norm_scale': (1.0, 0.6),
     'L0_attn_in_b': (0.0, 0.8),
     'L0_attn_conv_b': (0.0, 0.8),
     'L0_attn_D': (1.0, 0.6),
     'L0_attn_out_b': (0.0, 1.528),
     'L0_xattn_bq': (0.0, 0.35),
     'L0_xattn_bk': (0.0, 2.0),
     'L0_xattn_bv': (0.0, 0.1),
     'L0_xattn_bo': (0.0, 0.1)}
    factors = {'L0_attn_in_w': 8.0,
     'L0_attn_conv_w': 8.0,
     'L0_attn_xproj_w': 8.0,
     'L0_attn_dt_w': 8.0,
     'L0_attn_dt_b': 8.0,
     'L0_attn_A_log': 8.0,
     'L0_attn_out_w': 8.0,
     'L0_ffn_w_router': 8.0,
     'L0_ffn_wg': 8.0,
     'L0_ffn_wu': 8.0,
     'L0_ffn_wd': 8.0,
     'L0_ffn_wg_s': 8.0,
     'L0_ffn_wu_s': 8.0,
     'L0_ffn_wd_s': 8.0}
    for name, (base, spread) in spreads.items():
        noise = np.random.default_rng([zlib.crc32(name.encode()), seed]).standard_normal(out[name].shape)
        drawn = base * np.exp(spread * noise) if base else spread * noise
        out[name] = jnp.asarray(drawn.astype(out[name].dtype))
    for name, factor in factors.items():
        out[name] = (out[name] * factor).astype(out[name].dtype)
    return out
```

```python
from contextlib import ExitStack

import numpy as np

import concourse.bass as bass
from concourse import mybir

F32 = mybir.dt.float32
BF16 = mybir.dt.bfloat16
ALU = mybir.AluOpType
ACT = mybir.ActivationFunctionType
AX_X = mybir.AxisListType.X

BATCH, SEQ, D = 128, 64, 128
CHUNK_B = 8
T = CHUNK_B * SEQ
CHUNKS = BATCH // CHUNK_B
GROUPS = T // 128
INNER, STATE, RANK, TAPS = 256, 16, 64, 4
HALVES = INNER // 128
HEADS, HEAD_D = 16, 8
PAIRS = HEADS // 2
QUADS = PAIRS // 2
EXPERTS, TOP, EXPERT_I = 8, 2, 176
FFN_ROWS = (EXPERTS + 1) * EXPERT_I
FFN_TILES = -(-FFN_ROWS // 128)
BC = 2 * STATE
RMS_EPS, LN_EPS, TOP_EPS = 1e-6, 1e-5, 1e-20

V_NORM, V_INB, V_CONVW, V_CONVB, V_DTB, V_D, V_ALOG, V_BQ, V_BK = np.cumsum(
    [0, 1, 4, HALVES * TAPS, HALVES, HALVES, HALVES, HALVES * STATE, 1]).tolist()
VEC = V_BK + 1

FRONT = [("xnT", 0), ("xnT", 1), ("hid", 0), ("hid", 1), ("gate", 0), ("gate", 1),
         ("ts", 0), ("bc", 0), ("dt", 0), ("dt", 1)]


def back_steps():
    steps = [("mout", 0), ("x1T", 0), ("q", 0), ("k", 0), ("v", 0), ("v", 1), ("score", 0)]
    for b in range(CHUNK_B):
        if b + 1 < CHUNK_B:
            steps.append(("score", b + 1))
        steps += [("turn", b), ("mix", b)]
    steps += [("aout", 0), ("x2T", 0), ("route", 0), ("up_g", 0), ("up_u", 0), ("cwT", 0), ("cw", 0)]
    for j in range(1, FFN_TILES):
        steps += [("up_g", j), ("up_u", j), ("cw", j)]
    steps.append(("down", 0))
    return steps


BACK = back_steps()
assert len(FRONT) % 2 == 0 and len(BACK) % 2 == 0
STEPS = STATE * HALVES
SUM_LAG = 3
SLOTS = STEPS + SUM_LAG


def spread(slot, total):
    return range(slot * total // SLOTS, (slot + 1) * total // SLOTS)


class Signal:

    def __init__(self, sem, per_chunk, step=1):
        self.sem, self.per_chunk, self.step = sem, per_chunk, step

    def at(self, m, k=0):
        return (m * self.per_chunk + (k + 1)) * self.step


class Chunk:

    def __init__(self, m, parity, past):
        self.m, self.parity, self.past = m, parity, past


def ring_place(stage, step, m):
    steps = FRONT if stage == "front" else BACK
    at = steps.index(step)
    if stage == "front":
        backs = max(m - 2, 0) if isinstance(m, int) else m - 2
        before = m * (len(FRONT) // 2) + backs * (len(BACK) // 2)
    else:
        fronts = min(m + 3, CHUNKS) if isinstance(m, int) else m + 3
        before = fronts * (len(FRONT) // 2) + m * (len(BACK) // 2)
    return at % 2, before + at // 2


def build(nc, x, ctx_t, vec, rows, w_in, w_xproj, w_dt, w_out, w_attn, w_router, w_gate, w_up, w_down,
          c_masks, c_sel_bc, c_sel_cw, c_ident, c_tri, out):
    with ExitStack() as stack:
        def sb(name, shape, dt=F32):
            return stack.enter_context(nc.sbuf_tensor(name, shape, dt))

        def bank(name, dt=F32):
            return stack.enter_context(nc.psum_tensor(name, [128, 2048 // mybir.dt.size(dt)], dt))

        def signal(name, per_chunk=1, step=1):
            return Signal(stack.enter_context(nc.semaphore(name)), per_chunk, step)

        vecs = sb("vecs", [128, VEC])
        rowb = sb("rowb", [128, 3, D])
        win = sb("win", [128, 4, 128])
        wxp = sb("wxp", [128, HALVES, RANK + 3 * BC])
        wdt = sb("wdt", [RANK, INNER])
        wout = sb("wout", [128, HALVES, D])
        wattn = sb("wattn", [128, 4, 128])
        wrt = sb("wrt", [128, EXPERTS])
        wg = sb("wg", [128, FFN_TILES, 128])
        wu = sb("wu", [128, FFN_TILES, 128])
        wd = sb("wd", [128, FFN_TILES, 128])
        masks = sb("masks", [128, PAIRS + 2])
        sel_bc = sb("sel_bc", [3 * BC, BC], BF16)
        sel_cw = sb("sel_cw", [128, FFN_TILES, 128], BF16)
        ident = sb("ident", [128, 128])
        ident16 = sb("ident16", [128, 128], BF16)
        tri = sb("tri", [128, EXPERTS, EXPERTS])
        a_neg = sb("a_neg", [128, HALVES, STATE])
        halfv = sb("halfv", [128, 2 + HALVES * TAPS + HALVES])
        bqs = sb("bqs", [128, 2])
        mhalf = sb("mhalf", [128, GROUPS])
        xf = sb("xf", [128, GROUPS, D])
        ss = sb("ss", [128, GROUPS])
        ms = sb("ms", [128, GROUPS])
        rms = sb("rms", [128, GROUPS])
        xn = sb("xn", [128, GROUPS, D])
        xnT = sb("xnT", [128, T])
        hpad = sb("hpad", [128, HALVES, CHUNK_B, SEQ + TAPS - 1])
        zc = sb("zc", [128, HALVES, T])
        th = sb("th", [128, T])
        gh = sb("gh", [128, HALVES, T])
        gth = sb("gth", [128, T])
        h = sb("h", [128, 2, HALVES, T])
        gate = sb("gate", [128, 2, HALVES, T])
        delta = sb("delta", [128, 2, HALVES, T])
        u = sb("u", [128, 2, HALVES, T])
        bc16 = sb("bc16", [3 * BC, 2, T], BF16)
        bc_rest = sb("bc_rest", [3 * BC, T])
        ts_sb = sb("ts_sb", [RANK, T])
        sp_a = sb("sp_a", [128, T])
        sp_r = sb("sp_r", [128, T])
        sq = sp_a
        c_rep = sb("c_rep", [128, 2, T])
        drive = sb("drive", [128, 2, T])
        state = sb("state", [128, 3, T])
        prod = sb("prod", [128, 3, T])
        ysum = sb("ysum", [128, T])
        yg = sb("yg", [128, HALVES, T])
        xb = sb("xb", [128, GROUPS, D])
        ctxT = sb("ctxT", [128, CHUNK_B, 2, SEQ])
        res = sb("res", [128, GROUPS, D])
        stats = sb("stats", [128, GROUPS, 6])
        mv = sb("mv", [128, GROUPS, 2])
        var = sb("var", [128, GROUPS])
        rstd = sb("rstd", [128, GROUPS])
        x1 = sb("x1", [128, GROUPS, D])
        x1b = sb("x1b", [128, GROUPS, D])
        x1T = sb("x1T", [128, T])
        qs = sb("qs", [128, CHUNK_B, 2, SEQ])
        kT = sb("kT", [128, T])
        km = sb("km", [128, CHUNK_B, PAIRS, SEQ])
        vm = sb("vm", [128, CHUNK_B, QUADS, 128])
        shifted = sb("shifted", [128, 2, PAIRS, SEQ])
        smax = sb("smax", [128, PAIRS])
        ex = sb("ex", [128, 2, PAIRS, SEQ])
        den = sb("den", [128, PAIRS])
        rden = sb("rden", [128, 2, PAIRS])
        exT = sb("exT", [128, QUADS, 128])
        rd_wide = sb("rd_wide", [128, 128])
        rdT = sb("rdT", [128, 128])
        aT = sb("aT", [128, T])
        x2 = sb("x2", [128, GROUPS, D])
        x2T = sb("x2T", [128, T])
        r_max = sb("r_max", [128, GROUPS])
        r_log = sb("r_log", [128, GROUPS, EXPERTS])
        r_exp = sb("r_exp", [128, GROUPS, EXPERTS])
        r_sum = sb("r_sum", [128, GROUPS])
        r_rec = sb("r_rec", [128, GROUPS])
        r_prob = sb("r_prob", [128, GROUPS, EXPERTS])
        r_gt = sb("r_gt", [128, GROUPS, EXPERTS, EXPERTS])
        r_eq = sb("r_eq", [128, GROUPS, EXPERTS, EXPERTS])
        r_rank = sb("r_rank", [128, GROUPS, EXPERTS])
        r_sel = sb("r_sel", [128, GROUPS, EXPERTS])
        r_cw = sb("r_cw", [128, GROUPS, EXPERTS])
        r_rest = sb("r_rest", [128, GROUPS, EXPERTS])
        cw16 = sb("cw16", [128, GROUPS, 128], BF16)
        cwT = sb("cwT", [128, T], BF16)
        gt = exT[:].rearrange("p a q -> p (a q)")
        ga = kT[:]
        gu = shifted[:].rearrange("p i a k -> p i (a k)")
        cwr = ex[:].rearrange("p i a k -> p i (a k)")
        acts_more = sb("acts_more", [128, FFN_TILES - CHUNK_B, T])
        acts = [km[:, j, :, :].rearrange("p a k -> p (a k)") if j < CHUNK_B else
                acts_more[:, j - CHUNK_B, :] for j in range(FFN_TILES)]
        sel_cw32 = acts_more[:].rearrange("p j t -> p (j t)")[:, 0:FFN_TILES * 128]
        sel_bc32 = zc[0:3 * BC, 0, 0:BC]
        yout = x1

        p_decay = [bank(f"p_decay{j}") for j in range(HALVES)]
        p_b, p_c = bank("p_b"), bank("p_c")
        p_y = [bank(f"p_y{j}") for j in range(HALVES)]
        p_ring = [bank(f"p_ring{i}") for i in range(2)]

        n_weights = 18
        weights_in = signal("weights_in")
        ready_const = signal("ready_const")
        consts_v = signal("consts_v")
        CONSTS = 7
        ring_full = [signal(f"ring_full{i}") for i in range(2)]
        ring_free = [signal(f"ring_free{i}") for i in range(2)]
        x_in, xb_in, out_done = (signal(n, 1, 16) for n in ("x_in", "xb_in", "out_done"))
        ctx_in = signal("ctx_in", 2, 16)
        squares_done, mean_sq, rms_ready, xn_ready = (
            signal(n) for n in ("squares_done", "mean_sq", "rms_ready", "xn_ready"))
        xnT_ready, hid_ready, gateh_ready, conv_th, gate_th, h_ready, gate_ready = (
            signal(n, 2) for n in ("xnT_ready", "hid_ready", "gateh_ready", "conv_th", "gate_th",
                                   "h_ready", "gate_ready"))
        conv_tap = signal("conv_tap", HALVES * TAPS)
        ts_ready = signal("ts_ready")
        bc_part = signal("bc_part", 5)
        relu_ready, abs_ready, spexp_ready, spln_ready, delta_ready, u_ready = (
            signal(n, 2) for n in ("relu_ready", "abs_ready", "spexp_ready", "spln_ready",
                                   "delta_ready", "u_ready"))
        b_ready, b_used, c_ready, c_copied = (
            signal(n, STATE) for n in ("b_ready", "b_used", "c_ready", "c_copied"))
        decay_ready, drive_ready, state_ready, prod_ready, prod_used = (
            signal(n, STEPS) for n in ("decay_ready", "drive_ready", "state_ready", "prod_ready",
                                       "prod_used"))
        ysum_ready, yg_ready = signal("ysum_ready", 2), signal("yg_ready", 2)
        xb_ready, x1b_ready = signal("xb_ready"), signal("x1b_ready")
        res_ready, ln_stats, ln_aggr, ln_var, ln_rstd, ln_ready = (
            signal(n, 3) for n in ("res_ready", "ln_stats", "ln_aggr", "ln_var", "ln_rstd", "ln_ready"))
        x1T_ready, q_ready, k_ready, km_ready, v_ready, aT_ready, x2T_ready = (
            signal(n) for n in ("x1T_ready", "q_ready", "k_ready", "km_ready", "v_ready", "aT_ready",
                                "x2T_ready"))
        max_ready, shift_ready, exp_ready, den_ready, rden_ready, exT_ready, rdwide_ready, rdT_ready, mixed = (
            signal(n, CHUNK_B) for n in ("max_ready", "shift_ready", "exp_ready", "den_ready",
                                         "rden_ready", "exT_ready", "rdwide_ready", "rdT_ready", "mixed"))
        route_v, route_exp, route_g = signal("route_v", 16), signal("route_exp"), signal("route_g", 2)
        cwT_ready = signal("cwT_ready")
        gt_ready, ga_ready, gu_ready, cwr_ready, act_ready = (
            signal(n, FFN_TILES) for n in ("gt_ready", "ga_ready", "gu_ready", "cwr_ready", "act_ready"))

        def column(at):
            return vecs[:, at:at + 1]

        def by_group(a):
            return a.unsqueeze(2)

        def turns(eng, turn):
            front = lambda m, parity, past: Chunk(m, parity, past)
            for t in (-1, 0, 1):
                turn(front(t + 1, (t + 1) % 2, t + 1), Chunk(t, t % 2, t) if t >= 0 else None,
                     Chunk(t - 1, (t - 1) % 2, t - 1) if t >= 1 else None)
            with eng.Fori(2, 14, 2) as t0:
                for odd in range(2):
                    t = t0 + odd if odd else t0
                    turn(front(t + 1, 1 - odd, 3), Chunk(t, odd, 2), Chunk(t - 1, 1 - odd, 1))
            for t in range(14, CHUNKS + 1):
                turn(front(t + 1, (t + 1) % 2, t + 1) if t + 1 < CHUNKS else None,
                     Chunk(t, t % 2, t) if t < CHUNKS else None, Chunk(t - 1, (t - 1) % 2, t - 1))

        block = stack.enter_context(nc.Block())

        @block.sync
        def _(sp):
            for to, src in ((vecs[:], vec), (win[:], w_in), (ident[:], c_ident), (wxp[:], w_xproj),
                            (wdt[:], w_dt), (sel_bc32, c_sel_bc), (wout[:], w_out), (wattn[:], w_attn),
                            (wrt[:], w_router), (masks[:], c_masks), (tri[:], c_tri),
                            (sel_cw32, c_sel_cw), (wg[:], w_gate),
                            (wu[:], w_up), (wd[:], w_down),
                            (rowb[:, 0, :], rows[0].partition_broadcast(128)),
                            (rowb[:, 1, :], rows[1].partition_broadcast(128)),
                            (rowb[:, 2, :], rows[2].partition_broadcast(128))):
                sp.dma_start(to, src).then_inc(weights_in.sem, 16)

            def turn(front, scan, back):
                if front:
                    if front.past >= 1:
                        sp.wait_ge(xn_ready.sem, xn_ready.at(front.m - 1))
                    sp.dma_start(xf[:], x[bass.ds(front.m * T, T), :].rearrange("(g p) d -> p g d", p=128)
                                 ).then_inc(x_in.sem, 16)
                if back:
                    if back.past >= 1:
                        sp.wait_ge(res_ready.sem, res_ready.at(back.m - 1, 1))
                    sp.dma_start(xb[:], x[bass.ds(back.m * T, T), :].rearrange("(g p) d -> p g d", p=128)
                                 ).then_inc(xb_in.sem, 16)
                    for twice in range(2):
                        sp.dma_start(ctxT[:, :, twice, :], ctx_t[:, bass.ds(back.m * T, T)].rearrange(
                            "d (b t) -> d b t", t=SEQ)).then_inc(ctx_in.sem, 16)
                    sp.wait_ge(ln_ready.sem, ln_ready.at(back.m, 2))
                    sp.dma_start(out[bass.ds(back.m * T, T), :].rearrange("(g p) d -> p g d", p=128),
                                 yout[:]).then_inc(out_done.sem, 16)

            turns(sp, turn)
            sp.wait_ge(out_done.sem, out_done.at(CHUNKS - 1))

        @block.tensor
        def _(pe):
            pe.wait_ge(weights_in.sem, 16 * n_weights)
            pe.wait_ge(consts_v.sem, CONSTS)

            def fill(stage, step, c):
                i, before = ring_place(stage, step, c.m)
                if not isinstance(before, int) or before > 0:
                    pe.wait_ge(ring_free[i].sem, before)
                return p_ring[i], ring_full[i].sem

            def front_step(step, c):
                name, i = step
                par = c.parity
                p, full = fill("front", step, c)
                if name == "xnT":
                    pe.wait_ge(xn_ready.sem, xn_ready.at(c.m))
                    for g in range(2):
                        mm = pe.transpose(p[:, g * 128:(g + 1) * 128], xn[:, 2 * i + g, :], ident[:])
                elif name in ("hid", "gate"):
                    pe.wait_ge(xnT_ready.sem, xnT_ready.at(c.m, 1))
                    mm = pe.matmul(p[:], win[:, i + 2 * (name == "gate"), :], xnT[:], start=True, stop=True)
                elif name == "ts":
                    pe.wait_ge(h_ready.sem, h_ready.at(c.m, 1))
                    for j in range(HALVES):
                        mm = pe.matmul(p[0:RANK, :], wxp[:, j, 0:RANK], h[:, par, j, :],
                                       start=j == 0, stop=j == HALVES - 1)
                elif name == "bc":
                    for j in range(HALVES):
                        mm = pe.matmul(p[0:3 * BC, :], wxp[:, j, RANK:RANK + 3 * BC], h[:, par, j, :],
                                       start=j == 0, stop=j == HALVES - 1)
                else:
                    pe.wait_ge(ts_ready.sem, ts_ready.at(c.m))
                    mm = pe.matmul(p[:], wdt[:, i * 128:(i + 1) * 128], ts_sb[:], start=True, stop=True)
                mm.then_inc(full, 1)

            def back_step(step, c):
                name, i = step
                p, full = fill("back", step, c)
                if name == "mout":
                    pe.wait_ge(yg_ready.sem, yg_ready.at(c.m, 1))
                    for g in range(GROUPS):
                        for j in range(HALVES):
                            mm = pe.matmul(p[:, g * D:(g + 1) * D], yg[:, j, g * 128:(g + 1) * 128],
                                           wout[:, j, :], start=j == 0, stop=j == HALVES - 1)
                elif name in ("x1T", "x2T"):
                    src, ln = (x1, 0) if name == "x1T" else (x2, 1)
                    pe.wait_ge(ln_ready.sem, ln_ready.at(c.m, ln))
                    for g in range(GROUPS):
                        mm = pe.transpose(p[:, g * 128:(g + 1) * 128], src[:, g, :], ident[:])
                elif name == "q":
                    pe.wait_ge(x1T_ready.sem, x1T_ready.at(c.m))
                    mm = pe.matmul(p[:], wattn[:, 0, :], x1T[:], start=True, stop=True)
                elif name == "k":
                    pe.wait_ge(ctx_in.sem, ctx_in.at(c.m, 1))
                    mm = pe.matmul(p[:], wattn[:, 1, :], ctxT[:, :, 0, :], start=True, stop=True)
                elif name == "v":
                    for b in range(4):
                        twice = ctxT[:, 4 * i + b, :, :].rearrange("d a t -> d (a t)")
                        mm = pe.matmul(p[:, b * 128:(b + 1) * 128], twice, wattn[:, 2, :],
                                       start=True, stop=True)
                elif name == "score":
                    if i == 0:
                        pe.wait_ge(q_ready.sem, q_ready.at(c.m))
                        pe.wait_ge(km_ready.sem, km_ready.at(c.m))
                    mm = pe.matmul(p[:], qs[:, i, :, :].rearrange("p s q -> p (s q)"),
                                   km[:, i, :, :].rearrange("p a k -> p (a k)"), start=True, stop=True)
                elif name == "turn":
                    pe.wait_ge(exp_ready.sem, exp_ready.at(c.m, i))
                    for q in range(QUADS):
                        mm = pe.transpose(p[:, q * 128:(q + 1) * 128],
                                          ex[:, i % 2, 2 * q:2 * q + 2, :].rearrange("p a k -> p (a k)"),
                                          ident[:])
                elif name == "mix":
                    pe.wait_ge(exT_ready.sem, exT_ready.at(c.m, i))
                    if i == 0:
                        pe.wait_ge(v_ready.sem, v_ready.at(c.m))
                    for q in range(QUADS):
                        pe.matmul(p[:, 0:128], vm[:, i, q, :], exT[:, q, :],
                                  start=q == 0, stop=q == QUADS - 1)
                    pe.wait_ge(rdwide_ready.sem, rdwide_ready.at(c.m, i))
                    mm = pe.transpose(p[:, 128:256], rd_wide[:], ident[:])
                elif name == "aout":
                    pe.wait_ge(mixed.sem, mixed.at(c.m, CHUNK_B - 1))
                    for g in range(GROUPS):
                        mm = pe.matmul(p[:, g * D:(g + 1) * D], aT[:, g * 128:(g + 1) * 128],
                                       wattn[:, 3, :], start=True, stop=True)
                elif name == "route":
                    pe.wait_ge(x2T_ready.sem, x2T_ready.at(c.m))
                    for g in range(GROUPS):
                        mm = pe.matmul(p[:, g * EXPERTS:(g + 1) * EXPERTS], x2T[:, g * 128:(g + 1) * 128],
                                       wrt[:], start=True, stop=True)
                elif name in ("up_g", "up_u"):
                    mm = pe.matmul(p[:], (wg if name == "up_g" else wu)[:, i, :], x2T[:],
                                   start=True, stop=True)
                elif name == "cwT":
                    pe.wait_ge(route_v.sem, route_v.at(c.m, 15))
                    p16 = p[:].bitcast(BF16)
                    for g in range(GROUPS):
                        mm = pe.transpose(p16[:, g * 128:(g + 1) * 128], cw16[:, g, :], ident16[:])
                elif name == "cw":
                    if i == 0:
                        pe.wait_ge(cwT_ready.sem, cwT_ready.at(c.m))
                    mm = pe.matmul(p[:], sel_cw[:, i, :], cwT[:], start=True, stop=True)
                else:
                    pe.wait_ge(act_ready.sem, act_ready.at(c.m, FFN_TILES - 1))
                    for g in range(GROUPS):
                        for j in range(FFN_TILES):
                            mm = pe.matmul(p[:, g * D:(g + 1) * D], acts[j][:, g * 128:(g + 1) * 128],
                                           wd[:, j, :], start=j == 0, stop=j == FFN_TILES - 1)
                mm.then_inc(full, 1)

            def spread_bc(c, n):
                if n == 0:
                    pe.wait_ge(bc_part.sem, bc_part.at(c.m, 4))
                if n > 0 or c.past >= 1:
                    pe.wait_ge(b_used.sem, b_used.at(c.m, n - 1))
                pe.matmul(p_b[:], sel_bc[:, n:n + 1].to_broadcast([3 * BC, 128]), bc16[:, c.parity, :],
                          start=True, stop=True).then_inc(b_ready.sem, 1)
                if n > 0 or c.past >= 1:
                    pe.wait_ge(c_copied.sem, c_copied.at(c.m, n - 1))
                pe.matmul(p_c[:], sel_bc[:, STATE + n:STATE + n + 1].to_broadcast([3 * BC, 128]), bc16[:, c.parity, :],
                          start=True, stop=True).then_inc(c_ready.sem, 1)

            def sum_n(c, k):
                n, j = divmod(k, HALVES)
                if n == 0 and c.past >= 1:
                    pe.wait_ge(ysum_ready.sem, ysum_ready.at(c.m - 1, j))
                pe.wait_ge(prod_ready.sem, prod_ready.at(c.m, k))
                pe.matmul(p_y[j][:], ident[:], prod[:, k % 3, :],
                          start=n == 0, stop=n == STATE - 1).then_inc(prod_used.sem, 1)

            def turn(front, scan, back):
                if scan:
                    spread_bc(scan, 0)
                for s in range(SLOTS):
                    if scan:
                        if s % 2 == 1 and (s + 1) // 2 < STATE:
                            spread_bc(scan, (s + 1) // 2)
                        if s >= SUM_LAG:
                            sum_n(scan, s - SUM_LAG)
                    for at in spread(s, len(FRONT) + len(BACK)):
                        if at < len(FRONT):
                            if front:
                                front_step(FRONT[at], front)
                        elif back:
                            back_step(BACK[at - len(FRONT)], back)

            turns(pe, turn)

        @block.scalar
        def _(act):
            act.wait_ge(weights_in.sem, 16 * n_weights)
            act.activation(a_neg[:].rearrange("p a n -> p (a n)"), vecs[:, V_ALOG:V_ALOG + HALVES * STATE],
                           ACT.Exp).then_inc(ready_const.sem, 1)
            act.wait_ge(consts_v.sem, CONSTS)

            def content(stage, step, c):
                i, before = ring_place(stage, step, c.m)
                act.wait_ge(ring_full[i].sem, before + 1)
                return p_ring[i], ring_free[i].sem

            def front_norm(c):
                act.wait_ge(x_in.sem, x_in.at(c.m))
                if c.past >= 1:
                    act.wait_ge(mean_sq.sem, mean_sq.at(c.m - 1))
                for g in range(GROUPS):
                    a = act.activation(sq[:, g * D:(g + 1) * D], xf[:, g, :], ACT.Square, accum_out=ss[:, g:g + 1])
                a.then_inc(squares_done.sem, 1)

            def front_step(step, c):
                name, i = step
                par = c.parity
                if name == "bc":
                    return
                p, free = content("front", step, c)
                if name == "xnT":
                    act.activation(xnT[:, i * 256:(i + 1) * 256], p[:, 0:256], ACT.Copy,
                                   scale=column(V_NORM)).then_inc(xnT_ready.sem, 1)
                    act.wait_ge(xnT_ready.sem, xnT_ready.at(c.m, i))
                    act.sem_inc(free, 1)
                elif name == "hid":
                    if c.past >= 1:
                        act.wait_ge(conv_tap.sem, conv_tap.at(c.m - 1, i * TAPS + TAPS - 1))
                    act.activation(hpad[:, i, :, TAPS - 1:], p[:].rearrange("p (b t) -> p b t", t=SEQ),
                                   ACT.Identity, bias=column(V_INB + i)).then_inc(hid_ready.sem, 1)
                    act.wait_ge(hid_ready.sem, hid_ready.at(c.m, i))
                    act.sem_inc(free, 1)
                    if c.past >= 0:
                        pass
                elif name == "gate":
                    act.activation(gh[:, i, :], p[:], ACT.Identity, scale=0.5,
                                   bias=halfv[:, i:i + 1]).then_inc(gateh_ready.sem, 1)
                    act.wait_ge(gateh_ready.sem, gateh_ready.at(c.m, i))
                    act.sem_inc(free, 1)
                    if i > 0 or c.past >= 1:
                        act.wait_ge(gate_ready.sem, gate_ready.at(c.m, i - 1))
                    act.activation(gth[:], gh[:, i, :], ACT.Tanh).then_inc(gate_th.sem, 1)
                    act.wait_ge(conv_tap.sem, conv_tap.at(c.m, i * TAPS + TAPS - 1))
                    if i == 1:
                        act.wait_ge(h_ready.sem, h_ready.at(c.m, 0))
                    act.activation(th[:], zc[:, i, :], ACT.Tanh).then_inc(conv_th.sem, 1)
                elif name == "ts":
                    act.activation(ts_sb[:], p[0:RANK, :], ACT.Copy).then_inc(ts_ready.sem, 1)
                    act.wait_ge(ts_ready.sem, ts_ready.at(c.m))
                    act.sem_inc(free, 1)
                else:
                    if i == 1:
                        act.wait_ge(delta_ready.sem, delta_ready.at(c.m, 0))
                    act.activation(sp_r[:], p[:], ACT.Relu, bias=column(V_DTB + i)).then_inc(relu_ready.sem, 1)
                    act.activation(sp_a[:], p[:], ACT.Abs, bias=column(V_DTB + i)).then_inc(abs_ready.sem, 1)
                    act.wait_ge(abs_ready.sem, abs_ready.at(c.m, i))
                    act.sem_inc(free, 1)
                    act.activation(sp_a[:], sp_a[:], ACT.Exp, scale=-1.0).then_inc(spexp_ready.sem, 1)
                    act.wait_ge(spexp_ready.sem, spexp_ready.at(c.m, i))
                    act.activation(sp_a[:], sp_a[:], ACT.Ln, bias=1.0).then_inc(spln_ready.sem, 1)

            def back_step(step, c):
                name, i = step
                if name == "turn":
                    act.wait_ge(rden_ready.sem, rden_ready.at(c.m, i))
                    act.activation(rd_wide[:].rearrange("p (s a d) -> p s a d", s=2, d=HEAD_D),
                                   rden[:, i % 2, :].unsqueeze(1).unsqueeze(3).to_broadcast(
                                       [128, 2, PAIRS, HEAD_D]), ACT.Copy).then_inc(rdwide_ready.sem, 1)
                if name in ("mout", "v", "aout", "up_u", "down", "score", "route"):
                    if name == "score":
                        act.wait_ge(shift_ready.sem, shift_ready.at(c.m, i))
                        act.activation(ex[:, i % 2, :, :].rearrange("p a k -> p (a k)"),
                                       shifted[:, i % 2, :, :].rearrange("p a k -> p (a k)"),
                                       ACT.Exp).then_inc(exp_ready.sem, 1)
                    if name == "route":
                        act.wait_ge(route_v.sem, route_v.at(c.m, 1))
                        act.activation(r_exp[:].rearrange("p g e -> p (g e)"),
                                       r_log[:].rearrange("p g e -> p (g e)"),
                                       ACT.Exp).then_inc(route_exp.sem, 1)
                    return
                p, free = content("back", step, c)
                if name == "x1T":
                    act.activation(x1T[:], p[:], ACT.Copy).then_inc(x1T_ready.sem, 1)
                    act.wait_ge(x1T_ready.sem, x1T_ready.at(c.m))
                    act.sem_inc(free, 1)
                elif name == "x2T":
                    act.activation(x2T[:], p[:], ACT.Copy).then_inc(x2T_ready.sem, 1)
                    act.wait_ge(x2T_ready.sem, x2T_ready.at(c.m))
                    act.sem_inc(free, 1)
                elif name == "q":
                    for s in range(2):
                        a = act.activation(qs[:, :, s, :], p[:].rearrange("p (b t) -> p b t", t=SEQ),
                                           ACT.Identity, scale=masks[:, PAIRS + s:PAIRS + s + 1],
                                           bias=bqs[:, s:s + 1])
                    a.then_inc(q_ready.sem, 1)
                    act.wait_ge(q_ready.sem, q_ready.at(c.m))
                    act.sem_inc(free, 1)
                elif name == "k":
                    act.activation(kT[:], p[:], ACT.Identity, bias=column(V_BK)).then_inc(k_ready.sem, 1)
                    act.wait_ge(k_ready.sem, k_ready.at(c.m))
                    act.sem_inc(free, 1)
                elif name == "turn":
                    act.activation(exT[:].rearrange("p a q -> p (a q)"), p[:],
                                   ACT.Copy).then_inc(exT_ready.sem, 1)
                    act.wait_ge(exT_ready.sem, exT_ready.at(c.m, i))
                    act.sem_inc(free, 1)
                elif name == "mix":
                    if i > 0 or c.past >= 1:
                        act.wait_ge(mixed.sem, mixed.at(c.m, i - 1))
                    act.activation(rdT[:], p[:, 128:256], ACT.Copy).then_inc(rdT_ready.sem, 1)
                elif name == "up_g":
                    if i > 0 or c.past >= 1:
                        act.wait_ge(ga_ready.sem, ga_ready.at(c.m, i - 1))
                    act.activation(gt, p[:], ACT.Tanh, scale=0.5).then_inc(gt_ready.sem, 1)
                elif name == "cwT":
                    act.activation(cwT[:], p[:].bitcast(BF16)[:, 0:T], ACT.Copy).then_inc(cwT_ready.sem, 1)
                    act.wait_ge(cwT_ready.sem, cwT_ready.at(c.m))
                    act.sem_inc(free, 1)
                else:
                    if i > 1 or c.past >= 1:
                        act.wait_ge(act_ready.sem, act_ready.at(c.m, i - 2))
                    act.activation(cwr[:, i % 2, :], p[:], ACT.Copy).then_inc(cwr_ready.sem, 1)
                    act.wait_ge(cwr_ready.sem, cwr_ready.at(c.m, i))
                    act.sem_inc(free, 1)

            def copy_c(c, n):
                act.wait_ge(c_ready.sem, c_ready.at(c.m, n))
                if n > 1 or c.past >= 1:
                    act.wait_ge(prod_ready.sem, prod_ready.at(c.m, HALVES * (n - 1) - 1))
                act.activation(c_rep[:, n % 2, :], p_c[:], ACT.Copy).then_inc(c_copied.sem, 1)

            def decays(c, k):
                n, j = divmod(k, HALVES)
                if k == 0:
                    act.wait_ge(delta_ready.sem, delta_ready.at(c.m, 1))
                if n > 0 or c.past >= 1:
                    act.wait_ge(state_ready.sem, state_ready.at(c.m, k - HALVES))
                act.activation(p_decay[j][:].rearrange("p (b t) -> p b t", t=SEQ)[:, :, 1:],
                               delta[:, c.parity, j, :].rearrange("p (b t) -> p b t", t=SEQ)[:, :, 1:],
                               ACT.Exp, scale=a_neg[:, j, n:n + 1]).then_inc(decay_ready.sem, 1)

            def turn(front, scan, back):
                for s in range(SLOTS):
                    if scan and s < STEPS:
                        decays(scan, s)
                        if s % 2 == 0:
                            copy_c(scan, s // 2)
                    if s == 0 and front:
                        front_norm(front)
                    for at in spread(s, len(FRONT) + len(BACK)):
                        if at < len(FRONT):
                            if front:
                                front_step(FRONT[at], front)
                        elif back:
                            back_step(BACK[at - len(FRONT)], back)

            turns(act, turn)

        @block.vector
        def _(dve):
            for j in range(HALVES):
                dve.memset(p_decay[j][:], 0.0)
            dve.memset(hpad[:], 0.0)
            dve.memset(vm[:], 0.0)
            dve.memset(mhalf[:], -0.5)
            dve.memset(cw16[:], 0.0).then_inc(consts_v.sem, 1)
            dve.wait_ge(consts_v.sem, 1)
            dve.memset(cw16[:, :, 3 * EXPERTS:3 * EXPERTS + 1], 1.0).then_inc(consts_v.sem, 1)
            dve.wait_ge(weights_in.sem, 16 * n_weights)
            dve.tensor_scalar(halfv[:, 0:2], vecs[:, V_INB + 2:V_INB + 4], 0.5, None,
                              ALU.mult).then_inc(consts_v.sem, 1)
            dve.tensor_scalar(halfv[:, 2:], vecs[:, V_CONVW:V_CONVW + HALVES * TAPS + HALVES], 0.5, None,
                              ALU.mult).then_inc(consts_v.sem, 1)
            dve.tensor_scalar(bqs[:], masks[:, PAIRS:PAIRS + 2], column(V_BQ), None,
                              ALU.mult).then_inc(consts_v.sem, 1)
            dve.tensor_copy(ident16[:], ident[:])
            dve.tensor_copy(sel_bc[:], sel_bc32)
            dve.tensor_copy(sel_cw[:].rearrange("p j c -> p (j c)"), sel_cw32).then_inc(consts_v.sem, 1)
            dve.wait_ge(ready_const.sem, 1)
            dve.tensor_scalar(a_neg[:].rearrange("p a n -> p (a n)"), a_neg[:].rearrange("p a n -> p (a n)"),
                              -1.0, None, ALU.mult).then_inc(consts_v.sem, 1)
            dve.wait_ge(consts_v.sem, CONSTS)

            def content(stage, step, c):
                i, before = ring_place(stage, step, c.m)
                dve.wait_ge(ring_full[i].sem, before + 1)
                return p_ring[i], ring_free[i].sem

            def front_norm(c):
                dve.wait_ge(squares_done.sem, squares_done.at(c.m))
                if c.past >= 1:
                    dve.wait_ge(rms_ready.sem, rms_ready.at(c.m - 1))
                dve.tensor_scalar(ms[:], ss[:], 1.0 / D, RMS_EPS, ALU.mult, ALU.add).then_inc(mean_sq.sem, 1)
                dve.wait_ge(rms_ready.sem, rms_ready.at(c.m))
                if c.past >= 1:
                    dve.wait_ge(xnT_ready.sem, xnT_ready.at(c.m - 1, 1))
                dve.tensor_tensor(xn[:], xf[:], by_group(rms[:]).to_broadcast([128, GROUPS, D]),
                                  ALU.mult).then_inc(xn_ready.sem, 1)

            def convolve(c, j):
                dve.wait_ge(hid_ready.sem, hid_ready.at(c.m, j))
                z = zc[:, j, :].rearrange("p (b t) -> p b t", t=SEQ)
                for k in range(TAPS):
                    w = halfv[:, 2 + j * TAPS + k:3 + j * TAPS + k]
                    if k == 0:
                        if c.past >= 1:
                            dve.wait_ge(h_ready.sem, h_ready.at(c.m - 1, j))
                        b = halfv[:, 2 + HALVES * TAPS + j:3 + HALVES * TAPS + j]
                        dve.tensor_scalar(z, hpad[:, j, :, 0:SEQ], w, b, ALU.mult,
                                          ALU.add).then_inc(conv_tap.sem, 1)
                    else:
                        dve.wait_ge(conv_tap.sem, conv_tap.at(c.m, j * TAPS + k - 1))
                        dve.scalar_tensor_tensor(z, hpad[:, j, :, k:k + SEQ], w, z, ALU.mult,
                                                 ALU.add).then_inc(conv_tap.sem, 1)

            def front_step(step, c):
                name, i = step
                par = c.parity
                if name in ("xnT", "ts"):
                    return
                if name == "hid":
                    convolve(c, i)
                elif name == "gate":
                    dve.wait_ge(gate_th.sem, gate_th.at(c.m, i))
                    dve.scalar_tensor_tensor(gate[:, par, i, :], gth[:], 1.0, gh[:, i, :], ALU.add,
                                             ALU.mult).then_inc(gate_ready.sem, 1)
                    dve.wait_ge(conv_th.sem, conv_th.at(c.m, i))
                    dve.scalar_tensor_tensor(h[:, par, i, :], th[:], 1.0, zc[:, i, :], ALU.add,
                                             ALU.mult).then_inc(h_ready.sem, 1)
                elif name == "bc":
                    p, free = content("front", step, c)
                    if c.past >= 2:
                        dve.wait_ge(c_ready.sem, c_ready.at(c.m - 2, STATE - 1))
                    s16 = bc16[:, par, :]
                    dve.tensor_copy(s16, p[0:3 * BC, :]).then_inc(bc_part.sem, 1)
                    dve.wait_ge(bc_part.sem, bc_part.at(c.m, 0))
                    for q in (1, 2):
                        r = slice(q * BC, (q + 1) * BC)
                        d = dve.tensor_tensor(bc_rest[r, :], p[r, :], s16[r, :], ALU.subtract)
                    d.then_inc(bc_part.sem, 1)
                    dve.wait_ge(bc_part.sem, bc_part.at(c.m, 1))
                    dve.sem_inc(free, 1)
                    for q in (1, 2):
                        r = slice(q * BC, (q + 1) * BC)
                        d = dve.tensor_copy(s16[r, :], bc_rest[r, :])
                    d.then_inc(bc_part.sem, 1)
                    dve.wait_ge(bc_part.sem, bc_part.at(c.m, 2))
                    r = slice(2 * BC, 3 * BC)
                    dve.tensor_tensor(bc_rest[r, :], bc_rest[r, :], s16[r, :],
                                      ALU.subtract).then_inc(bc_part.sem, 1)
                    dve.wait_ge(bc_part.sem, bc_part.at(c.m, 3))
                    dve.tensor_copy(s16[r, :], bc_rest[r, :]).then_inc(bc_part.sem, 1)
                else:
                    dve.wait_ge(spln_ready.sem, spln_ready.at(c.m, i))
                    if c.past >= 2 and i == 0:
                        dve.wait_ge(decay_ready.sem, decay_ready.at(c.m - 2, STEPS - 1))
                    dve.tensor_tensor(delta[:, par, i, :], sp_r[:], sp_a[:], ALU.add
                                      ).then_inc(delta_ready.sem, 1)
                    dve.wait_ge(delta_ready.sem, delta_ready.at(c.m, i))
                    dve.tensor_tensor(u[:, par, i, :], delta[:, par, i, :], h[:, par, i, :], ALU.mult
                                      ).then_inc(u_ready.sem, 1)

            def layer_norm(c, ln, to):
                dve.wait_ge(res_ready.sem, res_ready.at(c.m, ln))
                for g in range(GROUPS):
                    d = dve.bn_stats(stats[:, g, :], res[:, g, :])
                d.then_inc(ln_stats.sem, 1)
                dve.wait_ge(consts_v.sem, CONSTS)
                dve.wait_ge(ln_stats.sem, ln_stats.at(c.m, ln))
                for g in range(GROUPS):
                    d = dve.bn_aggr(mv[:, g, :], stats[:, g, :])
                d.then_inc(ln_aggr.sem, 1)
                dve.wait_ge(ln_aggr.sem, ln_aggr.at(c.m, ln))
                dve.tensor_scalar(var[:], mv[:, :, 1], LN_EPS, None, ALU.add).then_inc(ln_var.sem, 1)
                dve.wait_ge(ln_rstd.sem, ln_rstd.at(c.m, ln))
                for g in range(GROUPS):
                    d = dve.tensor_scalar(to[:, g, :], res[:, g, :], mv[:, g, 0:1], rstd[:, g:g + 1],
                                          ALU.subtract, ALU.mult)
                d.then_inc(ln_ready.sem, 1)

            def route(c, p, free):
                at = lambda k: route_v.at(c.m, k)
                wide = [128, GROUPS, EXPERTS]
                dve.tensor_reduce(r_max[:], p[:, 0:GROUPS * EXPERTS].rearrange("p (g e) -> p g e", e=EXPERTS),
                                  AX_X, ALU.max).then_inc(route_v.sem, 1)
                dve.wait_ge(route_v.sem, at(0))
                dve.tensor_tensor(r_log[:], p[:, 0:GROUPS * EXPERTS].rearrange("p (g e) -> p g e", e=EXPERTS),
                                  by_group(r_max[:]).to_broadcast(wide), ALU.subtract
                                  ).then_inc(route_v.sem, 1)
                dve.wait_ge(route_v.sem, at(1))
                dve.sem_inc(free, 1)
                dve.wait_ge(route_exp.sem, route_exp.at(c.m))
                dve.tensor_reduce(r_sum[:], r_exp[:], AX_X, ALU.add).then_inc(route_v.sem, 1)
                dve.wait_ge(route_v.sem, at(2))
                dve.reciprocal(r_rec[:], r_sum[:]).then_inc(route_v.sem, 1)
                dve.wait_ge(route_v.sem, at(3))
                dve.tensor_tensor(r_prob[:], r_exp[:], by_group(r_rec[:]).to_broadcast(wide), ALU.mult
                                  ).then_inc(route_v.sem, 1)
                dve.wait_ge(route_v.sem, at(4))
                mine = r_prob[:].unsqueeze(3).to_broadcast([128, GROUPS, EXPERTS, EXPERTS])
                other = r_prob[:].unsqueeze(2).to_broadcast([128, GROUPS, EXPERTS, EXPERTS])
                dve.tensor_tensor(r_eq[:], other, mine, ALU.is_equal)
                dve.tensor_tensor(r_gt[:], other, mine, ALU.is_gt).then_inc(route_v.sem, 1)
                dve.wait_ge(route_g.sem, route_g.at(c.m, 1))
                dve.tensor_reduce(r_rank[:], r_gt[:], AX_X, ALU.add).then_inc(route_v.sem, 1)
                dve.wait_ge(route_v.sem, at(6))
                dve.scalar_tensor_tensor(r_sel[:], r_rank[:], float(TOP), r_prob[:], ALU.is_lt, ALU.mult
                                         ).then_inc(route_v.sem, 1)
                dve.wait_ge(route_v.sem, at(7))
                dve.tensor_reduce(r_sum[:], r_sel[:], AX_X, ALU.add).then_inc(route_v.sem, 1)
                dve.wait_ge(route_v.sem, at(8))
                dve.tensor_scalar(r_max[:], r_sum[:], TOP_EPS, None, ALU.add).then_inc(route_v.sem, 1)
                dve.wait_ge(route_v.sem, at(9))
                dve.reciprocal(r_rec[:], r_max[:]).then_inc(route_v.sem, 1)
                dve.wait_ge(route_v.sem, at(10))
                dve.tensor_tensor(r_cw[:], r_sel[:], by_group(r_rec[:]).to_broadcast(wide), ALU.mult
                                  ).then_inc(route_v.sem, 1)
                dve.wait_ge(route_v.sem, at(11))
                E = EXPERTS
                dve.tensor_copy(cw16[:, :, 0:E], r_cw[:]).then_inc(route_v.sem, 1)
                dve.wait_ge(route_v.sem, at(12))
                dve.tensor_tensor(r_rest[:], r_cw[:], cw16[:, :, 0:E], ALU.subtract
                                  ).then_inc(route_v.sem, 1)
                dve.wait_ge(route_v.sem, at(13))
                dve.tensor_copy(cw16[:, :, E:2 * E], r_rest[:]).then_inc(route_v.sem, 1)
                dve.wait_ge(route_v.sem, at(14))
                dve.tensor_tensor(cw16[:, :, 2 * E:3 * E], r_rest[:], cw16[:, :, E:2 * E], ALU.subtract
                                  ).then_inc(route_v.sem, 1)

            def back_step(step, c):
                name, i = step
                if name in ("x1T", "x2T", "q", "k", "turn", "cwT", "cw"):
                    return
                p, free = content("back", step, c)
                if name in ("mout", "aout", "down"):
                    ln, add, to = {"mout": (0, xb, x1), "aout": (1, x1b, x2), "down": (2, x2, yout)}[name]
                    if name == "mout":
                        dve.wait_ge(xb_ready.sem, xb_ready.at(c.m))
                        if c.past >= 1:
                            dve.wait_ge(out_done.sem, out_done.at(c.m - 1))
                    elif name == "aout":
                        dve.wait_ge(x1b_ready.sem, x1b_ready.at(c.m))
                    dve.tensor_tensor(res[:].rearrange("p g d -> p (g d)"), p[:],
                                      add[:].rearrange("p g d -> p (g d)"), ALU.add
                                      ).then_inc(res_ready.sem, 1)
                    dve.wait_ge(res_ready.sem, res_ready.at(c.m, ln))
                    dve.sem_inc(free, 1)
                    layer_norm(c, ln, to)
                elif name == "v":
                    for half in range(2):
                        r = slice(64 * half, 64 * half + 64)
                        for s in range(2):
                            src = p[r, :].rearrange("p (b s q a d) -> p b s q a d", b=4, s=2, q=QUADS, a=2)[
                                :, :, s, :, half, :]
                            bias = rowb[r, 1, :].rearrange("p (s q a d) -> p s q a d", s=2, q=QUADS, a=2)[
                                :, s, :, half, :].unsqueeze(1).to_broadcast([64, 4, QUADS, HEAD_D])
                            base = vm[r, 4 * i:4 * i + 4, :, :]
                            part = list(base.ap[:1]) + [(QUADS * 128, 4), (128 + 2 * HEAD_D, QUADS), (1, HEAD_D)]
                            to = bass.AP(base.tensor, base.offset + 64 * s + HEAD_D * half, part)
                            d = dve.tensor_tensor(to, src, bias, ALU.add)
                    if i == 0:
                        d.then_inc(free, 1)
                    else:
                        d.then_inc(v_ready.sem, 1)
                        dve.wait_ge(v_ready.sem, v_ready.at(c.m))
                        dve.sem_inc(free, 1)
                elif name == "score":
                    s3 = p[:].rearrange("p (a k) -> p a k", k=SEQ)
                    dve.tensor_reduce(smax[:], s3, AX_X, ALU.max).then_inc(max_ready.sem, 1)
                    dve.wait_ge(max_ready.sem, max_ready.at(c.m, i))
                    dve.tensor_tensor(shifted[:, i % 2, :, :], s3,
                                      by_group(smax[:]).to_broadcast([128, PAIRS, SEQ]), ALU.subtract
                                      ).then_inc(shift_ready.sem, 1)
                    dve.wait_ge(shift_ready.sem, shift_ready.at(c.m, i))
                    dve.sem_inc(free, 1)
                    dve.wait_ge(exp_ready.sem, exp_ready.at(c.m, i))
                    dve.tensor_reduce(den[:], ex[:, i % 2, :, :], AX_X, ALU.add).then_inc(den_ready.sem, 1)
                    dve.wait_ge(den_ready.sem, den_ready.at(c.m, i))
                    dve.reciprocal(rden[:, i % 2, :], den[:]).then_inc(rden_ready.sem, 1)
                elif name == "mix":
                    dve.wait_ge(rdT_ready.sem, rdT_ready.at(c.m, i))
                    for s in range(2):
                        r = slice(64 * s, 64 * s + 64)
                        d = dve.tensor_tensor(aT[r, i * SEQ:(i + 1) * SEQ], p[r, 64 * s:64 * s + 64],
                                              rdT[r, 64 * s:64 * s + 64], ALU.mult)
                    d.then_inc(mixed.sem, 1)
                    dve.wait_ge(mixed.sem, mixed.at(c.m, i))
                    dve.sem_inc(free, 1)
                elif name == "route":
                    route(c, p, free)
                elif name == "up_g":
                    dve.wait_ge(gt_ready.sem, gt_ready.at(c.m, i))
                    dve.scalar_tensor_tensor(ga, gt, 1.0, p[:], ALU.add, ALU.mult
                                             ).then_inc(ga_ready.sem, 1)
                    dve.wait_ge(ga_ready.sem, ga_ready.at(c.m, i))
                    dve.sem_inc(free, 1)
                elif name == "up_u":
                    if i > 1 or c.past >= 1:
                        dve.wait_ge(act_ready.sem, act_ready.at(c.m, i - 2))
                    dve.tensor_tensor(gu[:, i % 2, :], ga, p[:], ALU.mult).then_inc(gu_ready.sem, 1)
                    dve.wait_ge(gu_ready.sem, gu_ready.at(c.m, i))
                    dve.sem_inc(free, 1)

            def drives(c, n):
                if n == 0:
                    dve.wait_ge(u_ready.sem, u_ready.at(c.m, 1))
                dve.wait_ge(b_ready.sem, b_ready.at(c.m, n))
                for j in range(HALVES):
                    if n > 0 or c.past >= 1:
                        dve.wait_ge(state_ready.sem, state_ready.at(c.m, HALVES * (n - 1) + j))
                    d = dve.tensor_tensor(drive[:, j, :], u[:, c.parity, j, :], p_b[:], ALU.mult)
                    d.then_inc(drive_ready.sem, 1)
                dve.wait_ge(drive_ready.sem, drive_ready.at(c.m, HALVES * n + 1))
                dve.sem_inc(b_used.sem, 1)

            def scans(c, k):
                n, j = divmod(k, HALVES)
                dve.wait_ge(decay_ready.sem, decay_ready.at(c.m, k))
                if k >= 3 or c.past >= 1:
                    dve.wait_ge(prod_ready.sem, prod_ready.at(c.m, k - 3))
                dve.tensor_tensor_scan(state[:, k % 3, :], p_decay[j][:], drive[:, j, :], 0.0,
                                       ALU.mult, ALU.add).then_inc(state_ready.sem, 1)

            def gate_sum(c, j):
                dve.wait_ge(prod_used.sem, prod_used.at(c.m, STEPS - HALVES + j))
                if j > 0:
                    dve.wait_ge(yg_ready.sem, yg_ready.at(c.m, j - 1))
                dve.scalar_tensor_tensor(ysum[:], h[:, c.parity, j, :], column(V_D + j), p_y[j][:],
                                         ALU.mult, ALU.add).then_inc(ysum_ready.sem, 1)
                dve.wait_ge(ysum_ready.sem, ysum_ready.at(c.m, j))
                if c.past >= 1 and j == 0:
                    dve.wait_ge(res_ready.sem, res_ready.at(c.m - 1, 0))
                dve.tensor_tensor(yg[:, j, :], ysum[:], gate[:, c.parity, j, :], ALU.mult
                                  ).then_inc(yg_ready.sem, 1)

            def turn(front, scan, back):
                for s in range(SLOTS):
                    if scan and s < STEPS:
                        if s % 2 == 0:
                            drives(scan, s // 2)
                        scans(scan, s)
                    if s == 0 and front:
                        front_norm(front)
                    for at in spread(s, len(FRONT) + len(BACK)):
                        if at < len(FRONT):
                            if front:
                                front_step(FRONT[at], front)
                        elif back:
                            back_step(BACK[at - len(FRONT)], back)
                if scan:
                    for j in range(HALVES):
                        gate_sum(scan, j)

            turns(dve, turn)

        @block.gpsimd
        def _(pool):
            pool.wait_ge(weights_in.sem, 16 * n_weights)
            pool.wait_ge(consts_v.sem, CONSTS)

            def front_norm(c):
                pool.wait_ge(mean_sq.sem, mean_sq.at(c.m))
                if c.past >= 1:
                    pool.wait_ge(xn_ready.sem, xn_ready.at(c.m - 1))
                pool.tensor_tensor(rms[:], ms[:], mhalf[:], ALU.pow).then_inc(rms_ready.sem, 1)

            def ln_root(c, ln):
                pool.wait_ge(ln_var.sem, ln_var.at(c.m, ln))
                pool.tensor_tensor(rstd[:], var[:], mhalf[:], ALU.pow).then_inc(ln_rstd.sem, 1)

            def back_step(step, c):
                name, i = step
                if name == "mout":
                    pool.wait_ge(xb_in.sem, xb_in.at(c.m))
                    pool.tensor_tensor(xb[:], xb[:], rowb[:, 0, :].unsqueeze(1).to_broadcast(
                        [128, GROUPS, D]), ALU.add).then_inc(xb_ready.sem, 1)
                    ln_root(c, 0)
                elif name == "x1T":
                    pool.wait_ge(ln_ready.sem, ln_ready.at(c.m, 0))
                    pool.tensor_tensor(x1b[:], x1[:], rowb[:, 2, :].unsqueeze(1).to_broadcast(
                        [128, GROUPS, D]), ALU.add).then_inc(x1b_ready.sem, 1)
                elif name == "k":
                    pool.wait_ge(consts_v.sem, CONSTS)
                    pool.wait_ge(k_ready.sem, k_ready.at(c.m))
                    for a in range(PAIRS):
                        g = pool.tensor_scalar(km[:, :, a, :], kT[:].rearrange("p (b t) -> p b t", t=SEQ),
                                               masks[:, a:a + 1], 0.0, ALU.mult, ALU.add)
                    g.then_inc(km_ready.sem, 1)
                elif name == "aout":
                    ln_root(c, 1)
                elif name == "down":
                    ln_root(c, 2)
                elif name == "route":
                    pool.wait_ge(route_v.sem, route_v.at(c.m, 5))
                    pool.tensor_tensor(r_eq[:], r_eq[:], tri[:].unsqueeze(1).to_broadcast(
                        [128, GROUPS, EXPERTS, EXPERTS]), ALU.mult).then_inc(route_g.sem, 1)
                    pool.wait_ge(route_g.sem, route_g.at(c.m, 0))
                    pool.tensor_tensor(r_gt[:], r_gt[:], r_eq[:], ALU.add).then_inc(route_g.sem, 1)
                elif name == "cw":
                    pool.wait_ge(gu_ready.sem, gu_ready.at(c.m, i))
                    pool.wait_ge(cwr_ready.sem, cwr_ready.at(c.m, i))
                    if i == 0 and c.past >= 1:
                        pool.wait_ge(res_ready.sem, res_ready.at(c.m - 1, 2))
                    pool.tensor_tensor(acts[i], gu[:, i % 2, :], cwr[:, i % 2, :], ALU.mult
                                       ).then_inc(act_ready.sem, 1)

            def products(c, k):
                n, j = divmod(k, HALVES)
                pool.wait_ge(state_ready.sem, state_ready.at(c.m, k))
                pool.wait_ge(c_copied.sem, c_copied.at(c.m, n))
                if k >= 3 or c.past >= 1:
                    pool.wait_ge(prod_used.sem, prod_used.at(c.m, k - 3))
                pool.tensor_tensor(prod[:, k % 3, :], state[:, k % 3, :], c_rep[:, n % 2, :], ALU.mult
                                   ).then_inc(prod_ready.sem, 1)

            def turn(front, scan, back):
                for s in range(SLOTS):
                    if scan and s < STEPS:
                        products(scan, s)
                    if s == 0 and front:
                        front_norm(front)
                    for at in spread(s, len(FRONT) + len(BACK)):
                        if at >= len(FRONT) and back:
                            back_step(BACK[at - len(FRONT)], back)

            turns(pool, turn)


def constants():
    r = np.arange(128)
    masks = np.zeros((128, PAIRS + 2), np.float32)
    masks[r, (r // HEAD_D) % PAIRS] = 1.0
    masks[r, PAIRS + r // 64] = HEAD_D ** -0.5
    sel_bc = np.tile(np.eye(BC, dtype=np.float32), (3, 1))
    sel_cw = np.zeros((128, FFN_TILES * 128), np.float32)
    col = np.arange(FFN_ROWS)
    expert = col // EXPERT_I
    for part in range(3):
        routed = expert < EXPERTS
        sel_cw[part * EXPERTS + expert[routed], col[routed]] = 0.5
    sel_cw[3 * EXPERTS, col[expert == EXPERTS]] = 0.5
    e = np.arange(EXPERTS)
    tri = np.broadcast_to((e[None, :] < e[:, None]).astype(np.float32), (128, EXPERTS, EXPERTS))
    return {
        "c_masks": masks,
        "c_sel_bc": sel_bc,
        "c_sel_cw": sel_cw,
        "c_ident": np.eye(128, dtype=np.float32),
        "c_tri": np.ascontiguousarray(tri),
    }


def kernel(x, ctx_1024, L0_attn_norm_scale, L0_attn_in_w, L0_attn_in_b, L0_attn_conv_w, L0_attn_conv_b,
           L0_attn_xproj_w, L0_attn_dt_w, L0_attn_dt_b, L0_attn_A_log, L0_attn_D, L0_attn_out_w,
           L0_attn_out_b, L0_xattn_Wq, L0_xattn_bq, L0_xattn_Wk, L0_xattn_bk, L0_xattn_Wv, L0_xattn_bv,
           L0_xattn_Wo, L0_xattn_bo, L0_ffn_w_router, L0_ffn_wg, L0_ffn_wu, L0_ffn_wd, L0_ffn_wg_s,
           L0_ffn_wu_s, L0_ffn_wd_s):
    import concourse.bacc as bacc
    from concourse.bass_utils import run_bass_kernel_spmd

    def halves(a):
        a = np.asarray(a)
        return np.moveaxis(a.reshape(a.shape[:-1] + (HALVES, 128)), -1, 0).swapaxes(1, -1).reshape(128, -1)

    vec = np.concatenate([
        np.asarray(L0_attn_norm_scale).reshape(128, 1),
        np.asarray(L0_attn_in_b).reshape(4, 128).T,
        halves(L0_attn_conv_w), halves(L0_attn_conv_b), halves(L0_attn_dt_b), halves(L0_attn_D),
        halves(np.asarray(L0_attn_A_log).T),
        np.asarray(L0_xattn_bq).reshape(128, 1), np.asarray(L0_xattn_bk).reshape(128, 1)], axis=1)
    rows = np.stack([np.asarray(L0_attn_out_b), np.asarray(L0_xattn_bv), np.asarray(L0_xattn_bo)])
    xproj = np.asarray(L0_attn_xproj_w).reshape(HALVES, 128, RANK + BC)
    xproj = np.concatenate([xproj[:, :, :RANK]] + [xproj[:, :, RANK:]] * 3, axis=2).transpose(1, 0, 2)
    attn = np.stack([np.asarray(w).T for w in (L0_xattn_Wq, L0_xattn_Wk, L0_xattn_Wv, L0_xattn_Wo)], axis=1)
    pad = FFN_TILES * 128 - FFN_ROWS

    def up(routed, shared):
        a = np.asarray(routed).transpose(1, 0, 2).reshape(D, EXPERTS * EXPERT_I)
        shared = np.asarray(shared)
        return np.concatenate([a, shared, np.zeros((D, pad), shared.dtype)], axis=1).reshape(
            D, FFN_TILES, 128)

    shared = np.asarray(L0_ffn_wd_s)
    down = np.concatenate([np.asarray(L0_ffn_wd).reshape(EXPERTS * EXPERT_I, D), shared,
                           np.zeros((pad, D), shared.dtype)], axis=0)
    arrays = {
        "x": np.asarray(x).reshape(BATCH * SEQ, D),
        "ctx_t": np.asarray(ctx_1024).reshape(BATCH * SEQ, D).T,
        "vec": vec, "rows": rows,
        "w_in": np.asarray(L0_attn_in_w).reshape(128, 4, 128),
        "w_xproj": xproj, "w_dt": np.asarray(L0_attn_dt_w),
        "w_out": np.asarray(L0_attn_out_w).reshape(HALVES, 128, D).transpose(1, 0, 2),
        "w_attn": attn, "w_router": np.asarray(L0_ffn_w_router).T,
        "w_gate": up(L0_ffn_wg, L0_ffn_wg_s), "w_up": up(L0_ffn_wu, L0_ffn_wu_s),
        "w_down": down.reshape(FFN_TILES, 128, D).transpose(1, 0, 2),
        **constants(),
    }
    arrays = {k: np.ascontiguousarray(v) for k, v in arrays.items()}
    nc = bacc.Bacc("TRN2", target_bir_lowering=False, num_devices=1)
    args = {k: nc.dram_tensor(f"in_{k}", v.shape, mybir.dt.from_np(v.dtype), kind="ExternalInput").ap()
            for k, v in arrays.items()}
    out = nc.dram_tensor("out_y", (BATCH * SEQ, D), F32, kind="ExternalOutput").ap()
    build(nc, out=out, **args)
    r = run_bass_kernel_spmd(nc, [{f"in_{k}": v for k, v in arrays.items()}], core_ids=[0])
    return r.results[0]["out_y"].reshape(BATCH, SEQ, D)
```

```python
from contextlib import ExitStack

import numpy as np

import concourse.bass as bass
from concourse import mybir

F32 = mybir.dt.float32
BF16 = mybir.dt.bfloat16
ALU = mybir.AluOpType
ACT = mybir.ActivationFunctionType
AX_X = mybir.AxisListType.X

BATCH, SEQ, D = 128, 64, 128
CHUNK_B = 8
T = CHUNK_B * SEQ
CHUNKS = BATCH // CHUNK_B
GROUPS = T // 128
INNER, STATE, RANK, TAPS = 256, 16, 64, 4
HALVES = INNER // 128
HEADS, HEAD_D = 16, 8
PAIRS = HEADS // 2
QUADS = PAIRS // 2
EXPERTS, TOP, EXPERT_I = 8, 2, 176
FFN_ROWS = (EXPERTS + 1) * EXPERT_I
FFN_TILES = -(-FFN_ROWS // 128)
BC = 2 * STATE
RMS_EPS, LN_EPS, TOP_EPS = 1e-6, 1e-5, 1e-20

V_NORM, V_INB, V_CONVW, V_CONVB, V_DTB, V_D, V_ALOG, V_BQ, V_BK = np.cumsum(
    [0, 1, 4, HALVES * TAPS, HALVES, HALVES, HALVES, HALVES * STATE, 1]).tolist()
VEC = V_BK + 1

STEPS = STATE * HALVES
SUM_LAG = 2
BUFFERS = 4
BANKS = 3
CHUNK_OF = {"front": 1, "scan": 0, "back": -1, "tail": -2}


def make_plan():
    plan = [[] for _ in range(STEPS)]

    def put(slot, stage, *steps):
        plan[slot] += [(stage, name, i) for name, i in steps]

    for n in range(STATE):
        put((2 * n - 1) % STEPS, "scan" if n else "front", ("C", n))
    put(0, "tail", ("down", 0), ("down", 1))
    put(1, "tail", ("down", 2))
    put(2, "tail", ("down", 3))
    put(3, "tail", ("stats", 2))
    put(0, "front", ("squares", 0))
    put(0, "back", ("add_out_b", 0))
    put(1, "front", ("mean", 0))
    put(1, "back", ("gated", 0))
    put(2, "front", ("scaled", 0))
    put(2, "back", ("gated", 1))
    put(3, "back", ("mout", 0), ("k", 0))
    put(3, "front", ("xnT", 0))
    put(4, "tail", ("norm", 2))
    put(4, "back", ("stats", 0), ("v", 0))
    put(4, "front", ("xnT", 1))
    put(5, "back", ("norm", 0), ("v", 1))
    put(5, "front", ("hid", 0))
    put(6, "back", ("x1T", 0))
    put(6, "front", ("taps", 0), ("hid", 1))
    put(7, "back", ("q", 0), ("add_bo", 0))
    put(7, "front", ("taps", 1))
    first = 8
    for b in range(CHUNK_B):
        s = first + b
        put(s, "back", ("score", b))
    for s in range(first, first + CHUNK_B + 2):
        b = s - first
        early, late = [], []
        if 0 <= b - 1 < CHUNK_B:
            early.append(("exp", b - 1))
        if 0 <= b - 2:
            early.append(("widen", b - 2))
            late.append(("mix", b - 2))
        if 0 <= b - 1 < CHUNK_B:
            late += [("turn", b - 1), ("sum", b - 1)]
        plan[s] = [("back",) + e for e in early] + plan[s] + [("back",) + e for e in late]
    put(8, "front", ("taps", 2))
    put(9, "front", ("taps", 3))
    put(10, "front", ("tanh", 0))
    put(11, "front", ("silu", 0))
    put(12, "front", ("tanh", 1))
    put(13, "front", ("silu", 1))
    put(18, "back", ("aout", 0))
    put(18, "front", ("ts", 0))
    put(19, "back", ("stats", 1))
    put(19, "front", ("bc", 0), ("gate", 0))
    put(20, "back", ("norm", 1))
    put(20, "front", ("gate", 1), ("gated_h", 0))
    put(21, "back", ("x2T", 0), ("route", 0))
    put(21, "front", ("gated_h", 1))
    put(22, "back", ("up_g", 0), ("r_exp", 0), ("up_u", 0), ("r_rank", 0))
    put(23, "back", ("up_g", 1), ("up_u", 1), ("r_cw", 0))
    put(24, "back", ("up_g", 2), ("cwT", 0), ("up_u", 2))
    put(24, "front", ("dt", 0))
    put(25, "front", ("dt", 1))
    put(26, "front", ("soft", 0))
    put(28, "front", ("delta", 0))
    slots = [25, 25, 26, 27, 27, 28, 28, 29, 29, 30]
    for j, s in zip(range(3, FFN_TILES), slots):
        put(s, "back", ("up_g", j), ("cw", j - 3), ("up_u", j))
    put(30, "back", ("cw", 10))
    put(31, "back", ("cw", 11), ("cw", 12))
    return plan


PLAN = make_plan()
IN_RING = ("C", "down", "mout", "k", "xnT", "v", "hid", "x1T", "q", "score", "mix", "turn", "aout",
           "ts", "bc", "gate", "x2T", "route", "up_g", "up_u", "cwT", "cw", "dt")
RING = [step for slot in PLAN for step in slot if step[1] in IN_RING]
STAGE_OF = {step[1:]: step[0] for step in RING}
assert len(STAGE_OF) == len(RING)


class Signal:

    def __init__(self, sem, per_chunk, step=1):
        self.sem, self.per_chunk, self.step = sem, per_chunk, step

    def at(self, m, k=0):
        return (m * self.per_chunk + (k + 1)) * self.step


class Chunk:

    def __init__(self, m, parity, past):
        self.m, self.parity, self.past = m, parity, past


def ring_place(name, i, m):
    stage = STAGE_OF[name, i]
    at = RING.index((stage, name, i))
    bank = at % BANKS
    same = [j for j in range(bank, len(RING), BANKS)]
    if not isinstance(m, int):
        per_turn = len(same)
        ahead = sum(CHUNK_OF[RING[j][0]] - CHUNK_OF[stage] for j in same)
        return bank, m * per_turn + (ahead + sum(j < at for j in same))
    t = m - CHUNK_OF[stage]
    before = 0
    for j in same:
        chunk = t + CHUNK_OF[RING[j][0]]
        before += min(max(chunk, 0), CHUNKS) + (j < at and 0 <= chunk < CHUNKS)
    return bank, before


def build(nc, x, ctx_t, vec, rows, w_in, w_xproj, w_dt, w_out, w_attn, w_router, w_gate, w_up, w_down,
          c_masks, c_sel_bc, c_sel_cw, c_ident, c_tri, out):
    with ExitStack() as stack:
        def sb(name, shape, dt=F32):
            return stack.enter_context(nc.sbuf_tensor(name, shape, dt))

        def bank(name, dt=F32):
            return stack.enter_context(nc.psum_tensor(name, [128, 2048 // mybir.dt.size(dt)], dt))

        def signal(name, per_chunk=1, step=1):
            return Signal(stack.enter_context(nc.semaphore(name)), per_chunk, step)

        vecs = sb("vecs", [128, VEC])
        rowb = sb("rowb", [128, 3, D])
        win = sb("win", [128, 4, 128])
        wxp = sb("wxp", [128, HALVES, RANK + 3 * BC])
        wdt = sb("wdt", [RANK, INNER])
        wout = sb("wout", [128, HALVES, D])
        wattn = sb("wattn", [128, 4, 128])
        wrt = sb("wrt", [128, EXPERTS])
        wg = sb("wg", [128, FFN_TILES, 128])
        wu = sb("wu", [128, FFN_TILES, 128])
        wd = sb("wd", [128, FFN_TILES, 128])
        masks = sb("masks", [128, PAIRS + 2])
        sel_bc = sb("sel_bc", [3 * BC, BC], BF16)
        sel_cw = sb("sel_cw", [128, FFN_TILES, 128], BF16)
        ident = sb("ident", [128, 128])
        ident16 = sb("ident16", [128, 128], BF16)
        tri = sb("tri", [128, EXPERTS, EXPERTS])
        a_neg = sb("a_neg", [128, HALVES, STATE])
        halfv = sb("halfv", [128, 2 + HALVES * TAPS + HALVES])
        bqs = sb("bqs", [128, 2])
        mhalf = sb("mhalf", [128, GROUPS])
        xf = sb("xf", [128, GROUPS, D])
        ss = sb("ss", [128, GROUPS])
        ms = sb("ms", [128, GROUPS])
        rms = sb("rms", [128, GROUPS])
        xn = sb("xn", [128, GROUPS, D])
        xnT = sb("xnT", [128, T])
        hpad = sb("hpad", [128, HALVES, CHUNK_B, SEQ + TAPS - 1])
        zc = sb("zc", [128, HALVES, T])
        th = sb("th", [128, T])
        gh = sb("gh", [128, HALVES, T])
        gth = sb("gth", [128, T])
        h = sb("h", [128, 2, HALVES, T])
        gate = sb("gate", [128, 2, HALVES, T])
        delta = sb("delta", [128, 2, HALVES, T])
        u = sb("u", [128, 2, HALVES, T])
        bc16 = sb("bc16", [3 * BC, 2, T], BF16)
        bc_rest = sb("bc_rest", [3 * BC, T])
        ts_sb = sb("ts_sb", [RANK, T])
        sp_a = sb("sp_a", [128, HALVES, T])
        sq = sp_a[:, 0, :]
        c_rep = sb("c_rep", [128, 2, T])
        drive = sb("drive", [128, 2, T])
        state = sb("state", [128, BUFFERS, T])
        prod = sb("prod", [128, BUFFERS, T])
        yg = sb("yg", [128, HALVES, T])
        xb = sb("xb", [128, GROUPS, D])
        ctxT = sb("ctxT", [128, CHUNK_B, 2, SEQ])
        stats = sb("stats", [128, 3, GROUPS, 6])
        mv = sb("mv", [128, 3, GROUPS, 2])
        var = sb("var", [128, 3, GROUPS])
        rstd = sb("rstd", [128, 3, GROUPS])
        x1 = sb("x1", [128, GROUPS, D])
        x1b = sb("x1b", [128, GROUPS, D])
        x1T = sb("x1T", [128, T])
        qs = sb("qs", [128, CHUNK_B, 2, SEQ])
        kT = sb("kT", [128, T])
        km = sb("km", [128, CHUNK_B, PAIRS, SEQ])
        vm = sb("vm", [128, CHUNK_B, QUADS, 128])
        shifted = sb("shifted", [128, 2, PAIRS, SEQ])
        smax = sb("smax", [128, 2, PAIRS])
        ex = sb("ex", [128, 2, PAIRS, SEQ])
        den = sb("den", [128, 2, PAIRS])
        rden = sb("rden", [128, 2, PAIRS])
        exT = sb("exT", [128, QUADS, 128])
        rd_wide = sb("rd_wide", [128, 128])
        rdT = sb("rdT", [128, 128])
        aT = sb("aT", [128, T])
        x2 = sb("x2", [128, GROUPS, D])
        x2T = sb("x2T", [128, T])
        r_max = sb("r_max", [128, GROUPS])
        r_log = sb("r_log", [128, GROUPS, EXPERTS])
        r_exp = sb("r_exp", [128, GROUPS, EXPERTS])
        r_sum = sb("r_sum", [128, GROUPS])
        r_rec = sb("r_rec", [128, GROUPS])
        r_prob = sb("r_prob", [128, GROUPS, EXPERTS])
        r_rank = sb("r_rank", [128, GROUPS, EXPERTS])
        r_sel = sb("r_sel", [128, GROUPS, EXPERTS])
        r_cw = sb("r_cw", [128, GROUPS, EXPERTS])
        r_rest = sb("r_rest", [128, GROUPS, EXPERTS])
        cw16 = sb("cw16", [128, GROUPS, 128], BF16)
        cwT = sb("cwT", [128, T], BF16)
        gt = shifted[:].rearrange("p i a k -> p i (a k)")
        ga = kT[:]
        cwr = ex[:].rearrange("p i a k -> p i (a k)")
        pairwise = x1T[:].rearrange("p (w g a b) -> p w g a b", w=2, g=GROUPS, a=EXPERTS)
        r_gt, r_eq = pairwise[:, 0], pairwise[:, 1]
        acts_more = sb("acts_more", [128, FFN_TILES - CHUNK_B, T])
        acts = [km[:, j, :, :].rearrange("p a k -> p (a k)") if j < CHUNK_B else
                acts_more[:, j - CHUNK_B, :] for j in range(FFN_TILES)]
        sel_cw32 = acts_more[:].rearrange("p j t -> p (j t)")[:, 0:FFN_TILES * 128]
        sel_bc32 = zc[0:3 * BC, 0, 0:BC]

        p_decay = [bank(f"p_decay{j}") for j in range(HALVES)]
        p_b = bank("p_b")
        p_y = [bank(f"p_y{j}") for j in range(HALVES)]
        p_ring = [bank(f"p_ring{i}") for i in range(BANKS)]

        n_weights = 18
        weights_in = signal("weights_in")
        ready_const = signal("ready_const")
        consts_v = signal("consts_v")
        CONSTS = 7
        ring_full = [signal(f"ring_full{i}") for i in range(BANKS)]
        ring_free = [signal(f"ring_free{i}") for i in range(BANKS)]
        x_in, xb_in, out_done = (signal(n, 1, 16) for n in ("x_in", "xb_in", "out_done"))
        ctx_in = signal("ctx_in", 2, 16)
        squares_done, mean_sq, rms_ready, xn_ready = (
            signal(n) for n in ("squares_done", "mean_sq", "rms_ready", "xn_ready"))
        conv_th, gate_th, h_ready, gate_ready = (
            signal(n, HALVES) for n in ("conv_th", "gate_th", "h_ready", "gate_ready"))
        conv_tap = signal("conv_tap", HALVES * TAPS)
        bc_part = signal("bc_part", 4)
        spexp_ready, spln_ready, delta_ready, u_ready = (
            signal(n) for n in ("spexp_ready", "spln_ready", "delta_ready", "u_ready"))
        b_ready = signal("b_ready", STATE)
        decay_ready, drive_ready, state_ready, prod_ready, prod_used = (
            signal(n, STEPS) for n in ("decay_ready", "drive_ready", "state_ready", "prod_ready",
                                       "prod_used"))
        ysum_ready, yg_ready = signal("ysum_ready", 2), signal("yg_ready", 2)
        xb_ready, x1b_ready = signal("xb_ready"), signal("x1b_ready")
        ln_stats, ln_aggr, ln_var, ln_rstd, ln_ready = (
            [signal(f"{n}{ln}") for ln in range(3)]
            for n in ("ln_stats", "ln_aggr", "ln_var", "ln_rstd", "ln_ready"))
        km_ready = signal("km_ready")
        max_ready, exp_ready, den_ready, rden_ready, rdwide_ready, rdT_ready = (
            signal(n, CHUNK_B) for n in ("max_ready", "exp_ready", "den_ready", "rden_ready",
                                         "rdwide_ready", "rdT_ready"))
        route_v, route_exp, route_g = signal("route_v", 15), signal("route_exp"), signal("route_g", 2)
        gt_ready, act_ready = signal("gt_ready", FFN_TILES), signal("act_ready", FFN_TILES)

        def column(at):
            return vecs[:, at:at + 1]

        def filled(eng, name, i, m):
            r, before = ring_place(name, i, m)
            eng.wait_ge(ring_full[r].sem, before + 1)
            return p_ring[r]

        def emptied(eng, name, i, m):
            r, before = ring_place(name, i, m)
            eng.wait_ge(ring_free[r].sem, before + 1)

        def free(name, i):
            return ring_free[ring_place(name, i, 0)[0]].sem

        def by_group(a):
            return a.unsqueeze(2)

        def turns(eng, turn):
            def peeled(t):
                return {stage: Chunk(t + off, (t + off) % 2, t + off)
                        for stage, off in CHUNK_OF.items() if 0 <= t + off < CHUNKS}

            for t in (-1, 0, 1, 2):
                turn(peeled(t))
            with eng.Fori(3, 14, 2) as t0:
                for odd in range(2):
                    turn({stage: Chunk(t0 + (off + odd), (3 + odd + off) % 2, 3 + off)
                          for stage, off in CHUNK_OF.items()})
            for t in range(15, CHUNKS + 2):
                turn(peeled(t))

        block = stack.enter_context(nc.Block())

        @block.sync
        def _(sp):
            for to, src in ((vecs[:], vec), (win[:], w_in), (ident[:], c_ident), (wxp[:], w_xproj),
                            (wdt[:], w_dt), (sel_bc32, c_sel_bc), (wout[:], w_out), (wattn[:], w_attn),
                            (wrt[:], w_router), (masks[:], c_masks), (tri[:], c_tri),
                            (sel_cw32, c_sel_cw), (wg[:], w_gate),
                            (wu[:], w_up), (wd[:], w_down),
                            (rowb[:, 0, :], rows[0].partition_broadcast(128)),
                            (rowb[:, 1, :], rows[1].partition_broadcast(128)),
                            (rowb[:, 2, :], rows[2].partition_broadcast(128))):
                sp.dma_start(to, src).then_inc(weights_in.sem, 16)

            def turn(chunks):
                front, scan, tail = (chunks.get(n) for n in ("front", "scan", "tail"))
                if front:
                    if front.past >= 1:
                        sp.wait_ge(xn_ready.sem, xn_ready.at(front.m - 1))
                    sp.dma_start(xf[:], x[bass.ds(front.m * T, T), :].rearrange("(g p) d -> p g d", p=128)
                                 ).then_inc(x_in.sem, 16)
                if tail:
                    sp.wait_ge(ln_ready[2].sem, ln_ready[2].at(tail.m))
                    sp.dma_start(out[bass.ds(tail.m * T, T), :].rearrange("(g p) d -> p g d", p=128),
                                 x2[:]).then_inc(out_done.sem, 16)
                if scan:
                    if scan.past >= 1:
                        emptied(sp, "v", 1, scan.m - 1)
                    sp.dma_start(xb[:], x[bass.ds(scan.m * T, T), :].rearrange("(g p) d -> p g d", p=128)
                                 ).then_inc(xb_in.sem, 16)
                    for twice in range(2):
                        sp.dma_start(ctxT[:, :, twice, :], ctx_t[:, bass.ds(scan.m * T, T)].rearrange(
                            "d (b t) -> d b t", t=SEQ)).then_inc(ctx_in.sem, 16)

            turns(sp, turn)
            sp.wait_ge(out_done.sem, out_done.at(CHUNKS - 1))

        @block.tensor
        def _(pe):
            pe.wait_ge(weights_in.sem, 16 * n_weights)
            pe.wait_ge(consts_v.sem, CONSTS)

            def step(name, i, c):
                if name not in IN_RING:
                    return
                r, before = ring_place(name, i, c.m)
                if not isinstance(before, int) or before > 0:
                    pe.wait_ge(ring_free[r].sem, before)
                p = p_ring[r]
                if name == "C":
                    if i == 0:
                        pe.wait_ge(bc_part.sem, bc_part.at(c.m, 3))
                    mm = pe.matmul(p[:], sel_bc[:, STATE + i:STATE + i + 1].to_broadcast([3 * BC, 128]),
                                   bc16[:, c.parity, :], start=True, stop=True)
                elif name == "xnT":
                    pe.wait_ge(xn_ready.sem, xn_ready.at(c.m))
                    for g in range(2):
                        mm = pe.transpose(p[:, g * 128:(g + 1) * 128], xn[:, 2 * i + g, :], ident[:])
                elif name in ("hid", "gate"):
                    emptied(pe, "xnT", 1, c.m)
                    mm = pe.matmul(p[:], win[:, i + 2 * (name == "gate"), :], xnT[:], start=True, stop=True)
                elif name == "ts":
                    pe.wait_ge(h_ready.sem, h_ready.at(c.m, 1))
                    for j in range(HALVES):
                        mm = pe.matmul(p[0:RANK, :], wxp[:, j, 0:RANK], h[:, c.parity, j, :],
                                       start=j == 0, stop=j == HALVES - 1)
                elif name == "bc":
                    for j in range(HALVES):
                        mm = pe.matmul(p[0:3 * BC, :], wxp[:, j, RANK:RANK + 3 * BC], h[:, c.parity, j, :],
                                       start=j == 0, stop=j == HALVES - 1)
                elif name == "dt":
                    emptied(pe, "ts", 0, c.m)
                    mm = pe.matmul(p[:], wdt[:, i * 128:(i + 1) * 128], ts_sb[:], start=True, stop=True)
                elif name == "mout":
                    pe.wait_ge(yg_ready.sem, yg_ready.at(c.m, 1))
                    for g in range(GROUPS):
                        for j in range(HALVES):
                            mm = pe.matmul(p[:, g * D:(g + 1) * D], yg[:, j, g * 128:(g + 1) * 128],
                                           wout[:, j, :], start=j == 0, stop=j == HALVES - 1)
                elif name in ("x1T", "x2T"):
                    src, ln = (x1, 0) if name == "x1T" else (x2, 1)
                    pe.wait_ge(ln_ready[ln].sem, ln_ready[ln].at(c.m))
                    for g in range(GROUPS):
                        mm = pe.transpose(p[:, g * 128:(g + 1) * 128], src[:, g, :], ident[:])
                elif name == "q":
                    emptied(pe, "x1T", 0, c.m)
                    mm = pe.matmul(p[:], wattn[:, 0, :], x1T[:], start=True, stop=True)
                elif name == "k":
                    pe.wait_ge(ctx_in.sem, ctx_in.at(c.m, 1))
                    mm = pe.matmul(p[:], wattn[:, 1, :], ctxT[:, :, 0, :], start=True, stop=True)
                elif name == "v":
                    for b in range(4):
                        twice = ctxT[:, 4 * i + b, :, :].rearrange("d a t -> d (a t)")
                        mm = pe.matmul(p[:, b * 128:(b + 1) * 128], twice, wattn[:, 2, :],
                                       start=True, stop=True)
                elif name == "score":
                    if i == 0:
                        emptied(pe, "q", 0, c.m)
                        pe.wait_ge(km_ready.sem, km_ready.at(c.m))
                    mm = pe.matmul(p[:], qs[:, i, :, :].rearrange("p s q -> p (s q)"),
                                   km[:, i, :, :].rearrange("p a k -> p (a k)"), start=True, stop=True)
                elif name == "turn":
                    pe.wait_ge(exp_ready.sem, exp_ready.at(c.m, i))
                    for q in range(QUADS):
                        mm = pe.transpose(p[:, q * 128:(q + 1) * 128],
                                          ex[:, i % 2, 2 * q:2 * q + 2, :].rearrange("p a k -> p (a k)"),
                                          ident[:])
                elif name == "mix":
                    emptied(pe, "turn", i, c.m)
                    if i == 0:
                        emptied(pe, "v", 1, c.m)
                    for q in range(QUADS):
                        pe.matmul(p[:, 0:128], vm[:, i, q, :], exT[:, q, :],
                                  start=q == 0, stop=q == QUADS - 1)
                    pe.wait_ge(rdwide_ready.sem, rdwide_ready.at(c.m, i))
                    mm = pe.transpose(p[:, 128:256], rd_wide[:], ident[:])
                elif name == "aout":
                    emptied(pe, "mix", CHUNK_B - 1, c.m)
                    for g in range(GROUPS):
                        mm = pe.matmul(p[:, g * D:(g + 1) * D], aT[:, g * 128:(g + 1) * 128],
                                       wattn[:, 3, :], start=True, stop=True)
                elif name == "route":
                    emptied(pe, "x2T", 0, c.m)
                    for g in range(GROUPS):
                        mm = pe.matmul(p[:, g * EXPERTS:(g + 1) * EXPERTS], x2T[:, g * 128:(g + 1) * 128],
                                       wrt[:], start=True, stop=True)
                elif name in ("up_g", "up_u"):
                    mm = pe.matmul(p[:], (wg if name == "up_g" else wu)[:, i, :], x2T[:],
                                   start=True, stop=True)
                elif name == "cwT":
                    pe.wait_ge(route_v.sem, route_v.at(c.m, 14))
                    p16 = p[:].bitcast(BF16)
                    for g in range(GROUPS):
                        mm = pe.transpose(p16[:, g * 128:(g + 1) * 128], cw16[:, g, :], ident16[:])
                elif name == "cw":
                    if i == 0:
                        emptied(pe, "cwT", 0, c.m)
                    mm = pe.matmul(p[:], sel_cw[:, i, :], cwT[:], start=True, stop=True)
                else:
                    for j in range(FFN_TILES):
                        if i == 0 and j in (0, FFN_TILES - 2, FFN_TILES - 1):
                            pe.wait_ge(act_ready.sem, act_ready.at(c.m, max(j, FFN_TILES - 3)))
                        mm = pe.matmul(p[:, 0:D], acts[j][:, i * 128:(i + 1) * 128],
                                       wd[:, j, :], start=j == 0, stop=j == FFN_TILES - 1)
                mm.then_inc(ring_full[r].sem, 1)

            def spread_b(c, n):
                if n == 0:
                    pe.wait_ge(bc_part.sem, bc_part.at(c.m, 3))
                if n > 0 or c.past >= 1:
                    pe.wait_ge(drive_ready.sem, drive_ready.at(c.m, HALVES * n - 1))
                pe.matmul(p_b[:], sel_bc[:, n:n + 1].to_broadcast([3 * BC, 128]), bc16[:, c.parity, :],
                          start=True, stop=True).then_inc(b_ready.sem, 1)

            def sum_n(c, k):
                n, j = divmod(k, HALVES)
                if n == 0 and c.past >= 1:
                    pe.wait_ge(ysum_ready.sem, ysum_ready.at(c.m - 1, j))
                pe.wait_ge(prod_ready.sem, prod_ready.at(c.m, k))
                pe.matmul(p_y[j][:], ident[:], prod[:, k % BUFFERS, :],
                          start=n == 0, stop=n == STATE - 1).then_inc(prod_used.sem, 1)

            def turn(chunks):
                for s in range(STEPS):
                    if s % 2 == 1:
                        n = (s + 1) // 2 % STATE
                        if ("scan" if n else "front") in chunks:
                            spread_b(chunks["scan" if n else "front"], n)
                    own = [e for e in PLAN[s] if e[0] in chunks]
                    for e in own[:1]:
                        step(e[1], e[2], chunks[e[0]])
                    k = (s - SUM_LAG) % STEPS
                    if ("scan" if s >= SUM_LAG else "back") in chunks:
                        sum_n(chunks["scan" if s >= SUM_LAG else "back"], k)
                    for e in own[1:]:
                        step(e[1], e[2], chunks[e[0]])

            turns(pe, turn)

        @block.scalar
        def _(act):
            act.wait_ge(weights_in.sem, 16 * n_weights)
            act.activation(a_neg[:].rearrange("p a n -> p (a n)"), vecs[:, V_ALOG:V_ALOG + HALVES * STATE],
                           ACT.Exp).then_inc(ready_const.sem, 1)
            act.wait_ge(consts_v.sem, CONSTS)

            def step(name, i, c):
                par = c.parity
                if name == "squares":
                    act.wait_ge(x_in.sem, x_in.at(c.m))
                    if c.past >= 1:
                        act.wait_ge(mean_sq.sem, mean_sq.at(c.m - 1))
                        act.wait_ge(delta_ready.sem, delta_ready.at(c.m - 1))
                    for g in range(GROUPS):
                        a = act.activation(sq[:, g * D:(g + 1) * D], xf[:, g, :], ACT.Square,
                                           accum_out=ss[:, g:g + 1])
                    a.then_inc(squares_done.sem, 1)
                elif name == "C":
                    p = filled(act, name, i, c.m)
                    if i > 1:
                        act.wait_ge(prod_ready.sem, prod_ready.at(c.m, HALVES * (i - 1) - 1))
                    elif c.past >= 1:
                        act.wait_ge(prod_ready.sem, prod_ready.at(c.m - 1, STEPS + HALVES * (i - 1) - 1))
                    act.activation(c_rep[:, i % 2, :], p[:], ACT.Copy).then_inc(free(name, i), 1)
                elif name == "xnT":
                    p = filled(act, name, i, c.m)
                    act.activation(xnT[:, i * 256:(i + 1) * 256], p[:, 0:256], ACT.Copy,
                                   scale=column(V_NORM)).then_inc(free(name, i), 1)
                elif name == "hid":
                    p = filled(act, name, i, c.m)
                    if c.past >= 1:
                        act.wait_ge(conv_tap.sem, conv_tap.at(c.m - 1, i * TAPS + TAPS - 1))
                    act.activation(hpad[:, i, :, TAPS - 1:], p[:].rearrange("p (b t) -> p b t", t=SEQ),
                                   ACT.Identity, bias=column(V_INB + i)).then_inc(free(name, i), 1)
                elif name == "tanh":
                    act.wait_ge(conv_tap.sem, conv_tap.at(c.m, i * TAPS + TAPS - 1))
                    if i == 1:
                        act.wait_ge(h_ready.sem, h_ready.at(c.m, 0))
                    act.activation(th[:], zc[:, i, :], ACT.Tanh).then_inc(conv_th.sem, 1)
                elif name == "gate":
                    p = filled(act, name, i, c.m)
                    act.activation(gh[:, i, :], p[:], ACT.Identity, scale=0.5,
                                   bias=halfv[:, i:i + 1]).then_inc(free(name, i), 1)
                    if i > 0 or c.past >= 1:
                        act.wait_ge(gate_ready.sem, gate_ready.at(c.m, i - 1))
                    emptied(act, name, i, c.m)
                    act.activation(gth[:], gh[:, i, :], ACT.Tanh).then_inc(gate_th.sem, 1)
                elif name == "ts":
                    p = filled(act, name, i, c.m)
                    act.activation(ts_sb[:], p[0:RANK, :], ACT.Copy).then_inc(free(name, i), 1)
                elif name == "dt":
                    p = filled(act, name, i, c.m)
                    act.activation(delta[:, par, i, :], p[:], ACT.Relu, bias=column(V_DTB + i))
                    act.activation(sp_a[:, i, :], p[:], ACT.Abs,
                                   bias=column(V_DTB + i)).then_inc(free(name, i), 1)
                elif name == "soft":
                    both = sp_a[:].rearrange("p j t -> p (j t)")
                    emptied(act, "dt", 1, c.m)
                    act.activation(both, both, ACT.Exp, scale=-1.0).then_inc(spexp_ready.sem, 1)
                    act.wait_ge(spexp_ready.sem, spexp_ready.at(c.m))
                    act.activation(both, both, ACT.Ln, bias=1.0).then_inc(spln_ready.sem, 1)
                elif name == "k":
                    p = filled(act, name, i, c.m)
                    if c.past >= 1:
                        emptied(act, "up_u", FFN_TILES - 1, c.m - 1)
                    act.activation(kT[:], p[:], ACT.Identity, bias=column(V_BK)).then_inc(free(name, i), 1)
                elif name == "x1T":
                    p = filled(act, name, i, c.m)
                    act.activation(x1T[:], p[:], ACT.Copy).then_inc(free(name, i), 1)
                elif name == "q":
                    p = filled(act, name, i, c.m)
                    for s in range(2):
                        a = act.activation(qs[:, :, s, :], p[:].rearrange("p (b t) -> p b t", t=SEQ),
                                           ACT.Identity, scale=masks[:, PAIRS + s:PAIRS + s + 1],
                                           bias=bqs[:, s:s + 1])
                    a.then_inc(free(name, i), 1)
                elif name == "exp":
                    emptied(act, "score", i, c.m)
                    act.activation(ex[:, i % 2, :, :].rearrange("p a k -> p (a k)"),
                                   shifted[:, i % 2, :, :].rearrange("p a k -> p (a k)"),
                                   ACT.Exp).then_inc(exp_ready.sem, 1)
                elif name == "widen":
                    act.wait_ge(rden_ready.sem, rden_ready.at(c.m, i))
                    act.activation(rd_wide[:].rearrange("p (s a d) -> p s a d", s=2, d=HEAD_D),
                                   rden[:, i % 2, :].unsqueeze(1).unsqueeze(3).to_broadcast(
                                       [128, 2, PAIRS, HEAD_D]), ACT.Copy).then_inc(rdwide_ready.sem, 1)
                elif name == "turn":
                    p = filled(act, name, i, c.m)
                    act.activation(exT[:].rearrange("p a q -> p (a q)"), p[:],
                                   ACT.Copy).then_inc(free(name, i), 1)
                elif name == "mix":
                    p = filled(act, name, i, c.m)
                    if i > 0:
                        emptied(act, "mix", i - 1, c.m)
                    elif c.past >= 1:
                        emptied(act, "mix", CHUNK_B - 1, c.m - 1)
                    act.activation(rdT[:], p[:, 128:256], ACT.Copy).then_inc(rdT_ready.sem, 1)
                elif name == "x2T":
                    p = filled(act, name, i, c.m)
                    act.activation(x2T[:], p[:], ACT.Copy).then_inc(free(name, i), 1)
                elif name == "r_exp":
                    emptied(act, "route", 0, c.m)
                    act.activation(r_exp[:].rearrange("p g e -> p (g e)"),
                                   r_log[:].rearrange("p g e -> p (g e)"),
                                   ACT.Exp).then_inc(route_exp.sem, 1)
                elif name == "up_g":
                    p = filled(act, name, i, c.m)
                    if i >= 2:
                        emptied(act, "up_g", i - 2, c.m)
                    act.activation(gt[:, i % 2, :], p[:], ACT.Tanh, scale=0.5).then_inc(gt_ready.sem, 1)
                elif name == "cwT":
                    p = filled(act, name, i, c.m)
                    act.activation(cwT[:], p[:].bitcast(BF16)[:, 0:T], ACT.Copy).then_inc(free(name, i), 1)
                elif name == "cw":
                    p = filled(act, name, i, c.m)
                    if i > 1:
                        act.wait_ge(act_ready.sem, act_ready.at(c.m, i - 2))
                    act.activation(cwr[:, i % 2, :], p[:], ACT.Copy).then_inc(free(name, i), 1)

            def decays(c, k):
                n, j = divmod(k, HALVES)
                if k == 0:
                    act.wait_ge(delta_ready.sem, delta_ready.at(c.m))
                if n > 0 or c.past >= 1:
                    act.wait_ge(state_ready.sem, state_ready.at(c.m, k - HALVES))
                act.activation(p_decay[j][:].rearrange("p (b t) -> p b t", t=SEQ)[:, :, 1:],
                               delta[:, c.parity, j, :].rearrange("p (b t) -> p b t", t=SEQ)[:, :, 1:],
                               ACT.Exp, scale=a_neg[:, j, n:n + 1]).then_inc(decay_ready.sem, 1)

            def turn(chunks):
                for s in range(STEPS):
                    k = (s + 1) % STEPS
                    if ("scan" if k else "front") in chunks:
                        decays(chunks["scan" if k else "front"], k)
                    for stage, name, i in PLAN[s]:
                        if stage in chunks:
                            step(name, i, chunks[stage])

            turns(act, turn)

        @block.vector
        def _(dve):
            for j in range(HALVES):
                dve.memset(p_decay[j][:], 0.0)
            dve.memset(hpad[:], 0.0)
            dve.memset(vm[:], 0.0)
            dve.memset(mhalf[:], -0.5)
            dve.memset(cw16[:], 0.0).then_inc(consts_v.sem, 1)
            dve.wait_ge(consts_v.sem, 1)
            dve.memset(cw16[:, :, 3 * EXPERTS:3 * EXPERTS + 1], 1.0).then_inc(consts_v.sem, 1)
            dve.wait_ge(weights_in.sem, 16 * n_weights)
            dve.tensor_scalar(halfv[:, 0:2], vecs[:, V_INB + 2:V_INB + 4], 0.5, None,
                              ALU.mult).then_inc(consts_v.sem, 1)
            dve.tensor_scalar(halfv[:, 2:], vecs[:, V_CONVW:V_CONVW + HALVES * TAPS + HALVES], 0.5, None,
                              ALU.mult).then_inc(consts_v.sem, 1)
            dve.tensor_scalar(bqs[:], masks[:, PAIRS:PAIRS + 2], column(V_BQ), None,
                              ALU.mult).then_inc(consts_v.sem, 1)
            dve.tensor_copy(ident16[:], ident[:])
            dve.tensor_copy(sel_bc[:], sel_bc32)
            dve.tensor_copy(sel_cw[:].rearrange("p j c -> p (j c)"), sel_cw32).then_inc(consts_v.sem, 1)
            dve.wait_ge(ready_const.sem, 1)
            dve.tensor_scalar(a_neg[:].rearrange("p a n -> p (a n)"), a_neg[:].rearrange("p a n -> p (a n)"),
                              -1.0, None, ALU.mult).then_inc(consts_v.sem, 1)
            dve.wait_ge(consts_v.sem, CONSTS)

            def ln_statistics(c, ln, src):
                for g in range(GROUPS):
                    d = dve.bn_stats(stats[:, ln, g, :], src[:, g, :])
                d.then_inc(ln_stats[ln].sem, 1)
                dve.wait_ge(consts_v.sem, CONSTS)
                dve.wait_ge(ln_stats[ln].sem, ln_stats[ln].at(c.m))
                for g in range(GROUPS):
                    d = dve.bn_aggr(mv[:, ln, g, :], stats[:, ln, g, :])
                d.then_inc(ln_aggr[ln].sem, 1)
                dve.wait_ge(ln_aggr[ln].sem, ln_aggr[ln].at(c.m))
                dve.tensor_scalar(var[:, ln, :], mv[:, ln, :, 1], LN_EPS, None, ALU.add
                                  ).then_inc(ln_var[ln].sem, 1)

            def ln_normalise(c, ln, src, to):
                dve.wait_ge(ln_rstd[ln].sem, ln_rstd[ln].at(c.m))
                for g in range(GROUPS):
                    d = dve.tensor_scalar(to[:, g, :], src[:, g, :], mv[:, ln, g, 0:1],
                                          rstd[:, ln, g:g + 1], ALU.subtract, ALU.mult)
                d.then_inc(ln_ready[ln].sem, 1)

            wide = [128, GROUPS, EXPERTS]
            LN_IN, LN_OUT = (xb, x1b, x2), (x1, x2, x2)

            def step(name, i, c):
                par = c.parity
                if name == "mean":
                    dve.wait_ge(squares_done.sem, squares_done.at(c.m))
                    if c.past >= 1:
                        dve.wait_ge(rms_ready.sem, rms_ready.at(c.m - 1))
                    dve.tensor_scalar(ms[:], ss[:], 1.0 / D, RMS_EPS, ALU.mult, ALU.add
                                      ).then_inc(mean_sq.sem, 1)
                elif name == "scaled":
                    dve.wait_ge(rms_ready.sem, rms_ready.at(c.m))
                    if c.past >= 1:
                        emptied(dve, "xnT", 1, c.m - 1)
                    dve.tensor_tensor(xn[:], xf[:], by_group(rms[:]).to_broadcast([128, GROUPS, D]),
                                      ALU.mult).then_inc(xn_ready.sem, 1)
                elif name == "taps":
                    j, pair = divmod(i, 2)
                    z = zc[:, j, :].rearrange("p (b t) -> p b t", t=SEQ)
                    for k in range(2 * pair, 2 * pair + 2):
                        w = halfv[:, 2 + j * TAPS + k:3 + j * TAPS + k]
                        if k == 0:
                            emptied(dve, "hid", j, c.m)
                            if c.past >= 1:
                                dve.wait_ge(h_ready.sem, h_ready.at(c.m - 1, j))
                            b = halfv[:, 2 + HALVES * TAPS + j:3 + HALVES * TAPS + j]
                            dve.tensor_scalar(z, hpad[:, j, :, 0:SEQ], w, b, ALU.mult,
                                              ALU.add).then_inc(conv_tap.sem, 1)
                        else:
                            dve.wait_ge(conv_tap.sem, conv_tap.at(c.m, j * TAPS + k - 1))
                            dve.scalar_tensor_tensor(z, hpad[:, j, :, k:k + SEQ], w, z, ALU.mult,
                                                     ALU.add).then_inc(conv_tap.sem, 1)
                elif name == "silu":
                    dve.wait_ge(conv_th.sem, conv_th.at(c.m, i))
                    dve.scalar_tensor_tensor(h[:, par, i, :], th[:], 1.0, zc[:, i, :], ALU.add,
                                             ALU.mult).then_inc(h_ready.sem, 1)
                elif name == "gated_h":
                    dve.wait_ge(gate_th.sem, gate_th.at(c.m, i))
                    dve.scalar_tensor_tensor(gate[:, par, i, :], gth[:], 1.0, gh[:, i, :], ALU.add,
                                             ALU.mult).then_inc(gate_ready.sem, 1)
                elif name == "bc":
                    p = filled(dve, name, i, c.m)
                    s16 = bc16[:, par, :]
                    dve.tensor_copy(s16, p[0:3 * BC, :]).then_inc(bc_part.sem, 1)
                    dve.wait_ge(bc_part.sem, bc_part.at(c.m, 0))
                    for q in (1, 2):
                        r = slice(q * BC, (q + 1) * BC)
                        d = dve.tensor_tensor(bc_rest[r, :], p[r, :], s16[r, :], ALU.subtract)
                    d.then_inc(free(name, i), 1)
                    emptied(dve, name, i, c.m)
                    for q in (1, 2):
                        r = slice(q * BC, (q + 1) * BC)
                        d = dve.tensor_copy(s16[r, :], bc_rest[r, :])
                    d.then_inc(bc_part.sem, 1)
                    dve.wait_ge(bc_part.sem, bc_part.at(c.m, 1))
                    r = slice(2 * BC, 3 * BC)
                    dve.tensor_tensor(bc_rest[r, :], bc_rest[r, :], s16[r, :],
                                      ALU.subtract).then_inc(bc_part.sem, 1)
                    dve.wait_ge(bc_part.sem, bc_part.at(c.m, 2))
                    dve.tensor_copy(s16[r, :], bc_rest[r, :]).then_inc(bc_part.sem, 1)
                elif name == "delta":
                    dve.wait_ge(spln_ready.sem, spln_ready.at(c.m))
                    dve.tensor_tensor(delta[:, par, :, :], delta[:, par, :, :], sp_a[:], ALU.add
                                      ).then_inc(delta_ready.sem, 1)
                    dve.wait_ge(delta_ready.sem, delta_ready.at(c.m))
                    dve.tensor_tensor(u[:, par, :, :], delta[:, par, :, :], h[:, par, :, :], ALU.mult
                                      ).then_inc(u_ready.sem, 1)
                elif name == "gated":
                    dve.wait_ge(prod_used.sem, prod_used.at(c.m, STEPS - HALVES + i))
                    if c.past >= 1 and i == 0:
                        emptied(dve, "mout", 0, c.m - 1)
                    dve.scalar_tensor_tensor(yg[:, i, :], h[:, par, i, :], column(V_D + i), p_y[i][:],
                                             ALU.mult, ALU.add).then_inc(ysum_ready.sem, 1)
                    dve.wait_ge(ysum_ready.sem, ysum_ready.at(c.m, i))
                    dve.tensor_tensor(yg[:, i, :], yg[:, i, :], gate[:, par, i, :], ALU.mult
                                      ).then_inc(yg_ready.sem, 1)
                elif name == "down":
                    p = filled(dve, name, i, c.m)
                    dve.tensor_tensor(x2[:, i, :], p[:, 0:D], x2[:, i, :], ALU.add).then_inc(free(name, i), 1)
                elif name == "mout":
                    p = filled(dve, name, i, c.m)
                    dve.wait_ge(xb_ready.sem, xb_ready.at(c.m))
                    dve.tensor_tensor(xb[:].rearrange("p g d -> p (g d)"), p[:],
                                      xb[:].rearrange("p g d -> p (g d)"), ALU.add).then_inc(free(name, i), 1)
                elif name == "aout":
                    p = filled(dve, name, i, c.m)
                    dve.wait_ge(x1b_ready.sem, x1b_ready.at(c.m))
                    dve.tensor_tensor(x1b[:].rearrange("p g d -> p (g d)"), p[:],
                                      x1b[:].rearrange("p g d -> p (g d)"), ALU.add).then_inc(free(name, i), 1)
                elif name == "stats":
                    emptied(dve, *(("mout", 0), ("aout", 0), ("down", GROUPS - 1))[i], c.m)
                    ln_statistics(c, i, LN_IN[i])
                elif name == "norm":
                    if i == 1 and c.past >= 1:
                        dve.wait_ge(out_done.sem, out_done.at(c.m - 1))
                    ln_normalise(c, i, LN_IN[i], LN_OUT[i])
                elif name == "v":
                    p = filled(dve, name, i, c.m)
                    for half in range(2):
                        r = slice(64 * half, 64 * half + 64)
                        for s in range(2):
                            src = p[r, :].rearrange("p (b s q a d) -> p b s q a d", b=4, s=2, q=QUADS, a=2)[
                                :, :, s, :, half, :]
                            bias = rowb[r, 1, :].rearrange("p (s q a d) -> p s q a d", s=2, q=QUADS, a=2)[
                                :, s, :, half, :].unsqueeze(1).to_broadcast([64, 4, QUADS, HEAD_D])
                            base = vm[r, 4 * i:4 * i + 4, :, :]
                            part = list(base.ap[:1]) + [(QUADS * 128, 4), (128 + 2 * HEAD_D, QUADS), (1, HEAD_D)]
                            to = bass.AP(base.tensor, base.offset + 64 * s + HEAD_D * half, part)
                            d = dve.tensor_tensor(to, src, bias, ALU.add)
                    d.then_inc(free(name, i), 1)
                elif name == "score":
                    p = filled(dve, name, i, c.m)
                    s3 = p[:].rearrange("p (a k) -> p a k", k=SEQ)
                    dve.tensor_reduce(smax[:, i % 2, :], s3, AX_X, ALU.max).then_inc(max_ready.sem, 1)
                    dve.wait_ge(max_ready.sem, max_ready.at(c.m, i))
                    dve.tensor_tensor(shifted[:, i % 2, :, :], s3,
                                      by_group(smax[:, i % 2, :]).to_broadcast([128, PAIRS, SEQ]), ALU.subtract
                                      ).then_inc(free(name, i), 1)
                elif name == "sum":
                    dve.wait_ge(exp_ready.sem, exp_ready.at(c.m, i))
                    dve.tensor_reduce(den[:, i % 2, :], ex[:, i % 2, :, :], AX_X, ALU.add).then_inc(den_ready.sem, 1)
                    dve.wait_ge(den_ready.sem, den_ready.at(c.m, i))
                    dve.reciprocal(rden[:, i % 2, :], den[:, i % 2, :]).then_inc(rden_ready.sem, 1)
                elif name == "mix":
                    p = filled(dve, name, i, c.m)
                    dve.wait_ge(rdT_ready.sem, rdT_ready.at(c.m, i))
                    for s in range(2):
                        r = slice(64 * s, 64 * s + 64)
                        d = dve.tensor_tensor(aT[r, i * SEQ:(i + 1) * SEQ], p[r, 64 * s:64 * s + 64],
                                              rdT[r, 64 * s:64 * s + 64], ALU.mult)
                    d.then_inc(free(name, i), 1)
                elif name == "route":
                    p = filled(dve, name, i, c.m)
                    logits = p[:, 0:GROUPS * EXPERTS].rearrange("p (g e) -> p g e", e=EXPERTS)
                    dve.tensor_reduce(r_max[:], logits, AX_X, ALU.max).then_inc(route_v.sem, 1)
                    dve.wait_ge(route_v.sem, route_v.at(c.m, 0))
                    dve.tensor_tensor(r_log[:], logits, by_group(r_max[:]).to_broadcast(wide), ALU.subtract
                                      ).then_inc(free(name, i), 1)
                elif name == "r_rank":
                    dve.wait_ge(route_exp.sem, route_exp.at(c.m))
                    dve.tensor_reduce(r_sum[:], r_exp[:], AX_X, ALU.add).then_inc(route_v.sem, 1)
                    dve.wait_ge(route_v.sem, route_v.at(c.m, 1))
                    dve.reciprocal(r_rec[:], r_sum[:]).then_inc(route_v.sem, 1)
                    dve.wait_ge(route_v.sem, route_v.at(c.m, 2))
                    dve.tensor_tensor(r_prob[:], r_exp[:], by_group(r_rec[:]).to_broadcast(wide), ALU.mult
                                      ).then_inc(route_v.sem, 1)
                    dve.wait_ge(route_v.sem, route_v.at(c.m, 3))
                    mine = r_prob[:].unsqueeze(3).to_broadcast([128, GROUPS, EXPERTS, EXPERTS])
                    other = r_prob[:].unsqueeze(2).to_broadcast([128, GROUPS, EXPERTS, EXPERTS])
                    dve.tensor_tensor(r_eq, other, mine, ALU.is_equal)
                    dve.tensor_tensor(r_gt, other, mine, ALU.is_gt).then_inc(route_v.sem, 1)
                elif name == "r_cw":
                    dve.wait_ge(route_g.sem, route_g.at(c.m, 1))
                    dve.tensor_reduce(r_rank[:], r_gt, AX_X, ALU.add).then_inc(route_v.sem, 1)
                    dve.wait_ge(route_v.sem, route_v.at(c.m, 5))
                    dve.scalar_tensor_tensor(r_sel[:], r_rank[:], float(TOP), r_prob[:], ALU.is_lt, ALU.mult
                                             ).then_inc(route_v.sem, 1)
                    dve.wait_ge(route_v.sem, route_v.at(c.m, 6))
                    dve.tensor_reduce(r_sum[:], r_sel[:], AX_X, ALU.add).then_inc(route_v.sem, 1)
                    dve.wait_ge(route_v.sem, route_v.at(c.m, 7))
                    dve.tensor_scalar(r_max[:], r_sum[:], TOP_EPS, None, ALU.add).then_inc(route_v.sem, 1)
                    dve.wait_ge(route_v.sem, route_v.at(c.m, 8))
                    dve.reciprocal(r_rec[:], r_max[:]).then_inc(route_v.sem, 1)
                    dve.wait_ge(route_v.sem, route_v.at(c.m, 9))
                    dve.tensor_tensor(r_cw[:], r_sel[:], by_group(r_rec[:]).to_broadcast(wide), ALU.mult
                                      ).then_inc(route_v.sem, 1)
                    dve.wait_ge(route_v.sem, route_v.at(c.m, 10))
                    E = EXPERTS
                    dve.tensor_copy(cw16[:, :, 0:E], r_cw[:]).then_inc(route_v.sem, 1)
                    dve.wait_ge(route_v.sem, route_v.at(c.m, 11))
                    dve.tensor_tensor(r_rest[:], r_cw[:], cw16[:, :, 0:E], ALU.subtract
                                      ).then_inc(route_v.sem, 1)
                    dve.wait_ge(route_v.sem, route_v.at(c.m, 12))
                    dve.tensor_copy(cw16[:, :, E:2 * E], r_rest[:]).then_inc(route_v.sem, 1)
                    dve.wait_ge(route_v.sem, route_v.at(c.m, 13))
                    dve.tensor_tensor(cw16[:, :, 2 * E:3 * E], r_rest[:], cw16[:, :, E:2 * E], ALU.subtract
                                      ).then_inc(route_v.sem, 1)
                elif name == "up_g":
                    p = filled(dve, name, i, c.m)
                    dve.wait_ge(gt_ready.sem, gt_ready.at(c.m, i))
                    if i > 0:
                        emptied(dve, "up_u", i - 1, c.m)
                    dve.scalar_tensor_tensor(ga, gt[:, i % 2, :], 1.0, p[:], ALU.add, ALU.mult
                                             ).then_inc(free(name, i), 1)
                elif name == "up_u":
                    p = filled(dve, name, i, c.m)
                    emptied(dve, "up_g", i, c.m)
                    dve.tensor_tensor(acts[i], ga, p[:], ALU.mult).then_inc(free(name, i), 1)

            def drives(c, n):
                if n == 0:
                    dve.wait_ge(u_ready.sem, u_ready.at(c.m))
                dve.wait_ge(b_ready.sem, b_ready.at(c.m, n))
                for j in range(HALVES):
                    if n > 0 or c.past >= 1:
                        dve.wait_ge(state_ready.sem, state_ready.at(c.m, HALVES * (n - 1) + j))
                    dve.tensor_tensor(drive[:, j, :], u[:, c.parity, j, :], p_b[:], ALU.mult
                                      ).then_inc(drive_ready.sem, 1)

            def scans(c, k):
                n, j = divmod(k, HALVES)
                dve.wait_ge(decay_ready.sem, decay_ready.at(c.m, k))
                dve.wait_ge(drive_ready.sem, drive_ready.at(c.m, k))
                if k >= BUFFERS or c.past >= 1:
                    dve.wait_ge(prod_ready.sem, prod_ready.at(c.m, k - BUFFERS))
                dve.tensor_tensor_scan(state[:, k % BUFFERS, :], p_decay[j][:], drive[:, j, :], 0.0,
                                       ALU.mult, ALU.add).then_inc(state_ready.sem, 1)

            def turn(chunks):
                for s in range(STEPS):
                    if "scan" in chunks:
                        if s % 2 == 0:
                            drives(chunks["scan"], s // 2)
                        scans(chunks["scan"], s)
                    for stage, name, i in PLAN[s]:
                        if stage in chunks:
                            step(name, i, chunks[stage])

            turns(dve, turn)

        @block.gpsimd
        def _(pool):
            pool.wait_ge(weights_in.sem, 16 * n_weights)
            pool.wait_ge(consts_v.sem, CONSTS)

            def step(name, i, c):
                if name == "mean":
                    pool.wait_ge(mean_sq.sem, mean_sq.at(c.m))
                    if c.past >= 1:
                        pool.wait_ge(xn_ready.sem, xn_ready.at(c.m - 1))
                    pool.tensor_tensor(rms[:], ms[:], mhalf[:], ALU.pow).then_inc(rms_ready.sem, 1)
                elif name == "stats":
                    pool.wait_ge(ln_var[i].sem, ln_var[i].at(c.m))
                    pool.tensor_tensor(rstd[:, i, :], var[:, i, :], mhalf[:], ALU.pow
                                       ).then_inc(ln_rstd[i].sem, 1)
                elif name == "add_out_b":
                    pool.wait_ge(xb_in.sem, xb_in.at(c.m))
                    pool.tensor_tensor(xb[:], xb[:], rowb[:, 0, :].unsqueeze(1).to_broadcast(
                        [128, GROUPS, D]), ALU.add).then_inc(xb_ready.sem, 1)
                elif name == "add_bo":
                    pool.wait_ge(ln_ready[0].sem, ln_ready[0].at(c.m))
                    pool.tensor_tensor(x1b[:], x1[:], rowb[:, 2, :].unsqueeze(1).to_broadcast(
                        [128, GROUPS, D]), ALU.add).then_inc(x1b_ready.sem, 1)
                elif name == "k":
                    emptied(pool, "k", 0, c.m)
                    if c.past >= 1:
                        emptied(pool, "down", GROUPS - 1, c.m - 1)
                    k3 = kT[:].rearrange("p (b t) -> p b t", t=SEQ)
                    pool.tensor_tensor(km[:, :, 0, :], k3, masks[:, 0:1].unsqueeze(2).to_broadcast(
                        [128, CHUNK_B, SEQ]), ALU.mult)
                    for a in range(1, PAIRS):
                        g = pool.tensor_scalar(km[:, :, a, :], k3,
                                               masks[:, a:a + 1], 0.0, ALU.mult, ALU.add)
                    g.then_inc(km_ready.sem, 1)
                elif name == "r_rank":
                    pool.wait_ge(route_v.sem, route_v.at(c.m, 4))
                    pool.tensor_tensor(r_eq, r_eq, tri[:].unsqueeze(1).to_broadcast(
                        [128, GROUPS, EXPERTS, EXPERTS]), ALU.mult).then_inc(route_g.sem, 1)
                    pool.wait_ge(route_g.sem, route_g.at(c.m, 0))
                    pool.tensor_tensor(r_gt, r_gt, r_eq, ALU.add).then_inc(route_g.sem, 1)
                elif name == "cw":
                    emptied(pool, "up_u", i, c.m)
                    emptied(pool, "cw", i, c.m)
                    pool.tensor_tensor(acts[i], acts[i], cwr[:, i % 2, :], ALU.mult
                                       ).then_inc(act_ready.sem, 1)

            def products(c, k):
                n, j = divmod(k, HALVES)
                pool.wait_ge(state_ready.sem, state_ready.at(c.m, k))
                if j == 0:
                    emptied(pool, "C", n, c.m)
                if k >= BUFFERS or c.past >= 1:
                    pool.wait_ge(prod_used.sem, prod_used.at(c.m, k - BUFFERS))
                pool.tensor_tensor(prod[:, k % BUFFERS, :], state[:, k % BUFFERS, :], c_rep[:, n % 2, :], ALU.mult
                                   ).then_inc(prod_ready.sem, 1)

            def turn(chunks):
                for s in range(STEPS):
                    if "scan" in chunks:
                        products(chunks["scan"], s)
                    for stage, name, i in PLAN[s]:
                        if stage in chunks:
                            step(name, i, chunks[stage])

            turns(pool, turn)


def constants():
    r = np.arange(128)
    masks = np.zeros((128, PAIRS + 2), np.float32)
    masks[r, (r // HEAD_D) % PAIRS] = 1.0
    masks[r, PAIRS + r // 64] = HEAD_D ** -0.5
    sel_bc = np.tile(np.eye(BC, dtype=np.float32), (3, 1))
    sel_cw = np.zeros((128, FFN_TILES * 128), np.float32)
    col = np.arange(FFN_ROWS)
    expert = col // EXPERT_I
    for part in range(3):
        routed = expert < EXPERTS
        sel_cw[part * EXPERTS + expert[routed], col[routed]] = 0.5
    sel_cw[3 * EXPERTS, col[expert == EXPERTS]] = 0.5
    e = np.arange(EXPERTS)
    tri = np.broadcast_to((e[None, :] < e[:, None]).astype(np.float32), (128, EXPERTS, EXPERTS))
    return {
        "c_masks": masks,
        "c_sel_bc": sel_bc,
        "c_sel_cw": sel_cw,
        "c_ident": np.eye(128, dtype=np.float32),
        "c_tri": np.ascontiguousarray(tri),
    }


def kernel(x, ctx_1024, L0_attn_norm_scale, L0_attn_in_w, L0_attn_in_b, L0_attn_conv_w, L0_attn_conv_b,
           L0_attn_xproj_w, L0_attn_dt_w, L0_attn_dt_b, L0_attn_A_log, L0_attn_D, L0_attn_out_w,
           L0_attn_out_b, L0_xattn_Wq, L0_xattn_bq, L0_xattn_Wk, L0_xattn_bk, L0_xattn_Wv, L0_xattn_bv,
           L0_xattn_Wo, L0_xattn_bo, L0_ffn_w_router, L0_ffn_wg, L0_ffn_wu, L0_ffn_wd, L0_ffn_wg_s,
           L0_ffn_wu_s, L0_ffn_wd_s):
    import concourse.bacc as bacc
    from concourse.bass_utils import run_bass_kernel_spmd

    def halves(a):
        a = np.asarray(a)
        return np.moveaxis(a.reshape(a.shape[:-1] + (HALVES, 128)), -1, 0).swapaxes(1, -1).reshape(128, -1)

    vec = np.concatenate([
        np.asarray(L0_attn_norm_scale).reshape(128, 1),
        np.asarray(L0_attn_in_b).reshape(4, 128).T,
        halves(L0_attn_conv_w), halves(L0_attn_conv_b), halves(L0_attn_dt_b), halves(L0_attn_D),
        halves(np.asarray(L0_attn_A_log).T),
        np.asarray(L0_xattn_bq).reshape(128, 1), np.asarray(L0_xattn_bk).reshape(128, 1)], axis=1)
    rows = np.stack([np.asarray(L0_attn_out_b), np.asarray(L0_xattn_bv), np.asarray(L0_xattn_bo)])
    xproj = np.asarray(L0_attn_xproj_w).reshape(HALVES, 128, RANK + BC)
    xproj = np.concatenate([xproj[:, :, :RANK]] + [xproj[:, :, RANK:]] * 3, axis=2).transpose(1, 0, 2)
    attn = np.stack([np.asarray(w).T for w in (L0_xattn_Wq, L0_xattn_Wk, L0_xattn_Wv, L0_xattn_Wo)], axis=1)
    pad = FFN_TILES * 128 - FFN_ROWS

    def up(routed, shared):
        a = np.asarray(routed).transpose(1, 0, 2).reshape(D, EXPERTS * EXPERT_I)
        shared = np.asarray(shared)
        return np.concatenate([a, shared, np.zeros((D, pad), shared.dtype)], axis=1).reshape(
            D, FFN_TILES, 128)

    shared = np.asarray(L0_ffn_wd_s)
    down = np.concatenate([np.asarray(L0_ffn_wd).reshape(EXPERTS * EXPERT_I, D), shared,
                           np.zeros((pad, D), shared.dtype)], axis=0)
    arrays = {
        "x": np.asarray(x).reshape(BATCH * SEQ, D),
        "ctx_t": np.asarray(ctx_1024).reshape(BATCH * SEQ, D).T,
        "vec": vec, "rows": rows,
        "w_in": np.asarray(L0_attn_in_w).reshape(128, 4, 128),
        "w_xproj": xproj, "w_dt": np.asarray(L0_attn_dt_w),
        "w_out": np.asarray(L0_attn_out_w).reshape(HALVES, 128, D).transpose(1, 0, 2),
        "w_attn": attn, "w_router": np.asarray(L0_ffn_w_router).T,
        "w_gate": up(L0_ffn_wg, L0_ffn_wg_s), "w_up": up(L0_ffn_wu, L0_ffn_wu_s),
        "w_down": down.reshape(FFN_TILES, 128, D).transpose(1, 0, 2),
        **constants(),
    }
    arrays = {k: np.ascontiguousarray(v) for k, v in arrays.items()}
    nc = bacc.Bacc("TRN2", target_bir_lowering=False, num_devices=1)
    args = {k: nc.dram_tensor(f"in_{k}", v.shape, mybir.dt.from_np(v.dtype), kind="ExternalInput").ap()
            for k, v in arrays.items()}
    out = nc.dram_tensor("out_y", (BATCH * SEQ, D), F32, kind="ExternalOutput").ap()
    build(nc, out=out, **args)
    r = run_bass_kernel_spmd(nc, [{f"in_{k}": v for k, v in arrays.items()}], core_ids=[0])
    return r.results[0]["out_y"].reshape(BATCH, SEQ, D)
```

```python
from contextlib import ExitStack

import numpy as np

import concourse.bass as bass
from concourse import mybir

F32 = mybir.dt.float32
BF16 = mybir.dt.bfloat16
ALU = mybir.AluOpType
ACT = mybir.ActivationFunctionType
AX_X = mybir.AxisListType.X

BATCH, SEQ, D = 128, 64, 128
CHUNK_B = 8
T = CHUNK_B * SEQ
CHUNKS = BATCH // CHUNK_B
GROUPS = T // 128
INNER, STATE, RANK, TAPS = 256, 16, 64, 4
HALVES = INNER // 128
HEADS, HEAD_D = 16, 8
PAIRS = HEADS // 2
QUADS = PAIRS // 2
EXPERTS, TOP, EXPERT_I = 8, 2, 176
FFN_ROWS = (EXPERTS + 1) * EXPERT_I
FFN_TILES = -(-FFN_ROWS // 128)
BC = 2 * STATE
RMS_EPS, LN_EPS, TOP_EPS = 1e-6, 1e-5, 1e-20

V_NORM, V_INB, V_CONVW, V_CONVB, V_DTB, V_D, V_ALOG, V_BQ, V_BK, V_BV = np.cumsum(
    [0, 1, 4, HALVES * TAPS, HALVES, HALVES, HALVES, HALVES * STATE, 1, 1]).tolist()
VEC = V_BV + 1

STEPS = STATE * HALVES
SUM_LAG = 2
KM_POOL = 5
BUFFERS = 4
JOINED = (1, 9, 11, 13)
SUMS = STEPS - HALVES * len(JOINED)
BANKS = 5
CHUNK_OF = {"head": 2, "front": 1, "scan": 0, "back": -1, "tail": -2}


PLAN_TEXT = (
    "back.gated0 front.taps0 back.add_out_b0 tail.down0 front.taps1 front.taps2 tail.down1",
    "scan.C1",
    "back.gated1 front.taps3",
    "tail.down2 scan.C2 back.mout0 back.mout1 back.stats0 back.stats1 tail.down3 front.tanh0 "
    "front.silu0",
    "back.norm0 back.norm1 tail.stats4 tail.stats5 back.k0 tail.norm4 tail.norm5 back.v0",
    "back.km0 back.x1T0 back.x1T1 back.v1 scan.C3 back.add_bo0 front.tanh1",
    "back.q0 front.silu1 front.ts0 front.gate_tanh0",
    "scan.C4 front.gated_h0 front.gate_tanh1",
    "back.score0 front.gated_h1 front.dt0",
    "scan.C5 back.score1",
    "front.dt1 back.exp0 back.score2 back.turn0 back.sum0",
    "scan.C6 back.exp1 back.widen0 back.score3 back.mix0 back.turn1 back.sum1",
    "back.exp2 back.widen1 back.score4 back.mix1 back.turn2 back.sum2",
    "scan.C7 back.exp3 back.widen2 back.score5 back.mix2 back.turn3 back.sum3",
    "back.widen3 back.exp4 back.score6 back.mix3 back.turn4 back.sum4",
    "scan.C8 back.exp5 back.widen4 back.score7 back.mix4 back.turn5 back.sum5 back.aout0",
    "back.stats2 back.exp6 back.widen5 back.mix5 back.turn6 back.sum6",
    "back.norm2 scan.C9 back.exp7 back.widen6 back.mix6 back.turn7 back.sum7",
    "back.widen7 back.mix7 back.aout1 front.soft0 back.stats3 front.soft_ln0",
    "scan.C10 back.x2T0 back.norm3 front.bc0 front.delta0",
    "back.x2T1 back.route0",
    "back.up_g0 back.r_exp0 scan.C11 back.r_rank0 back.up_u0",
    "head.squares0 back.up_g1 back.up_u1 head.mean0 back.r_cw0",
    "scan.C12 back.up_g2 back.up_u2 head.scaled0 back.up_g3 back.up_u3",
    "back.cwT0 back.cw0 back.up_g4 back.cw1",
    "back.up_u4 scan.C13 head.xnT0 back.cw2",
    "back.up_g5 back.up_u5",
    "back.up_g6 back.cw3 head.xnT1 back.up_u6 back.up_g7 back.cw4 back.up_u7 scan.C14 "
    "front.bc_split0",
    "back.up_g8 back.up_u8 head.hid0 head.hid1",
    "back.cw5 back.up_g9 back.cw6 back.up_u9 back.up_g10 scan.C15",
    "back.cw7 back.up_u10 back.up_g11 back.cw8 back.up_u11 head.gate0",
    "back.up_g12 back.cw9 back.up_u12 back.cw10 head.gate1 front.C0 back.cw11 back.cw12",
)


def read_step(text):
    stage, name = text.split(".")
    bare = name.rstrip("0123456789")
    return stage, bare, int(name[len(bare):])


PLAN = [[read_step(text) for text in slot.split()] for slot in PLAN_TEXT]
assert len(PLAN) == STEPS
IN_RING = ("C", "down", "mout", "k", "xnT", "v", "hid", "x1T", "q", "score", "mix", "turn", "aout",
           "ts", "bc", "gate", "x2T", "route", "up_g", "up_u", "cwT", "cw", "dt")
RING = [step for slot in PLAN for step in slot if step[1] in IN_RING]
STAGE_OF = {step[1:]: step[0] for step in RING}
assert len(STAGE_OF) == len(RING)


class Signal:

    def __init__(self, sem, per_chunk, step=1):
        self.sem, self.per_chunk, self.step = sem, per_chunk, step

    def at(self, m, k=0):
        return (m * self.per_chunk + (k + 1)) * self.step


class Chunk:

    def __init__(self, m, parity, past):
        self.m, self.parity, self.past = m, parity, past


def joined(k):
    return k // HALVES in JOINED


def held_back(k):
    return k // HALVES + 1 in JOINED


def sum_index(k):
    return sum(not held_back(i) for i in range(k))


def join_index(k):
    return sum(joined(i) for i in range(k))


def ring_place(name, i, m):
    stage = STAGE_OF[name, i]
    at = RING.index((stage, name, i))
    bank = at % BANKS
    same = [j for j in range(bank, len(RING), BANKS)]
    if not isinstance(m, int):
        per_turn = len(same)
        ahead = sum(CHUNK_OF[RING[j][0]] - CHUNK_OF[stage] for j in same)
        return bank, m * per_turn + (ahead + sum(j < at for j in same))
    t = m - CHUNK_OF[stage]
    before = 0
    for j in same:
        chunk = t + CHUNK_OF[RING[j][0]]
        before += min(max(chunk, 0), CHUNKS) + (j < at and 0 <= chunk < CHUNKS)
    return bank, before


def build(nc, x, ctx_t, vec, rows, w_in, w_xproj, w_dt, w_out, w_attn, w_router, w_gate, w_up, w_down,
          c_masks, c_sel_bc, c_sel_cw, c_ident, c_tri, out):
    with ExitStack() as stack:
        def sb(name, shape, dt=F32):
            return stack.enter_context(nc.sbuf_tensor(name, shape, dt))

        def bank(name, dt=F32):
            return stack.enter_context(nc.psum_tensor(name, [128, 2048 // mybir.dt.size(dt)], dt))

        def signal(name, per_chunk=1, step=1):
            return Signal(stack.enter_context(nc.semaphore(name)), per_chunk, step)

        vecs = sb("vecs", [128, VEC])
        rowb = sb("rowb", [128, 2, D])
        win = sb("win", [128, 4, 128])
        wxp = sb("wxp", [128, HALVES, RANK + 3 * BC])
        wdt = sb("wdt", [RANK, INNER])
        wout = sb("wout", [128, HALVES, D])
        wattn = sb("wattn", [128, 4, 128])
        wrt = sb("wrt", [128, EXPERTS])
        wg = sb("wg", [128, FFN_TILES, 128])
        wu = sb("wu", [128, FFN_TILES, 128])
        wd = sb("wd", [128, FFN_TILES, 128])
        masks = sb("masks", [128, PAIRS + 2])
        sel_bc = sb("sel_bc", [3 * BC, BC], BF16)
        sel_cw = sb("sel_cw", [128, FFN_TILES, 128], BF16)
        ident = sb("ident", [128, 128])
        ident16 = sb("ident16", [128, 128], BF16)
        tri = sb("tri", [128, EXPERTS, EXPERTS])
        a_neg = sb("a_neg", [128, HALVES, STATE])
        halfv = sb("halfv", [128, 2 + HALVES * TAPS + HALVES])
        bqs = sb("bqs", [128, 2])
        mhalf = sb("mhalf", [128, GROUPS])
        xf = sb("xf", [128, GROUPS, D])
        ss = sb("ss", [128, GROUPS])
        ms = sb("ms", [128, GROUPS])
        rms = sb("rms", [128, GROUPS])
        xn = sb("xn", [128, GROUPS, D])
        xnT = sb("xnT", [128, T])
        hpad = sb("hpad", [128, HALVES, CHUNK_B, SEQ + TAPS - 1])
        zc = sb("zc", [128, HALVES, T])
        gh = sb("gh", [128, HALVES, T])
        h = sb("h", [128, 2, HALVES, T])
        gate = sb("gate", [128, 2, HALVES, T])
        delta = sb("delta", [128, 2, HALVES, T])
        u = sb("u", [128, 2, HALVES, T])
        bc16 = sb("bc16", [3 * BC, 2, T], BF16)
        bc_rest = sb("bc_rest", [3 * BC, T])
        ts_sb = sb("ts_sb", [RANK, T])
        sp_a = sb("sp_a", [128, HALVES, T])
        sq = sp_a[:, 0, :]
        decay = sb("decay", [128, HALVES, T])
        c_rep = sb("c_rep", [128, 2, T])
        drive = sb("drive", [128, 2, T])
        state = sb("state", [128, BUFFERS, T])
        prod = sb("prod", [128, BUFFERS, T])
        yg = sb("yg", [128, HALVES, T])
        xb = sb("xb", [128, GROUPS, D])
        ctxT = sb("ctxT", [128, CHUNK_B, 2, SEQ])
        stats = sb("stats", [128, 3, GROUPS, 6])
        mv = sb("mv", [128, 3, GROUPS, 2])
        var = sb("var", [128, 3, GROUPS])
        rstd = sb("rstd", [128, 3, GROUPS])
        x1 = sb("x1", [128, GROUPS, D])
        x1b = sb("x1b", [128, GROUPS, D])
        x1T = sb("x1T", [128, T])
        qs = sb("qs", [128, CHUNK_B, 2, SEQ])
        kT = sb("kT", [128, T])
        km = sb("km", [128, CHUNK_B, PAIRS, SEQ])
        vm = sb("vm", [128, CHUNK_B, QUADS, 128])
        shifted = sb("shifted", [128, 2, PAIRS, SEQ])
        smax = sb("smax", [128, 2, PAIRS])
        ex = sb("ex", [128, 2, PAIRS, SEQ])
        den = sb("den", [128, 2, PAIRS])
        rden = sb("rden", [128, 2, PAIRS])
        exT = sb("exT", [128, QUADS, 128])
        rd_wide = sb("rd_wide", [128, 128])
        rdT = sb("rdT", [128, 128])
        aT = sb("aT", [128, T])
        x2 = sb("x2", [128, GROUPS, D])
        x2T = sb("x2T", [128, T])
        r_max = sb("r_max", [128, GROUPS])
        r_log = sb("r_log", [128, GROUPS, EXPERTS])
        r_exp = sb("r_exp", [128, GROUPS, EXPERTS])
        r_sum = sb("r_sum", [128, GROUPS])
        r_rec = sb("r_rec", [128, GROUPS])
        r_prob = sb("r_prob", [128, GROUPS, EXPERTS])
        r_rank = sb("r_rank", [128, GROUPS, EXPERTS])
        r_sel = sb("r_sel", [128, GROUPS, EXPERTS])
        r_cw = sb("r_cw", [128, GROUPS, EXPERTS])
        r_rest = sb("r_rest", [128, GROUPS, EXPERTS])
        cw16 = sb("cw16", [128, GROUPS, 128], BF16)
        cwT = sb("cwT", [128, T], BF16)
        th = exT[:].rearrange("p a q -> p (a q)")
        gth = ex[:, 0].rearrange("p a k -> p (a k)")
        gt = shifted[:].rearrange("p i a k -> p i (a k)")
        ga = kT[:]
        cwr = ex[:].rearrange("p i a k -> p i (a k)")
        pairwise = x1T[:].rearrange("p (w g a b) -> p w g a b", w=2, g=GROUPS, a=EXPERTS)
        r_gt, r_eq = pairwise[:, 0], pairwise[:, 1]
        acts_more = sb("acts_more", [128, FFN_TILES - CHUNK_B, T])
        acts = [km[:, j, :, :].rearrange("p a k -> p (a k)") if j < CHUNK_B else
                acts_more[:, j - CHUNK_B, :] for j in range(FFN_TILES)]
        sel_cw32 = acts_more[:].rearrange("p j t -> p (j t)")[:, 0:FFN_TILES * 128]
        sel_bc32 = zc[0:3 * BC, 0, 0:BC]

        p_b = bank("p_b")
        p_y = [bank(f"p_y{j}") for j in range(HALVES)]
        p_ring = [bank(f"p_ring{i}") for i in range(BANKS)]

        n_weights = 17
        weights_in = signal("weights_in")
        ready_const = signal("ready_const")
        bv_ready = signal("bv_ready")
        consts_v = signal("consts_v")
        CONSTS = 8
        ring_full = [signal(f"ring_full{i}") for i in range(BANKS)]
        ring_free = [signal(f"ring_free{i}") for i in range(BANKS)]
        x_in, xb_in, out_done = (signal(n, 1, 16) for n in ("x_in", "xb_in", "out_done"))
        ctx_in = signal("ctx_in", 2, 16)
        squares_done, mean_sq, rms_ready, xn_ready = (
            signal(n) for n in ("squares_done", "mean_sq", "rms_ready", "xn_ready"))
        conv_th, gate_th, h_ready, gate_ready = (
            signal(n, HALVES) for n in ("conv_th", "gate_th", "h_ready", "gate_ready"))
        conv_tap = signal("conv_tap", HALVES * TAPS)
        bc_part = signal("bc_part", 5)
        spexp_ready, spln_ready, delta_ready, u_ready = (
            signal(n) for n in ("spexp_ready", "spln_ready", "delta_ready", "u_ready"))
        b_ready = signal("b_ready", STATE)
        decay_ready, drive_ready, state_ready, prod_ready = (
            signal(n, STEPS) for n in ("decay_ready", "drive_ready", "state_ready", "prod_ready"))
        join_ready = signal("join_ready", STEPS - SUMS)
        prod_used = signal("prod_used", SUMS)
        p_y_read, yg_ready = signal("p_y_read", 2), signal("yg_ready", 2)
        xb_ready, x1b_ready = signal("xb_ready"), signal("x1b_ready")
        ln_aggr, ln_var, ln_rstd, ln_ready = (
            [signal(f"{n}{ln}", 2) for ln in range(3)] for n in ("ln_aggr", "ln_var", "ln_rstd", "ln_ready"))
        ln_stats = [[signal(f"ln_stats{ln}_{half}") for half in range(2)] for ln in range(3)]
        km_ready, km_more = signal("km_ready"), signal("km_more")
        max_ready, shift_ready, exp_ready, den_ready, rden_ready, rdwide_ready, rdT_ready = (
            signal(n, CHUNK_B) for n in ("max_ready", "shift_ready", "exp_ready", "den_ready", "rden_ready",
                                         "rdwide_ready", "rdT_ready"))
        route_v, route_exp, route_g = signal("route_v", 15), signal("route_exp"), signal("route_g", 2)
        gt_ready, act_ready = signal("gt_ready", FFN_TILES), signal("act_ready", FFN_TILES)

        def column(at):
            return vecs[:, at:at + 1]

        def filled(eng, name, i, m):
            r, before = ring_place(name, i, m)
            eng.wait_ge(ring_full[r].sem, before + 1)
            return p_ring[r]

        def emptied(eng, name, i, m):
            r, before = ring_place(name, i, m)
            eng.wait_ge(ring_free[r].sem, before + 1)

        def free(name, i):
            return ring_free[ring_place(name, i, 0)[0]].sem

        def by_group(a):
            return a.unsqueeze(2)

        def turns(eng, turn):
            def peeled(t):
                return {stage: Chunk(t + off, (t + off) % 2, t + off)
                        for stage, off in CHUNK_OF.items() if 0 <= t + off < CHUNKS}

            for t in range(-2, 3):
                turn(peeled(t))
            with eng.Fori(3, 12, 2) as t0:
                for odd in range(2):
                    turn({stage: Chunk(t0 + (off + odd), (3 + odd + off) % 2, 3 + off)
                          for stage, off in CHUNK_OF.items()})
            for t in range(13, CHUNKS + 2):
                turn(peeled(t))

        block = stack.enter_context(nc.Block())

        @block.sync
        def _(sp):
            for to, src in ((vecs[:], vec), (win[:], w_in), (ident[:], c_ident), (wxp[:], w_xproj),
                            (wdt[:], w_dt), (sel_bc32, c_sel_bc), (wout[:], w_out), (wattn[:], w_attn),
                            (wrt[:], w_router), (masks[:], c_masks), (tri[:], c_tri),
                            (sel_cw32, c_sel_cw), (wg[:], w_gate),
                            (wu[:], w_up), (wd[:], w_down),
                            (rowb[:, 0, :], rows[0].partition_broadcast(128)),
                            (rowb[:, 1, :], rows[1].partition_broadcast(128))):
                sp.dma_start(to, src).then_inc(weights_in.sem, 16)

            def turn(chunks):
                head, scan, tail = (chunks.get(n) for n in ("head", "scan", "tail"))
                if head:
                    if head.past >= 1:
                        sp.wait_ge(xn_ready.sem, xn_ready.at(head.m - 1))
                    sp.dma_start(xf[:], x[bass.ds(head.m * T, T), :].rearrange("(g p) d -> p g d", p=128)
                                 ).then_inc(x_in.sem, 16)
                if tail:
                    sp.wait_ge(ln_ready[2].sem, ln_ready[2].at(tail.m, 1))
                    sp.dma_start(out[bass.ds(tail.m * T, T), :].rearrange("(g p) d -> p g d", p=128),
                                 x2[:]).then_inc(out_done.sem, 16)
                if scan:
                    if scan.past >= 1:
                        emptied(sp, "v", 1, scan.m - 1)
                    sp.dma_start(xb[:], x[bass.ds(scan.m * T, T), :].rearrange("(g p) d -> p g d", p=128)
                                 ).then_inc(xb_in.sem, 16)
                    for twice in range(2):
                        sp.dma_start(ctxT[:, :, twice, :], ctx_t[:, bass.ds(scan.m * T, T)].rearrange(
                            "d (b t) -> d b t", t=SEQ)).then_inc(ctx_in.sem, 16)

            turns(sp, turn)
            sp.wait_ge(out_done.sem, out_done.at(CHUNKS - 1))

        @block.tensor
        def _(pe):
            pe.wait_ge(weights_in.sem, 16 * n_weights)
            pe.matmul(p_b[:, 0:D], column(V_BV).to_broadcast([128, 128]), wattn[:, 3, :],
                      start=True, stop=True).then_inc(bv_ready.sem, 1)
            pe.wait_ge(consts_v.sem, CONSTS)

            def step(name, i, c):
                if name not in IN_RING:
                    return
                r, before = ring_place(name, i, c.m)
                if not isinstance(before, int) or before > 0:
                    pe.wait_ge(ring_free[r].sem, before)
                p = p_ring[r]
                if name == "C":
                    if i == 0:
                        pe.wait_ge(bc_part.sem, bc_part.at(c.m, 4))
                    mm = pe.matmul(p[:], sel_bc[:, STATE + i:STATE + i + 1].to_broadcast([3 * BC, 128]),
                                   bc16[:, c.parity, :], start=True, stop=True)
                elif name == "xnT":
                    pe.wait_ge(xn_ready.sem, xn_ready.at(c.m))
                    for g in range(2):
                        mm = pe.transpose(p[:, g * 128:(g + 1) * 128], xn[:, 2 * i + g, :], ident[:])
                elif name in ("hid", "gate"):
                    emptied(pe, "xnT", 1, c.m)
                    mm = pe.matmul(p[:], win[:, i + 2 * (name == "gate"), :], xnT[:], start=True, stop=True)
                elif name == "ts":
                    pe.wait_ge(h_ready.sem, h_ready.at(c.m, 1))
                    for j in range(HALVES):
                        mm = pe.matmul(p[0:RANK, :], wxp[:, j, 0:RANK], h[:, c.parity, j, :],
                                       start=j == 0, stop=j == HALVES - 1)
                elif name == "bc":
                    for j in range(HALVES):
                        mm = pe.matmul(p[0:3 * BC, :], wxp[:, j, RANK:RANK + 3 * BC], h[:, c.parity, j, :],
                                       start=j == 0, stop=j == HALVES - 1)
                elif name == "dt":
                    emptied(pe, "ts", 0, c.m)
                    mm = pe.matmul(p[:], wdt[:, i * 128:(i + 1) * 128], ts_sb[:], start=True, stop=True)
                elif name == "mout":
                    pe.wait_ge(yg_ready.sem, yg_ready.at(c.m, 1))
                    for g in range(2):
                        for j in range(HALVES):
                            mm = pe.matmul(p[:, g * D:(g + 1) * D],
                                           yg[:, j, (2 * i + g) * 128:(2 * i + g + 1) * 128],
                                           wout[:, j, :], start=j == 0, stop=j == HALVES - 1)
                elif name in ("x1T", "x2T"):
                    src, ln = (x1, 0) if name == "x1T" else (x2, 1)
                    pe.wait_ge(ln_ready[ln].sem, ln_ready[ln].at(c.m, i))
                    for g in range(2):
                        mm = pe.transpose(p[:, g * 128:(g + 1) * 128], src[:, 2 * i + g, :], ident[:])
                elif name == "q":
                    emptied(pe, "x1T", 1, c.m)
                    mm = pe.matmul(p[:], wattn[:, 0, :], x1T[:], start=True, stop=True)
                elif name == "k":
                    pe.wait_ge(ctx_in.sem, ctx_in.at(c.m, 1))
                    mm = pe.matmul(p[:], wattn[:, 1, :], ctxT[:, :, 0, :], start=True, stop=True)
                elif name == "v":
                    for b in range(4):
                        twice = ctxT[:, 4 * i + b, :, :].rearrange("d a t -> d (a t)")
                        mm = pe.matmul(p[:, b * 128:(b + 1) * 128], twice, wattn[:, 2, :],
                                       start=True, stop=True)
                elif name == "score":
                    if i == 0:
                        emptied(pe, "q", 0, c.m)
                        pe.wait_ge(km_ready.sem, km_ready.at(c.m))
                        pe.wait_ge(km_more.sem, km_more.at(c.m))
                    mm = pe.matmul(p[:], qs[:, i, :, :].rearrange("p s q -> p (s q)"),
                                   km[:, i, :, :].rearrange("p a k -> p (a k)"), start=True, stop=True)
                elif name == "turn":
                    pe.wait_ge(exp_ready.sem, exp_ready.at(c.m, i))
                    for q in range(QUADS):
                        mm = pe.transpose(p[:, q * 128:(q + 1) * 128],
                                          ex[:, i % 2, 2 * q:2 * q + 2, :].rearrange("p a k -> p (a k)"),
                                          ident[:])
                elif name == "mix":
                    emptied(pe, "turn", i, c.m)
                    if i == 0:
                        emptied(pe, "v", 1, c.m)
                    for q in range(QUADS):
                        pe.matmul(p[:, 0:128], vm[:, i, q, :], exT[:, q, :],
                                  start=q == 0, stop=q == QUADS - 1)
                    pe.wait_ge(rdwide_ready.sem, rdwide_ready.at(c.m, i))
                    mm = pe.transpose(p[:, 128:256], rd_wide[:], ident[:])
                elif name == "aout":
                    emptied(pe, "mix", (i + 1) * CHUNK_B // 2 - 1, c.m)
                    for g in range(2):
                        mm = pe.matmul(p[:, g * D:(g + 1) * D],
                                       aT[:, (2 * i + g) * 128:(2 * i + g + 1) * 128],
                                       wattn[:, 3, :], start=True, stop=True)
                elif name == "route":
                    emptied(pe, "x2T", 1, c.m)
                    for g in range(GROUPS):
                        mm = pe.matmul(p[:, g * EXPERTS:(g + 1) * EXPERTS], x2T[:, g * 128:(g + 1) * 128],
                                       wrt[:], start=True, stop=True)
                elif name in ("up_g", "up_u"):
                    mm = pe.matmul(p[:], (wg if name == "up_g" else wu)[:, i, :], x2T[:],
                                   start=True, stop=True)
                elif name == "cwT":
                    pe.wait_ge(route_v.sem, route_v.at(c.m, 14))
                    p16 = p[:].bitcast(BF16)
                    for g in range(GROUPS):
                        mm = pe.transpose(p16[:, g * 128:(g + 1) * 128], cw16[:, g, :], ident16[:])
                elif name == "cw":
                    if i == 0:
                        emptied(pe, "cwT", 0, c.m)
                    mm = pe.matmul(p[:], sel_cw[:, i, :], cwT[:], start=True, stop=True)
                else:
                    for j in range(FFN_TILES):
                        if i == 0 and j in (0, FFN_TILES - 2, FFN_TILES - 1):
                            pe.wait_ge(act_ready.sem, act_ready.at(c.m, max(j, FFN_TILES - 3)))
                        mm = pe.matmul(p[:, 0:D], acts[j][:, i * 128:(i + 1) * 128],
                                       wd[:, j, :], start=j == 0, stop=j == FFN_TILES - 1)
                mm.then_inc(ring_full[r].sem, 1)

            def spread_b(c, n):
                if n == 0:
                    pe.wait_ge(bc_part.sem, bc_part.at(c.m, 4))
                if n > 0 or c.past >= 1:
                    pe.wait_ge(drive_ready.sem, drive_ready.at(c.m, HALVES * n - 1))
                pe.matmul(p_b[:], sel_bc[:, n:n + 1].to_broadcast([3 * BC, 128]), bc16[:, c.parity, :],
                          start=True, stop=True).then_inc(b_ready.sem, 1)

            def sum_n(c, k):
                n, j = divmod(k, HALVES)
                if held_back(k):
                    return
                first = sum_index(k) == j
                if first and c.past >= 1:
                    pe.wait_ge(p_y_read.sem, p_y_read.at(c.m - 1, j))
                if joined(k):
                    pe.wait_ge(join_ready.sem, join_ready.at(c.m, join_index(k)))
                else:
                    pe.wait_ge(prod_ready.sem, prod_ready.at(c.m, k))
                pe.matmul(p_y[j][:], ident[:], prod[:, k % BUFFERS, :],
                          start=first, stop=n == STATE - 1).then_inc(prod_used.sem, 1)

            def turn(chunks):
                for s in range(STEPS):
                    if s % 2 == 1:
                        n = (s + 1) // 2 % STATE
                        if ("scan" if n else "front") in chunks:
                            spread_b(chunks["scan" if n else "front"], n)
                    own = [e for e in PLAN[s] if e[0] in chunks]
                    for e in own[:1]:
                        step(e[1], e[2], chunks[e[0]])
                    k = (s - SUM_LAG) % STEPS
                    if ("scan" if s >= SUM_LAG else "back") in chunks:
                        sum_n(chunks["scan" if s >= SUM_LAG else "back"], k)
                    for e in own[1:]:
                        step(e[1], e[2], chunks[e[0]])

            turns(pe, turn)

        @block.scalar
        def _(act):
            act.wait_ge(weights_in.sem, 16 * n_weights)
            act.activation(a_neg[:].rearrange("p a n -> p (a n)"), vecs[:, V_ALOG:V_ALOG + HALVES * STATE],
                           ACT.Exp).then_inc(ready_const.sem, 1)
            act.wait_ge(consts_v.sem, CONSTS)

            def step(name, i, c):
                par = c.parity
                if name == "squares":
                    act.wait_ge(x_in.sem, x_in.at(c.m))
                    if c.past >= 1:
                        act.wait_ge(mean_sq.sem, mean_sq.at(c.m - 1))
                        act.wait_ge(delta_ready.sem, delta_ready.at(c.m - 1))
                    for g in range(GROUPS):
                        a = act.activation(sq[:, g * D:(g + 1) * D], xf[:, g, :], ACT.Square,
                                           accum_out=ss[:, g:g + 1])
                    a.then_inc(squares_done.sem, 1)
                elif name == "C":
                    p = filled(act, name, i, c.m)
                    if i > 1:
                        act.wait_ge(prod_ready.sem, prod_ready.at(c.m, HALVES * (i - 1) - 1))
                    elif c.past >= 1:
                        act.wait_ge(prod_ready.sem, prod_ready.at(c.m - 1, STEPS + HALVES * (i - 1) - 1))
                    act.activation(c_rep[:, i % 2, :], p[:], ACT.Copy).then_inc(free(name, i), 1)
                elif name == "xnT":
                    p = filled(act, name, i, c.m)
                    act.activation(xnT[:, i * 256:(i + 1) * 256], p[:, 0:256], ACT.Copy,
                                   scale=column(V_NORM)).then_inc(free(name, i), 1)
                elif name == "hid":
                    p = filled(act, name, i, c.m)
                    if c.past >= 1:
                        act.wait_ge(conv_tap.sem, conv_tap.at(c.m - 1, i * TAPS + TAPS - 1))
                    act.activation(hpad[:, i, :, TAPS - 1:], p[:].rearrange("p (b t) -> p b t", t=SEQ),
                                   ACT.Identity, bias=column(V_INB + i)).then_inc(free(name, i), 1)
                elif name == "tanh":
                    act.wait_ge(conv_tap.sem, conv_tap.at(c.m, i * TAPS + TAPS - 1))
                    if i == 1:
                        act.wait_ge(h_ready.sem, h_ready.at(c.m, 0))
                    act.activation(th, zc[:, i, :], ACT.Tanh).then_inc(conv_th.sem, 1)
                elif name == "gate":
                    p = filled(act, name, i, c.m)
                    if c.past >= 1:
                        act.wait_ge(gate_ready.sem, gate_ready.at(c.m - 1, i))
                    act.activation(gh[:, i, :], p[:], ACT.Identity, scale=0.5,
                                   bias=halfv[:, i:i + 1]).then_inc(free(name, i), 1)
                elif name == "gate_tanh":
                    emptied(act, "gate", i, c.m)
                    if i > 0 or c.past >= 1:
                        act.wait_ge(gate_ready.sem, gate_ready.at(c.m, i - 1))
                    act.activation(gth, gh[:, i, :], ACT.Tanh).then_inc(gate_th.sem, 1)
                elif name == "ts":
                    p = filled(act, name, i, c.m)
                    act.activation(ts_sb[:], p[0:RANK, :], ACT.Copy).then_inc(free(name, i), 1)
                elif name == "bc":
                    p = filled(act, name, i, c.m)
                    act.activation(bc_rest[:], p[0:3 * BC, :], ACT.Copy).then_inc(free(name, i), 1)
                elif name == "dt":
                    p = filled(act, name, i, c.m)
                    act.activation(delta[:, par, i, :], p[:], ACT.Relu, bias=column(V_DTB + i))
                    act.activation(sp_a[:, i, :], p[:], ACT.Abs,
                                   bias=column(V_DTB + i)).then_inc(free(name, i), 1)
                elif name == "soft":
                    both = sp_a[:].rearrange("p j t -> p (j t)")
                    emptied(act, "dt", 1, c.m)
                    act.activation(both, both, ACT.Exp, scale=-1.0).then_inc(spexp_ready.sem, 1)
                elif name == "soft_ln":
                    both = sp_a[:].rearrange("p j t -> p (j t)")
                    act.wait_ge(spexp_ready.sem, spexp_ready.at(c.m))
                    act.activation(both, both, ACT.Ln, bias=1.0).then_inc(spln_ready.sem, 1)
                elif name == "k":
                    p = filled(act, name, i, c.m)
                    if c.past >= 1:
                        emptied(act, "up_u", FFN_TILES - 1, c.m - 1)
                    act.activation(kT[:], p[:], ACT.Identity, bias=column(V_BK)).then_inc(free(name, i), 1)
                elif name == "x1T":
                    p = filled(act, name, i, c.m)
                    act.activation(x1T[:, i * 256:(i + 1) * 256], p[:, 0:256], ACT.Copy).then_inc(free(name, i), 1)
                elif name == "q":
                    p = filled(act, name, i, c.m)
                    for s in range(2):
                        a = act.activation(qs[:, :, s, :], p[:].rearrange("p (b t) -> p b t", t=SEQ),
                                           ACT.Identity, scale=masks[:, PAIRS + s:PAIRS + s + 1],
                                           bias=bqs[:, s:s + 1])
                    a.then_inc(free(name, i), 1)
                elif name == "v":
                    p = filled(act, name, i, c.m)
                    for half in range(2):
                        r = slice(64 * half, 64 * half + 64)
                        for s in range(2):
                            src = p[r, :].rearrange("p (b s q a d) -> p b s q a d", b=4, s=2, q=QUADS, a=2)[
                                :, :, s, :, half, :]
                            base = vm[r, 4 * i:4 * i + 4, :, :]
                            part = list(base.ap[:1]) + [(QUADS * 128, 4), (128 + 2 * HEAD_D, QUADS), (1, HEAD_D)]
                            to = bass.AP(base.tensor, base.offset + 64 * s + HEAD_D * half, part)
                            a = act.activation(to, src, ACT.Copy)
                    a.then_inc(free(name, i), 1)
                elif name == "km":
                    emptied(act, "k", 0, c.m)
                    if c.past >= 1:
                        emptied(act, "down", GROUPS - 1, c.m - 1)
                    for pair in range(KM_POOL, PAIRS):
                        a = act.activation(km[:, :, pair, :], kT[:].rearrange("p (b t) -> p b t", t=SEQ),
                                           ACT.Copy, scale=masks[:, pair:pair + 1])
                    a.then_inc(km_more.sem, 1)
                elif name == "score":
                    p = filled(act, name, i, c.m)
                    if i >= 2:
                        act.wait_ge(exp_ready.sem, exp_ready.at(c.m, i - 2))
                    act.activation(shifted[:, i % 2, :, :].rearrange("p a k -> p (a k)"), p[:],
                                   ACT.Copy).then_inc(free(name, i), 1)
                elif name == "exp":
                    act.wait_ge(shift_ready.sem, shift_ready.at(c.m, i))
                    act.activation(ex[:, i % 2, :, :].rearrange("p a k -> p (a k)"),
                                   shifted[:, i % 2, :, :].rearrange("p a k -> p (a k)"),
                                   ACT.Exp).then_inc(exp_ready.sem, 1)
                elif name == "widen":
                    act.wait_ge(rden_ready.sem, rden_ready.at(c.m, i))
                    act.activation(rd_wide[:].rearrange("p (s a d) -> p s a d", s=2, d=HEAD_D),
                                   rden[:, i % 2, :].unsqueeze(1).unsqueeze(3).to_broadcast(
                                       [128, 2, PAIRS, HEAD_D]), ACT.Copy).then_inc(rdwide_ready.sem, 1)
                elif name == "turn":
                    p = filled(act, name, i, c.m)
                    act.activation(exT[:].rearrange("p a q -> p (a q)"), p[:],
                                   ACT.Copy).then_inc(free(name, i), 1)
                elif name == "mix":
                    p = filled(act, name, i, c.m)
                    if i > 0:
                        emptied(act, "mix", i - 1, c.m)
                    elif c.past >= 1:
                        emptied(act, "mix", CHUNK_B - 1, c.m - 1)
                    act.activation(rdT[:], p[:, 128:256], ACT.Copy).then_inc(rdT_ready.sem, 1)
                elif name == "x2T":
                    p = filled(act, name, i, c.m)
                    act.activation(x2T[:, i * 256:(i + 1) * 256], p[:, 0:256], ACT.Copy).then_inc(free(name, i), 1)
                elif name == "r_exp":
                    emptied(act, "route", 0, c.m)
                    act.activation(r_exp[:].rearrange("p g e -> p (g e)"),
                                   r_log[:].rearrange("p g e -> p (g e)"),
                                   ACT.Exp).then_inc(route_exp.sem, 1)
                elif name == "up_g":
                    p = filled(act, name, i, c.m)
                    if i >= 2:
                        emptied(act, "up_g", i - 2, c.m)
                    act.activation(gt[:, i % 2, :], p[:], ACT.Tanh, scale=0.5).then_inc(gt_ready.sem, 1)
                elif name == "cwT":
                    p = filled(act, name, i, c.m)
                    act.activation(cwT[:], p[:].bitcast(BF16)[:, 0:T], ACT.Copy).then_inc(free(name, i), 1)
                elif name == "cw":
                    p = filled(act, name, i, c.m)
                    if i > 1:
                        act.wait_ge(act_ready.sem, act_ready.at(c.m, i - 2))
                    act.activation(cwr[:, i % 2, :], p[:], ACT.Copy).then_inc(free(name, i), 1)

            def decays(c, k):
                n, j = divmod(k, HALVES)
                if k == 0:
                    act.wait_ge(delta_ready.sem, delta_ready.at(c.m))
                if n > 0 or c.past >= 1:
                    act.wait_ge(state_ready.sem, state_ready.at(c.m, k - HALVES))
                act.activation(decay[:, j, :].rearrange("p (b t) -> p b t", t=SEQ)[:, :, 1:],
                               delta[:, c.parity, j, :].rearrange("p (b t) -> p b t", t=SEQ)[:, :, 1:],
                               ACT.Exp, scale=a_neg[:, j, n:n + 1]).then_inc(decay_ready.sem, 1)

            def turn(chunks):
                for s in range(STEPS):
                    k = (s + 1) % STEPS
                    if ("scan" if k else "front") in chunks:
                        decays(chunks["scan" if k else "front"], k)
                    for stage, name, i in PLAN[s]:
                        if stage in chunks:
                            step(name, i, chunks[stage])

            turns(act, turn)

        @block.vector
        def _(dve):
            dve.memset(decay[:], 0.0)
            dve.memset(hpad[:], 0.0)
            dve.memset(vm[:], 0.0)
            dve.memset(mhalf[:], -0.5)
            dve.memset(cw16[:], 0.0).then_inc(consts_v.sem, 1)
            dve.wait_ge(consts_v.sem, 1)
            dve.memset(cw16[:, :, 3 * EXPERTS:3 * EXPERTS + 1], 1.0).then_inc(consts_v.sem, 1)
            dve.wait_ge(weights_in.sem, 16 * n_weights)
            dve.tensor_scalar(halfv[:, 0:2], vecs[:, V_INB + 2:V_INB + 4], 0.5, None,
                              ALU.mult).then_inc(consts_v.sem, 1)
            dve.tensor_scalar(halfv[:, 2:], vecs[:, V_CONVW:V_CONVW + HALVES * TAPS + HALVES], 0.5, None,
                              ALU.mult).then_inc(consts_v.sem, 1)
            dve.tensor_scalar(bqs[:], masks[:, PAIRS:PAIRS + 2], column(V_BQ), None,
                              ALU.mult).then_inc(consts_v.sem, 1)
            dve.tensor_copy(ident16[:], ident[:])
            dve.tensor_copy(sel_bc[:], sel_bc32)
            dve.tensor_copy(sel_cw[:].rearrange("p j c -> p (j c)"), sel_cw32).then_inc(consts_v.sem, 1)
            dve.wait_ge(bv_ready.sem, 1)
            dve.tensor_tensor(rowb[:, 1, :], rowb[:, 1, :], p_b[:, 0:D], ALU.add).then_inc(consts_v.sem, 1)
            dve.wait_ge(ready_const.sem, 1)
            dve.tensor_scalar(a_neg[:].rearrange("p a n -> p (a n)"), a_neg[:].rearrange("p a n -> p (a n)"),
                              -1.0, None, ALU.mult).then_inc(consts_v.sem, 1)
            dve.wait_ge(consts_v.sem, CONSTS)

            def ln_statistics(c, ln, half, src):
                groups = range(2 * half, 2 * half + 2)
                for g in groups:
                    d = dve.bn_stats(stats[:, ln, g, :], src[:, g, :])
                d.then_inc(ln_stats[ln][half].sem, 1)
                dve.wait_ge(consts_v.sem, CONSTS)
                dve.wait_ge(ln_stats[ln][half].sem, ln_stats[ln][half].at(c.m))
                for g in groups:
                    d = dve.bn_aggr(mv[:, ln, g, :], stats[:, ln, g, :])
                d.then_inc(ln_aggr[ln].sem, 1)
                dve.wait_ge(ln_aggr[ln].sem, ln_aggr[ln].at(c.m, half))
                dve.tensor_scalar(var[:, ln, 2 * half:2 * half + 2], mv[:, ln, 2 * half:2 * half + 2, 1],
                                  LN_EPS, None, ALU.add).then_inc(ln_var[ln].sem, 1)

            def ln_normalise(c, ln, half, src, to):
                dve.wait_ge(ln_rstd[ln].sem, ln_rstd[ln].at(c.m, half))
                for g in range(2 * half, 2 * half + 2):
                    d = dve.tensor_scalar(to[:, g, :], src[:, g, :], mv[:, ln, g, 0:1],
                                          rstd[:, ln, g:g + 1], ALU.subtract, ALU.mult)
                d.then_inc(ln_ready[ln].sem, 1)

            wide = [128, GROUPS, EXPERTS]
            LN_IN, LN_OUT = (xb, x1b, x2), (x1, x2, x2)

            def step(name, i, c):
                par = c.parity
                if name == "mean":
                    dve.wait_ge(squares_done.sem, squares_done.at(c.m))
                    if c.past >= 1:
                        dve.wait_ge(rms_ready.sem, rms_ready.at(c.m - 1))
                    dve.tensor_scalar(ms[:], ss[:], 1.0 / D, RMS_EPS, ALU.mult, ALU.add
                                      ).then_inc(mean_sq.sem, 1)
                elif name == "scaled":
                    dve.wait_ge(rms_ready.sem, rms_ready.at(c.m))
                    if c.past >= 1:
                        emptied(dve, "xnT", 1, c.m - 1)
                    dve.tensor_tensor(xn[:], xf[:], by_group(rms[:]).to_broadcast([128, GROUPS, D]),
                                      ALU.mult).then_inc(xn_ready.sem, 1)
                elif name == "taps":
                    j, pair = divmod(i, 2)
                    z = zc[:, j, :].rearrange("p (b t) -> p b t", t=SEQ)
                    for k in range(2 * pair, 2 * pair + 2):
                        w = halfv[:, 2 + j * TAPS + k:3 + j * TAPS + k]
                        if k == 0:
                            emptied(dve, "hid", j, c.m)
                            if c.past >= 1:
                                dve.wait_ge(h_ready.sem, h_ready.at(c.m - 1, j))
                            b = halfv[:, 2 + HALVES * TAPS + j:3 + HALVES * TAPS + j]
                            dve.tensor_scalar(z, hpad[:, j, :, 0:SEQ], w, b, ALU.mult,
                                              ALU.add).then_inc(conv_tap.sem, 1)
                        else:
                            dve.wait_ge(conv_tap.sem, conv_tap.at(c.m, j * TAPS + k - 1))
                            dve.scalar_tensor_tensor(z, hpad[:, j, :, k:k + SEQ], w, z, ALU.mult,
                                                     ALU.add).then_inc(conv_tap.sem, 1)
                elif name == "silu":
                    dve.wait_ge(conv_th.sem, conv_th.at(c.m, i))
                    dve.scalar_tensor_tensor(h[:, par, i, :], th, 1.0, zc[:, i, :], ALU.add,
                                             ALU.mult).then_inc(h_ready.sem, 1)
                elif name == "gated_h":
                    dve.wait_ge(gate_th.sem, gate_th.at(c.m, i))
                    dve.scalar_tensor_tensor(gate[:, par, i, :], gth, 1.0, gh[:, i, :], ALU.add,
                                             ALU.mult).then_inc(gate_ready.sem, 1)
                elif name == "bc_split":
                    emptied(dve, "bc", 0, c.m)
                    s16 = bc16[:, par, :]
                    dve.tensor_copy(s16, bc_rest[:]).then_inc(bc_part.sem, 1)
                    dve.wait_ge(bc_part.sem, bc_part.at(c.m, 0))
                    for q in (1, 2):
                        r = slice(q * BC, (q + 1) * BC)
                        d = dve.tensor_tensor(bc_rest[r, :], bc_rest[r, :], s16[r, :], ALU.subtract)
                    d.then_inc(bc_part.sem, 1)
                    dve.wait_ge(bc_part.sem, bc_part.at(c.m, 1))
                    for q in (1, 2):
                        r = slice(q * BC, (q + 1) * BC)
                        d = dve.tensor_copy(s16[r, :], bc_rest[r, :])
                    d.then_inc(bc_part.sem, 1)
                    dve.wait_ge(bc_part.sem, bc_part.at(c.m, 2))
                    r = slice(2 * BC, 3 * BC)
                    dve.tensor_tensor(bc_rest[r, :], bc_rest[r, :], s16[r, :],
                                      ALU.subtract).then_inc(bc_part.sem, 1)
                    dve.wait_ge(bc_part.sem, bc_part.at(c.m, 3))
                    dve.tensor_copy(s16[r, :], bc_rest[r, :]).then_inc(bc_part.sem, 1)
                elif name == "delta":
                    dve.wait_ge(spln_ready.sem, spln_ready.at(c.m))
                    dve.tensor_tensor(delta[:, par, :, :], delta[:, par, :, :], sp_a[:], ALU.add
                                      ).then_inc(delta_ready.sem, 1)
                    dve.wait_ge(delta_ready.sem, delta_ready.at(c.m))
                    dve.tensor_tensor(u[:, par, :, :], delta[:, par, :, :], h[:, par, :, :], ALU.mult
                                      ).then_inc(u_ready.sem, 1)
                elif name == "gated":
                    dve.wait_ge(prod_used.sem, prod_used.at(c.m, SUMS - HALVES + i))
                    if c.past >= 1 and i == 0:
                        emptied(dve, "mout", 1, c.m - 1)
                    dve.scalar_tensor_tensor(yg[:, i, :], h[:, par, i, :], column(V_D + i), p_y[i][:],
                                             ALU.mult, ALU.add).then_inc(p_y_read.sem, 1)
                    dve.wait_ge(p_y_read.sem, p_y_read.at(c.m, i))
                    dve.tensor_tensor(yg[:, i, :], yg[:, i, :], gate[:, par, i, :], ALU.mult
                                      ).then_inc(yg_ready.sem, 1)
                elif name == "down":
                    p = filled(dve, name, i, c.m)
                    dve.tensor_tensor(x2[:, i, :], p[:, 0:D], x2[:, i, :], ALU.add).then_inc(free(name, i), 1)
                elif name == "mout":
                    p = filled(dve, name, i, c.m)
                    dve.wait_ge(xb_ready.sem, xb_ready.at(c.m))
                    half = xb[:, 2 * i:2 * i + 2, :].rearrange("p g d -> p (g d)")
                    dve.tensor_tensor(half, p[:, 0:256], half, ALU.add).then_inc(free(name, i), 1)
                elif name == "aout":
                    p = filled(dve, name, i, c.m)
                    dve.wait_ge(x1b_ready.sem, x1b_ready.at(c.m))
                    half = x1b[:, 2 * i:2 * i + 2, :].rearrange("p g d -> p (g d)")
                    dve.tensor_tensor(half, p[:, 0:256], half, ALU.add).then_inc(free(name, i), 1)
                elif name == "stats":
                    ln, half = divmod(i, 2)
                    emptied(dve, *(("mout", half), ("aout", half), ("down", 2 * half + 1))[ln], c.m)
                    ln_statistics(c, ln, half, LN_IN[ln])
                elif name == "norm":
                    ln, half = divmod(i, 2)
                    if i == 2 and c.past >= 1:
                        dve.wait_ge(out_done.sem, out_done.at(c.m - 1))
                    ln_normalise(c, ln, half, LN_IN[ln], LN_OUT[ln])
                elif name == "score":
                    emptied(dve, name, i, c.m)
                    dve.tensor_reduce(smax[:, i % 2, :], shifted[:, i % 2, :, :], AX_X, ALU.max).then_inc(max_ready.sem, 1)
                elif name == "sum":
                    dve.wait_ge(exp_ready.sem, exp_ready.at(c.m, i))
                    dve.tensor_reduce(den[:, i % 2, :], ex[:, i % 2, :, :], AX_X, ALU.add).then_inc(den_ready.sem, 1)
                    dve.wait_ge(den_ready.sem, den_ready.at(c.m, i))
                    dve.reciprocal(rden[:, i % 2, :], den[:, i % 2, :]).then_inc(rden_ready.sem, 1)
                elif name == "mix":
                    p = filled(dve, name, i, c.m)
                    dve.wait_ge(rdT_ready.sem, rdT_ready.at(c.m, i))
                    for s in range(2):
                        r = slice(64 * s, 64 * s + 64)
                        d = dve.tensor_tensor(aT[r, i * SEQ:(i + 1) * SEQ], p[r, 64 * s:64 * s + 64],
                                              rdT[r, 64 * s:64 * s + 64], ALU.mult)
                    d.then_inc(free(name, i), 1)
                elif name == "route":
                    p = filled(dve, name, i, c.m)
                    logits = p[:, 0:GROUPS * EXPERTS].rearrange("p (g e) -> p g e", e=EXPERTS)
                    dve.tensor_reduce(r_max[:], logits, AX_X, ALU.max).then_inc(route_v.sem, 1)
                    dve.wait_ge(route_v.sem, route_v.at(c.m, 0))
                    dve.tensor_tensor(r_log[:], logits, by_group(r_max[:]).to_broadcast(wide), ALU.subtract
                                      ).then_inc(free(name, i), 1)
                elif name == "r_rank":
                    dve.wait_ge(route_exp.sem, route_exp.at(c.m))
                    dve.tensor_reduce(r_sum[:], r_exp[:], AX_X, ALU.add).then_inc(route_v.sem, 1)
                    dve.wait_ge(route_v.sem, route_v.at(c.m, 1))
                    dve.reciprocal(r_rec[:], r_sum[:]).then_inc(route_v.sem, 1)
                    dve.wait_ge(route_v.sem, route_v.at(c.m, 2))
                    dve.tensor_tensor(r_prob[:], r_exp[:], by_group(r_rec[:]).to_broadcast(wide), ALU.mult
                                      ).then_inc(route_v.sem, 1)
                    dve.wait_ge(route_v.sem, route_v.at(c.m, 3))
                    mine = r_prob[:].unsqueeze(3).to_broadcast([128, GROUPS, EXPERTS, EXPERTS])
                    other = r_prob[:].unsqueeze(2).to_broadcast([128, GROUPS, EXPERTS, EXPERTS])
                    dve.tensor_tensor(r_eq, other, mine, ALU.is_equal)
                    dve.tensor_tensor(r_gt, other, mine, ALU.is_gt).then_inc(route_v.sem, 1)
                elif name == "r_cw":
                    dve.wait_ge(route_g.sem, route_g.at(c.m, 1))
                    dve.tensor_reduce(r_rank[:], r_gt, AX_X, ALU.add).then_inc(route_v.sem, 1)
                    dve.wait_ge(route_v.sem, route_v.at(c.m, 5))
                    dve.scalar_tensor_tensor(r_sel[:], r_rank[:], float(TOP), r_prob[:], ALU.is_lt, ALU.mult
                                             ).then_inc(route_v.sem, 1)
                    dve.wait_ge(route_v.sem, route_v.at(c.m, 6))
                    dve.tensor_reduce(r_sum[:], r_sel[:], AX_X, ALU.add).then_inc(route_v.sem, 1)
                    dve.wait_ge(route_v.sem, route_v.at(c.m, 7))
                    dve.tensor_scalar(r_max[:], r_sum[:], TOP_EPS, None, ALU.add).then_inc(route_v.sem, 1)
                    dve.wait_ge(route_v.sem, route_v.at(c.m, 8))
                    dve.reciprocal(r_rec[:], r_max[:]).then_inc(route_v.sem, 1)
                    dve.wait_ge(route_v.sem, route_v.at(c.m, 9))
                    dve.tensor_tensor(r_cw[:], r_sel[:], by_group(r_rec[:]).to_broadcast(wide), ALU.mult
                                      ).then_inc(route_v.sem, 1)
                    dve.wait_ge(route_v.sem, route_v.at(c.m, 10))
                    E = EXPERTS
                    dve.tensor_copy(cw16[:, :, 0:E], r_cw[:]).then_inc(route_v.sem, 1)
                    dve.wait_ge(route_v.sem, route_v.at(c.m, 11))
                    dve.tensor_tensor(r_rest[:], r_cw[:], cw16[:, :, 0:E], ALU.subtract
                                      ).then_inc(route_v.sem, 1)
                    dve.wait_ge(route_v.sem, route_v.at(c.m, 12))
                    dve.tensor_copy(cw16[:, :, E:2 * E], r_rest[:]).then_inc(route_v.sem, 1)
                    dve.wait_ge(route_v.sem, route_v.at(c.m, 13))
                    dve.tensor_tensor(cw16[:, :, 2 * E:3 * E], r_rest[:], cw16[:, :, E:2 * E], ALU.subtract
                                      ).then_inc(route_v.sem, 1)
                elif name == "up_g":
                    p = filled(dve, name, i, c.m)
                    dve.wait_ge(gt_ready.sem, gt_ready.at(c.m, i))
                    if i > 0:
                        emptied(dve, "up_u", i - 1, c.m)
                    dve.scalar_tensor_tensor(ga, gt[:, i % 2, :], 1.0, p[:], ALU.add, ALU.mult
                                             ).then_inc(free(name, i), 1)
                elif name == "up_u":
                    p = filled(dve, name, i, c.m)
                    emptied(dve, "up_g", i, c.m)
                    dve.tensor_tensor(acts[i], ga, p[:], ALU.mult).then_inc(free(name, i), 1)

            def drives(c, n):
                if n == 0:
                    dve.wait_ge(u_ready.sem, u_ready.at(c.m))
                dve.wait_ge(b_ready.sem, b_ready.at(c.m, n))
                for j in range(HALVES):
                    if n > 0 or c.past >= 1:
                        dve.wait_ge(state_ready.sem, state_ready.at(c.m, HALVES * (n - 1) + j))
                    dve.tensor_tensor(drive[:, j, :], u[:, c.parity, j, :], p_b[:], ALU.mult
                                      ).then_inc(drive_ready.sem, 1)

            def scans(c, k):
                n, j = divmod(k, HALVES)
                dve.wait_ge(decay_ready.sem, decay_ready.at(c.m, k))
                dve.wait_ge(drive_ready.sem, drive_ready.at(c.m, k))
                if k >= BUFFERS or c.past >= 1:
                    dve.wait_ge(prod_ready.sem, prod_ready.at(c.m, k - BUFFERS))
                dve.tensor_tensor_scan(state[:, k % BUFFERS, :], decay[:, j, :], drive[:, j, :], 0.0,
                                       ALU.mult, ALU.add).then_inc(state_ready.sem, 1)

            def turn(chunks):
                for s in range(STEPS):
                    if "scan" in chunks:
                        if s % 2 == 0:
                            drives(chunks["scan"], s // 2)
                        scans(chunks["scan"], s)
                    for stage, name, i in PLAN[s]:
                        if stage in chunks:
                            step(name, i, chunks[stage])

            turns(dve, turn)

        @block.gpsimd
        def _(pool):
            pool.wait_ge(weights_in.sem, 16 * n_weights)
            pool.wait_ge(consts_v.sem, CONSTS)

            def step(name, i, c):
                if name == "mean":
                    pool.wait_ge(mean_sq.sem, mean_sq.at(c.m))
                    if c.past >= 1:
                        pool.wait_ge(xn_ready.sem, xn_ready.at(c.m - 1))
                    pool.tensor_tensor(rms[:], ms[:], mhalf[:], ALU.pow).then_inc(rms_ready.sem, 1)
                elif name == "stats":
                    ln, half = divmod(i, 2)
                    g = slice(2 * half, 2 * half + 2)
                    pool.wait_ge(ln_var[ln].sem, ln_var[ln].at(c.m, half))
                    pool.tensor_tensor(rstd[:, ln, g], var[:, ln, g], mhalf[:, 0:2], ALU.pow
                                       ).then_inc(ln_rstd[ln].sem, 1)
                elif name == "add_out_b":
                    pool.wait_ge(xb_in.sem, xb_in.at(c.m))
                    pool.tensor_tensor(xb[:], xb[:], rowb[:, 0, :].unsqueeze(1).to_broadcast(
                        [128, GROUPS, D]), ALU.add).then_inc(xb_ready.sem, 1)
                elif name == "add_bo":
                    pool.wait_ge(ln_ready[0].sem, ln_ready[0].at(c.m, 1))
                    pool.tensor_tensor(x1b[:], x1[:], rowb[:, 1, :].unsqueeze(1).to_broadcast(
                        [128, GROUPS, D]), ALU.add).then_inc(x1b_ready.sem, 1)
                elif name == "k":
                    emptied(pool, "k", 0, c.m)
                    if c.past >= 1:
                        emptied(pool, "down", GROUPS - 1, c.m - 1)
                    k3 = kT[:].rearrange("p (b t) -> p b t", t=SEQ)
                    pool.tensor_tensor(km[:, :, 0, :], k3, masks[:, 0:1].unsqueeze(2).to_broadcast(
                        [128, CHUNK_B, SEQ]), ALU.mult)
                    for a in range(1, KM_POOL):
                        g = pool.tensor_scalar(km[:, :, a, :], k3,
                                               masks[:, a:a + 1], 0.0, ALU.mult, ALU.add)
                    g.then_inc(km_ready.sem, 1)
                elif name == "score":
                    pool.wait_ge(max_ready.sem, max_ready.at(c.m, i))
                    pool.tensor_tensor(shifted[:, i % 2, :, :], shifted[:, i % 2, :, :],
                                       by_group(smax[:, i % 2, :]).to_broadcast([128, PAIRS, SEQ]),
                                       ALU.subtract).then_inc(shift_ready.sem, 1)
                elif name == "r_rank":
                    pool.wait_ge(route_v.sem, route_v.at(c.m, 4))
                    pool.tensor_tensor(r_eq, r_eq, tri[:].unsqueeze(1).to_broadcast(
                        [128, GROUPS, EXPERTS, EXPERTS]), ALU.mult).then_inc(route_g.sem, 1)
                    pool.wait_ge(route_g.sem, route_g.at(c.m, 0))
                    pool.tensor_tensor(r_gt, r_gt, r_eq, ALU.add).then_inc(route_g.sem, 1)
                elif name == "cw":
                    emptied(pool, "up_u", i, c.m)
                    emptied(pool, "cw", i, c.m)
                    pool.tensor_tensor(acts[i], acts[i], cwr[:, i % 2, :], ALU.mult
                                       ).then_inc(act_ready.sem, 1)

            def products(c, k):
                n, j = divmod(k, HALVES)
                pool.wait_ge(state_ready.sem, state_ready.at(c.m, k))
                if j == 0:
                    emptied(pool, "C", n, c.m)
                if k >= BUFFERS or c.past >= 1:
                    last = (k - BUFFERS) % STEPS
                    m = c.m if k >= BUFFERS else c.m - 1
                    if held_back(last):
                        pool.wait_ge(join_ready.sem, join_ready.at(m, join_index(last + HALVES)))
                    else:
                        pool.wait_ge(prod_used.sem, prod_used.at(m, sum_index(last)))
                pool.tensor_tensor(prod[:, k % BUFFERS, :], state[:, k % BUFFERS, :], c_rep[:, n % 2, :], ALU.mult
                                   ).then_inc(prod_ready.sem, 1)
                if joined(k):
                    pool.wait_ge(prod_ready.sem, prod_ready.at(c.m, k))
                    pool.tensor_tensor(prod[:, k % BUFFERS, :], prod[:, k % BUFFERS, :],
                                       prod[:, (k - HALVES) % BUFFERS, :], ALU.add).then_inc(join_ready.sem, 1)

            def turn(chunks):
                for s in range(STEPS):
                    if "scan" in chunks:
                        products(chunks["scan"], s)
                    for stage, name, i in PLAN[s]:
                        if stage in chunks:
                            step(name, i, chunks[stage])

            turns(pool, turn)


def constants():
    r = np.arange(128)
    masks = np.zeros((128, PAIRS + 2), np.float32)
    masks[r, (r // HEAD_D) % PAIRS] = 1.0
    masks[r, PAIRS + r // 64] = HEAD_D ** -0.5
    sel_bc = np.tile(np.eye(BC, dtype=np.float32), (3, 1))
    sel_cw = np.zeros((128, FFN_TILES * 128), np.float32)
    col = np.arange(FFN_ROWS)
    expert = col // EXPERT_I
    for part in range(3):
        routed = expert < EXPERTS
        sel_cw[part * EXPERTS + expert[routed], col[routed]] = 0.5
    sel_cw[3 * EXPERTS, col[expert == EXPERTS]] = 0.5
    e = np.arange(EXPERTS)
    tri = np.broadcast_to((e[None, :] < e[:, None]).astype(np.float32), (128, EXPERTS, EXPERTS))
    return {
        "c_masks": masks,
        "c_sel_bc": sel_bc,
        "c_sel_cw": sel_cw,
        "c_ident": np.eye(128, dtype=np.float32),
        "c_tri": np.ascontiguousarray(tri),
    }


def kernel(x, ctx_1024, L0_attn_norm_scale, L0_attn_in_w, L0_attn_in_b, L0_attn_conv_w, L0_attn_conv_b,
           L0_attn_xproj_w, L0_attn_dt_w, L0_attn_dt_b, L0_attn_A_log, L0_attn_D, L0_attn_out_w,
           L0_attn_out_b, L0_xattn_Wq, L0_xattn_bq, L0_xattn_Wk, L0_xattn_bk, L0_xattn_Wv, L0_xattn_bv,
           L0_xattn_Wo, L0_xattn_bo, L0_ffn_w_router, L0_ffn_wg, L0_ffn_wu, L0_ffn_wd, L0_ffn_wg_s,
           L0_ffn_wu_s, L0_ffn_wd_s):
    import concourse.bacc as bacc
    from concourse.bass_utils import run_bass_kernel_spmd

    def halves(a):
        a = np.asarray(a)
        return np.moveaxis(a.reshape(a.shape[:-1] + (HALVES, 128)), -1, 0).swapaxes(1, -1).reshape(128, -1)

    vec = np.concatenate([
        np.asarray(L0_attn_norm_scale).reshape(128, 1),
        np.asarray(L0_attn_in_b).reshape(4, 128).T,
        halves(L0_attn_conv_w), halves(L0_attn_conv_b), halves(L0_attn_dt_b), halves(L0_attn_D),
        halves(np.asarray(L0_attn_A_log).T),
        np.asarray(L0_xattn_bq).reshape(128, 1), np.asarray(L0_xattn_bk).reshape(128, 1),
        np.asarray(L0_xattn_bv).reshape(128, 1)], axis=1)
    rows = np.stack([np.asarray(L0_attn_out_b), np.asarray(L0_xattn_bo)])
    xproj = np.asarray(L0_attn_xproj_w).reshape(HALVES, 128, RANK + BC)
    xproj = np.concatenate([xproj[:, :, :RANK]] + [xproj[:, :, RANK:]] * 3, axis=2).transpose(1, 0, 2)
    attn = np.stack([np.asarray(w).T for w in (L0_xattn_Wq, L0_xattn_Wk, L0_xattn_Wv, L0_xattn_Wo)], axis=1)
    pad = FFN_TILES * 128 - FFN_ROWS

    def up(routed, shared):
        a = np.asarray(routed).transpose(1, 0, 2).reshape(D, EXPERTS * EXPERT_I)
        shared = np.asarray(shared)
        return np.concatenate([a, shared, np.zeros((D, pad), shared.dtype)], axis=1).reshape(
            D, FFN_TILES, 128)

    shared = np.asarray(L0_ffn_wd_s)
    down = np.concatenate([np.asarray(L0_ffn_wd).reshape(EXPERTS * EXPERT_I, D), shared,
                           np.zeros((pad, D), shared.dtype)], axis=0)
    arrays = {
        "x": np.asarray(x).reshape(BATCH * SEQ, D),
        "ctx_t": np.asarray(ctx_1024).reshape(BATCH * SEQ, D).T,
        "vec": vec, "rows": rows,
        "w_in": np.asarray(L0_attn_in_w).reshape(128, 4, 128),
        "w_xproj": xproj, "w_dt": np.asarray(L0_attn_dt_w),
        "w_out": np.asarray(L0_attn_out_w).reshape(HALVES, 128, D).transpose(1, 0, 2),
        "w_attn": attn, "w_router": np.asarray(L0_ffn_w_router).T,
        "w_gate": up(L0_ffn_wg, L0_ffn_wg_s), "w_up": up(L0_ffn_wu, L0_ffn_wu_s),
        "w_down": down.reshape(FFN_TILES, 128, D).transpose(1, 0, 2),
        **constants(),
    }
    arrays = {k: np.ascontiguousarray(v) for k, v in arrays.items()}
    nc = bacc.Bacc("TRN2", target_bir_lowering=False, num_devices=1)
    args = {k: nc.dram_tensor(f"in_{k}", v.shape, mybir.dt.from_np(v.dtype), kind="ExternalInput").ap()
            for k, v in arrays.items()}
    out = nc.dram_tensor("out_y", (BATCH * SEQ, D), F32, kind="ExternalOutput").ap()
    build(nc, out=out, **args)
    r = run_bass_kernel_spmd(nc, [{f"in_{k}": v for k, v in arrays.items()}], core_ids=[0])
    return r.results[0]["out_y"].reshape(BATCH, SEQ, D)
```
